# Optimizing a Trainium2 kernel written in Bass

```python
import numpy as np
import jax
import jax.numpy as jnp

def _softmax(x, axis=-1):
    return jax.nn.softmax(x, axis=axis)

def _gelu(x):
    return jax.nn.gelu(x, approximate=True)

def _silu(x):
    return jax.nn.silu(x)

def _sigmoid(x):
    return jax.nn.sigmoid(x)

def _layernorm(x, axis=-1, eps=1e-05):
    m = jnp.mean(x, axis=axis, keepdims=True)
    v = jnp.var(x, axis=axis, keepdims=True)
    return (x - m) / jnp.sqrt(v + eps)

def _scatter_add(tgt, idx, src, axis=0):
    return tgt.at[idx].add(src)

def _segment_sum(src, seg, n):
    return jax.ops.segment_sum(src, seg, n)
kernel_name = 'mk_seq_preln_d2_jaxref_r8_738048'

def setup_inputs(seed: int=0):
    np.random.seed(seed)
    _w = jnp.asarray

    def _L0_attn_setup():
        import jax, jax.numpy as jnp
        import numpy as np
        CHUNK = 32

        def l2norm(x):
            return x * jax.lax.rsqrt(jnp.sum(x * x, -1, keepdims=True) + 1e-06)

        def causal_dwconv(x, w):
            k = w.shape[-1]
            xt = jnp.transpose(x, (0, 2, 1))
            xt = jnp.pad(xt, ((0, 0), (0, 0), (k - 1, 0)))
            y = jax.lax.conv_general_dilated(xt, w, (1,), 'VALID', dimension_numbers=('NCH', 'OIH', 'NCH'), feature_group_count=xt.shape[1])
            return jnp.transpose(y, (0, 2, 1))

        def delta_rule_chunkwise(q, k, v, beta):
            b, h, L, dk = q.shape
            dv = v.shape[-1]
            n = L // CHUNK
            q = l2norm(q)
            k = l2norm(k)
            v = v * beta[..., None]
            kb = k * beta[..., None]
            resh = lambda t: t.reshape(b, h, n, CHUNK, t.shape[-1])
            q, k, v, kb = (resh(t) for t in (q, k, v, kb))
            strict = jnp.tril(jnp.ones((CHUNK, CHUNK), bool), -1)
            A = jnp.where(strict, -(kb @ jnp.swapaxes(k, -1, -2)), 0.0)
            eye = jnp.eye(CHUNK, dtype=A.dtype)
            T = jax.scipy.linalg.solve_triangular(eye - A, jnp.broadcast_to(eye, A.shape), lower=True)
            u = T @ v
            w = T @ kb
            incl = jnp.tril(jnp.ones((CHUNK, CHUNK), bool))

            def step(S, xs):
                q_i, k_i, u_i, w_i = xs
                attn = jnp.where(incl, q_i @ jnp.swapaxes(k_i, -1, -2), 0.0)
                u_hat = u_i - w_i @ S
                o_i = q_i @ S + attn @ u_hat
                return (S + jnp.swapaxes(k_i, -1, -2) @ u_hat, o_i)
            xs = tuple((jnp.moveaxis(t, 2, 0) for t in (q, k, u, w)))
            S0 = jnp.zeros((b, h, dk, dv), q.dtype)
            S, o = jax.lax.scan(step, S0, xs)
            o = jnp.moveaxis(o, 0, 2).reshape(b, h, L, dv)
            return (o, S)

        def branch_stats(x):
            m = jnp.mean(x, -1, keepdims=True)
            s = jnp.std(x, -1, keepdims=True, ddof=1)
            a = jnp.mean(jnp.abs(x), -1, keepdims=True)
            l = jnp.sqrt(jnp.sum(x * x, -1, keepdims=True))
            return jnp.concatenate([m, s, a, l], -1)
        key = jax.random.key(seed)
        B, L, D, H = (2, 256, 128, 4)
        dk = dv = D // H
        S = 6
        ks = iter(jax.random.split(key, 32))
        nrm = lambda shape, s=0.02: jax.random.normal(next(ks), shape, jnp.float32) * s

        def fir(kw):
            base = jnp.zeros((H * dv, 1, kw), jnp.float32).at[:, 0, -1].set(1.0)
            return base + nrm((H * dv, 1, kw))
        gate_in_dim = D + S * 4 * H
        hgd = D * 2 // 2
        b2 = np.zeros(H * S, np.float32)
        for h in range(H):
            b2[h * S + S - 1] = 2.0
        return {'hidden_states': jax.random.normal(next(ks), (B, L, D), jnp.float32), 'q_w': nrm((D, D)), 'k_w': nrm((D, D)), 'v_w': nrm((D, D)), 'b_w': nrm((D, H)), 'qc_w': nrm((D, 1, 4), 0.3), 'kc_w': nrm((D, 1, 4), 0.3), 'vc_w': nrm((D, 1, 4), 0.3), 'fir_w1': fir(1), 'fir_w3': fir(3), 'fir_w7': fir(7), 'fir_w31': fir(31), 'mlp_w1': nrm((gate_in_dim, hgd)), 'mlp_b1': jnp.zeros((hgd,), jnp.float32), 'mlp_w2': nrm((hgd, H * S)), 'mlp_b2': jnp.asarray(b2), 'gate_log_temp': jnp.zeros((H,), jnp.float32), 'onorm_w': jnp.ones((dv,), jnp.float32), 'o_w': nrm((D, D))}
    _L0_attn_in = _L0_attn_setup()

    def _L0_ffn_setup():
        import jax, jax.numpy as jnp
        import numpy as np
        B, S, IN, OUT, E, R = (8, 512, 128, 128, 8, 8)
        LORA_ALPHA = 16
        SCALING = LORA_ALPHA / R
        key = jax.random.key(seed)
        k = jax.random.split(key, 6)
        x = jax.random.normal(k[0], (B, S, IN), dtype=jnp.float32)
        base_w = jax.random.normal(k[1], (OUT, IN), dtype=jnp.float32) * 0.02
        base_b = jnp.zeros((OUT,), dtype=jnp.float32)
        lora_A = jax.random.normal(k[2], (IN, R), dtype=jnp.float32) * 0.02
        lora_B = jax.random.normal(k[3], (E, R, OUT), dtype=jnp.float32) * 0.02
        router_w = jax.random.normal(k[4], (E, IN), dtype=jnp.float32) * 0.02
        router_b = jnp.zeros((E,), dtype=jnp.float32)
        return {'x': x, 'base_w': base_w, 'base_b': base_b, 'lora_A': lora_A, 'lora_B': lora_B, 'router_w': router_w, 'router_b': router_b}
    _L0_ffn_in = _L0_ffn_setup()

    def _L1_attn_setup():
        import jax, jax.numpy as jnp
        import numpy as np
        EMBED_DIM = 128
        NUM_HEADS = 16
        HEAD_DIM = EMBED_DIM // NUM_HEADS
        FEATURE_EPS = 1e-06
        DEN_EPS = 1e-06
        key = jax.random.key(seed)
        k_x, k_qw, k_qb, k_ow, k_ob = jax.random.split(key, 5)
        b, l = (2, 256)
        x = jax.random.normal(k_x, (b, l, EMBED_DIM), dtype=jnp.float32)
        s = 1.0 / np.sqrt(EMBED_DIM)
        qkv_w = jax.random.uniform(k_qw, (3 * EMBED_DIM, EMBED_DIM), minval=-s, maxval=s, dtype=jnp.float32)
        qkv_b = jax.random.uniform(k_qb, (3 * EMBED_DIM,), minval=-s, maxval=s, dtype=jnp.float32)
        out_w = jax.random.uniform(k_ow, (EMBED_DIM, EMBED_DIM), minval=-s, maxval=s, dtype=jnp.float32)
        out_b = jax.random.uniform(k_ob, (EMBED_DIM,), minval=-s, maxval=s, dtype=jnp.float32)
        return {'x': x, 'qkv_w': qkv_w, 'qkv_b': qkv_b, 'out_w': out_w, 'out_b': out_b}
    _L1_attn_in = _L1_attn_setup()

    def _L1_ffn_setup():
        import jax, jax.numpy as jnp
        import numpy as np
        B, S, D = (2, 256, 128)
        E, H, K = (8, 704, 2)
        N_RESERVED = 4
        key = jax.random.key(seed)
        ks = jax.random.split(key, 5)
        scale = 0.02
        x = jax.random.normal(ks[0], (B, S, D), dtype=jnp.float32)
        gate_w = jax.random.normal(ks[1], (E, D), dtype=jnp.float32) * scale
        w1 = jax.random.normal(ks[2], (E, D, H), dtype=jnp.float32) * scale
        w3 = jax.random.normal(ks[3], (E, D, H), dtype=jnp.float32) * scale
        w2 = jax.random.normal(ks[4], (E, H, D), dtype=jnp.float32) * scale
        return {'x': x, 'gate_w': gate_w, 'w1': w1, 'w2': w2, 'w3': w3}
    _L1_ffn_in = _L1_ffn_setup()
    _d = {'L0_attn_hidden_states': _L0_attn_in['hidden_states'], 'L0_attn_q_w': _L0_attn_in['q_w'], 'L0_attn_k_w': _L0_attn_in['k_w'], 'L0_attn_v_w': _L0_attn_in['v_w'], 'L0_attn_b_w': _L0_attn_in['b_w'], 'L0_attn_qc_w': _L0_attn_in['qc_w'], 'L0_attn_kc_w': _L0_attn_in['kc_w'], 'L0_attn_vc_w': _L0_attn_in['vc_w'], 'L0_attn_fir_w1': _L0_attn_in['fir_w1'], 'L0_attn_fir_w3': _L0_attn_in['fir_w3'], 'L0_attn_fir_w7': _L0_attn_in['fir_w7'], 'L0_attn_fir_w31': _L0_attn_in['fir_w31'], 'L0_attn_mlp_w1': _L0_attn_in['mlp_w1'], 'L0_attn_mlp_b1': _L0_attn_in['mlp_b1'], 'L0_attn_mlp_w2': _L0_attn_in['mlp_w2'], 'L0_attn_mlp_b2': _L0_attn_in['mlp_b2'], 'L0_attn_gate_log_temp': _L0_attn_in['gate_log_temp'], 'L0_attn_onorm_w': _L0_attn_in['onorm_w'], 'L0_attn_o_w': _L0_attn_in['o_w'], 'L0_ffn_base_w': _L0_ffn_in['base_w'], 'L0_ffn_base_b': _L0_ffn_in['base_b'], 'L0_ffn_lora_A': _L0_ffn_in['lora_A'], 'L0_ffn_lora_B': _L0_ffn_in['lora_B'], 'L0_ffn_router_w': _L0_ffn_in['router_w'], 'L0_ffn_router_b': _L0_ffn_in['router_b'], 'L1_attn_qkv_w': _L1_attn_in['qkv_w'], 'L1_attn_qkv_b': _L1_attn_in['qkv_b'], 'L1_attn_out_w': _L1_attn_in['out_w'], 'L1_attn_out_b': _L1_attn_in['out_b'], 'L1_ffn_gate_w': _L1_ffn_in['gate_w'], 'L1_ffn_w1': _L1_ffn_in['w1'], 'L1_ffn_w2': _L1_ffn_in['w2'], 'L1_ffn_w3': _L1_ffn_in['w3']}
    _x0 = _d['L0_attn_hidden_states']
    _d['L0_attn_hidden_states'] = jax.random.normal(jax.random.fold_in(jax.random.key(seed), 1), (1, 2048, 128), dtype=_x0.dtype)
    del _x0
    return _d

def reference(L0_attn_hidden_states, L0_attn_q_w, L0_attn_k_w, L0_attn_v_w, L0_attn_b_w, L0_attn_qc_w, L0_attn_kc_w, L0_attn_vc_w, L0_attn_fir_w1, L0_attn_fir_w3, L0_attn_fir_w7, L0_attn_fir_w31, L0_attn_mlp_w1, L0_attn_mlp_b1, L0_attn_mlp_w2, L0_attn_mlp_b2, L0_attn_gate_log_temp, L0_attn_onorm_w, L0_attn_o_w, L0_ffn_base_w, L0_ffn_base_b, L0_ffn_lora_A, L0_ffn_lora_B, L0_ffn_router_w, L0_ffn_router_b, L1_attn_qkv_w, L1_attn_qkv_b, L1_attn_out_w, L1_attn_out_b, L1_ffn_gate_w, L1_ffn_w1, L1_ffn_w2, L1_ffn_w3):

    def _L0_attn_ref(hidden_states, q_w, k_w, v_w, b_w, qc_w, kc_w, vc_w, fir_w1, fir_w3, fir_w7, fir_w31, mlp_w1, mlp_b1, mlp_w2, mlp_b2, gate_log_temp, onorm_w, o_w):
        import jax, jax.numpy as jnp
        import numpy as np
        CHUNK = 32

        def l2norm(x):
            return x * jax.lax.rsqrt(jnp.sum(x * x, -1, keepdims=True) + 1e-06)

        def causal_dwconv(x, w):
            k = w.shape[-1]
            xt = jnp.transpose(x, (0, 2, 1))
            xt = jnp.pad(xt, ((0, 0), (0, 0), (k - 1, 0)))
            y = jax.lax.conv_general_dilated(xt, w, (1,), 'VALID', dimension_numbers=('NCH', 'OIH', 'NCH'), feature_group_count=xt.shape[1])
            return jnp.transpose(y, (0, 2, 1))

        def delta_rule_chunkwise(q, k, v, beta):
            b, h, L, dk = q.shape
            dv = v.shape[-1]
            n = L // CHUNK
            q = l2norm(q)
            k = l2norm(k)
            v = v * beta[..., None]
            kb = k * beta[..., None]
            resh = lambda t: t.reshape(b, h, n, CHUNK, t.shape[-1])
            q, k, v, kb = (resh(t) for t in (q, k, v, kb))
            strict = jnp.tril(jnp.ones((CHUNK, CHUNK), bool), -1)
            A = jnp.where(strict, -(kb @ jnp.swapaxes(k, -1, -2)), 0.0)
            eye = jnp.eye(CHUNK, dtype=A.dtype)
            T = jax.scipy.linalg.solve_triangular(eye - A, jnp.broadcast_to(eye, A.shape), lower=True)
            u = T @ v
            w = T @ kb
            incl = jnp.tril(jnp.ones((CHUNK, CHUNK), bool))

            def step(S, xs):
                q_i, k_i, u_i, w_i = xs
                attn = jnp.where(incl, q_i @ jnp.swapaxes(k_i, -1, -2), 0.0)
                u_hat = u_i - w_i @ S
                o_i = q_i @ S + attn @ u_hat
                return (S + jnp.swapaxes(k_i, -1, -2) @ u_hat, o_i)
            xs = tuple((jnp.moveaxis(t, 2, 0) for t in (q, k, u, w)))
            S0 = jnp.zeros((b, h, dk, dv), q.dtype)
            S, o = jax.lax.scan(step, S0, xs)
            o = jnp.moveaxis(o, 0, 2).reshape(b, h, L, dv)
            return (o, S)

        def branch_stats(x):
            m = jnp.mean(x, -1, keepdims=True)
            s = jnp.std(x, -1, keepdims=True, ddof=1)
            a = jnp.mean(jnp.abs(x), -1, keepdims=True)
            l = jnp.sqrt(jnp.sum(x * x, -1, keepdims=True))
            return jnp.concatenate([m, s, a, l], -1)
        B, L, D = hidden_states.shape
        H = gate_log_temp.shape[0]
        dk = q_w.shape[1] // H
        dv = v_w.shape[1] // H
        q = jax.nn.silu(causal_dwconv(hidden_states @ q_w, qc_w))
        k = jax.nn.silu(causal_dwconv(hidden_states @ k_w, kc_w))
        v = jax.nn.silu(causal_dwconv(hidden_states @ v_w, vc_w))
        q = q.reshape(B, L, H, dk)
        k = k.reshape(B, L, H, dk)
        v_direct = v.reshape(B, L, H, dv)
        beta = jax.nn.sigmoid(hidden_states @ b_w)
        delta_out, _ = delta_rule_chunkwise(jnp.transpose(q, (0, 2, 1, 3)), jnp.transpose(k, (0, 2, 1, 3)), jnp.transpose(v_direct, (0, 2, 1, 3)), jnp.transpose(beta, (0, 2, 1)))
        delta_out = jnp.transpose(delta_out, (0, 2, 1, 3))
        v_flat = v_direct.reshape(B, L, H * dv)
        firs = [causal_dwconv(v_flat, w).reshape(B, L, H, dv) for w in (fir_w1, fir_w3, fir_w7, fir_w31)]
        branches = firs + [delta_out, v_direct]
        S = len(branches)
        stats = jnp.concatenate([branch_stats(x) for x in branches], -1)
        gate_in = jnp.concatenate([hidden_states, stats.reshape(B, L, H * S * 4)], -1)
        hgate = jax.nn.gelu(gate_in @ mlp_w1 + mlp_b1, approximate=False)
        logits = (hgate @ mlp_w2 + mlp_b2).reshape(B, L, H, S)
        temp = jax.nn.softplus(gate_log_temp) + 0.5
        weights = jax.nn.softmax(logits / temp[None, None, :, None], axis=-1)
        fused = sum((weights[..., i, None] * br for i, br in enumerate(branches)))
        fused = fused * jax.lax.rsqrt(jnp.mean(fused * fused, -1, keepdims=True) + 1e-05) * onorm_w
        return fused.reshape(B, L, H * dv) @ o_w

    def _L0_ffn_ref(x, base_w, base_b, lora_A, lora_B, router_w, router_b):
        import jax, jax.numpy as jnp
        import numpy as np
        B, S, IN, OUT, E, R = (8, 512, 128, 128, 8, 8)
        LORA_ALPHA = 16
        SCALING = LORA_ALPHA / R
        result = jnp.einsum('bsd,od->bso', x, base_w) + base_b
        logits = jnp.einsum('bsd,ed->bse', x, router_w) + router_b
        gating = jax.nn.softmax(logits, axis=-1).astype(jnp.bfloat16)
        mid = jnp.einsum('bsd,dr->bsr', x, lora_A)
        lora_out = jnp.einsum('bsr,erd,bse->bsd', mid, lora_B, gating.astype(jnp.float32))
        return result + lora_out * SCALING

    def _L1_attn_ref(x, qkv_w, qkv_b, out_w, out_b):
        import jax, jax.numpy as jnp
        import numpy as np
        EMBED_DIM = 128
        NUM_HEADS = 16
        HEAD_DIM = EMBED_DIM // NUM_HEADS
        FEATURE_EPS = 1e-06
        DEN_EPS = 1e-06
        b, l, e = x.shape
        qkv = (x @ qkv_w.T + qkv_b).reshape(b, l, 3, NUM_HEADS, HEAD_DIM)
        qkv = jnp.transpose(qkv, (2, 0, 3, 1, 4))
        q, k, v = (qkv[0], qkv[1], qkv[2])
        q = jax.nn.relu(q) + FEATURE_EPS
        k = jax.nn.relu(k) + FEATURE_EPS
        kv = jnp.cumsum(jnp.einsum('bhld,bhle->bhlde', k, v), axis=2)
        k_cum = jnp.cumsum(k, axis=2)
        num = jnp.einsum('bhld,bhlde->bhle', q, kv)
        den = jnp.maximum(jnp.einsum('bhld,bhld->bhl', q, k_cum)[..., None], DEN_EPS)
        out = num / den
        out = jnp.transpose(out, (0, 2, 1, 3)).reshape(b, l, e)
        return out @ out_w.T + out_b

    def _L1_ffn_ref(x, gate_w, w1, w2, w3):
        import jax, jax.numpy as jnp
        import numpy as np
        B, S, D = (2, 256, 128)
        E, H, K = (8, 704, 2)
        N_RESERVED = 4
        b, s, d = x.shape
        T = b * s
        xf = x.reshape(T, d)
        logits = xf @ gate_w.T
        expert_ids = jnp.arange(E)
        logits = jnp.where(expert_ids[None, :] >= E - N_RESERVED, -jnp.inf, logits)
        weights = jax.nn.softmax(logits, axis=-1)
        top_w, top_idx = jax.lax.top_k(weights, K)
        top_w = top_w / jnp.sum(top_w, axis=-1, keepdims=True)
        cw = jnp.zeros((T, E), dtype=x.dtype).at[jnp.arange(T)[:, None], top_idx].add(top_w)
        h = jax.nn.silu(jnp.einsum('td,edh->teh', xf, w1)) * jnp.einsum('td,edh->teh', xf, w3)
        y = jnp.einsum('teh,ehd->ted', h, w2)
        out = jnp.einsum('te,ted->td', cw, y)
        return out.reshape(b, s, d)
    x = L0_attn_hidden_states
    x = x + _L0_attn_ref(_layernorm(x, axis=-1), L0_attn_q_w, L0_attn_k_w, L0_attn_v_w, L0_attn_b_w, L0_attn_qc_w, L0_attn_kc_w, L0_attn_vc_w, L0_attn_fir_w1, L0_attn_fir_w3, L0_attn_fir_w7, L0_attn_fir_w31, L0_attn_mlp_w1, L0_attn_mlp_b1, L0_attn_mlp_w2, L0_attn_mlp_b2, L0_attn_gate_log_temp, L0_attn_onorm_w, L0_attn_o_w)
    x = x + _L0_ffn_ref(_layernorm(x, axis=-1), L0_ffn_base_w, L0_ffn_base_b, L0_ffn_lora_A, L0_ffn_lora_B, L0_ffn_router_w, L0_ffn_router_b)
    x = x + _L1_attn_ref(_layernorm(x, axis=-1), L1_attn_qkv_w, L1_attn_qkv_b, L1_attn_out_w, L1_attn_out_b)
    x = x + _L1_ffn_ref(_layernorm(x, axis=-1), L1_ffn_gate_w, L1_ffn_w1, L1_ffn_w2, L1_ffn_w3)
    return x

_drawn_inputs = setup_inputs


def setup_inputs(seed=0):
    import zlib

    import numpy as np

    out = dict(_drawn_inputs(seed))
    spreads = {'L0_attn_mlp_b1': (0.0, 2.0),
     'L0_attn_gate_log_temp': (0.0, 2.0),
     'L0_attn_onorm_w': (1.0, 0.2),
     'L0_ffn_base_b': (0.0, 0.1),
     'L0_ffn_router_b': (0.0, 0.8)}
    factors = {'L0_attn_q_w': 30.024,
     'L0_attn_k_w': 29.168,
     'L0_attn_b_w': 64.0,
     'L0_attn_qc_w': 30.032,
     'L0_attn_kc_w': 29.952,
     'L0_attn_fir_w1': 64.0,
     'L0_attn_fir_w3': 64.0,
     'L0_attn_fir_w7': 23.776,
     'L0_attn_fir_w31': 23.072,
     'L0_attn_mlp_w1': 56.634,
     'L0_attn_mlp_w2': 64.0,
     'L0_attn_mlp_b2': 8.0,
     'L0_ffn_lora_A': 6.572,
     'L0_ffn_lora_B': 6.368,
     'L0_ffn_router_w': 8.0,
     'L1_ffn_gate_w': 8.0,
     'L1_ffn_w1': 6.178,
     'L1_ffn_w2': 6.147,
     'L1_ffn_w3': 6.144}
    for name, (base, spread) in spreads.items():
        noise = np.random.default_rng([zlib.crc32(name.encode()), seed]).standard_normal(out[name].shape)
        drawn = base * np.exp(spread * noise) if base else spread * noise
        out[name] = jnp.asarray(drawn.astype(out[name].dtype))
    for name, factor in factors.items():
        out[name] = (out[name] * factor).astype(out[name].dtype)
    return out
```

```python
from contextlib import ExitStack

import numpy as np
import concourse.bass as bass
from concourse import mybir

ACT = mybir.ActivationFunctionType
ALU = mybir.AluOpType
AX = mybir.AxisListType
F32 = mybir.dt.float32

P = 128
L, D = 2048, 128
NT = L // P
TB = 4
BL = TB * P
NB = L // BL
H, DK = 4, 32
C = 32
CB = BL // C
NBR = 6
KQ = 4
FIRS = (1, 3, 7, 31)
PAD = max(FIRS) - 1
EXP, HID = 4, 704
NE = 8


def const_columns():
    p = np.arange(P)
    i, j = p[:, None], p[None, :]
    same = (i // C) == (j // C)
    cols = {}
    cols["ident"] = np.eye(P)
    cols["same32"] = same * 1.0
    cols["lower"] = (same & (i > j)) * 1.0
    cols["upper"] = (same & (i <= j)) * 1.0
    cols["causal"] = (i <= j) * 1.0
    jj = np.arange(C)[None, :]
    ii = (p % C)[:, None]
    for m in (1, 2, 4, 8, 16):
        at = (ii // (2 * m) == jj // (2 * m)) & ((ii // m) % 2 == 0) & ((jj // m) % 2 == 1)
        cols[f"level{m}"] = at * -1.0
    cols["eye32"] = (ii == jj) * 1.0
    head = p // DK
    w = P + NBR - 1
    for name, rows in (("meanX", {0: 1 / DK}), ("meanA", {32: 1 / DK}), ("sumQ", {64: 1 / (DK - 1), 96: 1.0})):
        a = np.zeros((P, w))
        for off, val in rows.items():
            a[p, NBR - 1 + off + head * NBR] = val
        cols[name] = a
    a = np.zeros((P, P))
    r = np.arange(H * NBR)
    a[r, 64 + r] = -DK / (DK - 1)
    cols["less_mean2"] = a
    for b in range(NBR):
        a = np.zeros((P, P))
        for h in range(H):
            a[h * NBR + b, h * DK:(h + 1) * DK] = 1.0
        cols[f"spread{b}"] = a
    cols["head_mean"] = same / DK
    cols["head_own"] = np.kron((np.arange(P)[:, None] // 8 == np.arange(16)[None, :]) * 1.0, np.ones((1, 9)))
    cols["head_of4"] = ((p[:, None] % 32) // 8 == np.arange(4)[None, :]) * 1.0
    cols["earlier"] = np.tile((np.arange(EXP)[None, :] < np.arange(EXP)[:, None]).reshape(1, -1) * 1.0, (P, 1))
    for n, v in (("eps5", 1e-5), ("eps6", 1e-6)):
        cols[n] = np.full((P, 1), v)
    at, where = 0, {}
    for n, a in cols.items():
        where[n] = (at, a.shape[1])
        at += a.shape[1]
    return np.concatenate(list(cols.values()), 1).astype(np.float32), where


CONSTS, CONST_AT = const_columns()


class Signals:

    def __init__(self, nc, phase):
        self.nc, self.phase, self.of = nc, phase, {}

    def __call__(self, name):
        if name not in self.of:
            self.of[name] = self.nc.alloc_semaphore(name=f"{self.phase}_{name}")
        return self.of[name]

    def clear(self):
        self.nc.clear_and_free_semaphores(list(self.of.values()))
        self.nc.all_engine_barrier()


def columns(t, b, n, width=BL):
    return t[:, bass.ds(b * BL + n, width)]


def layernorm_moments(nc, dve, s, b, x_sb, stats, mv, ve):
    v = nc.vector
    for j in range(TB):
        v.bn_stats(stats[:, j, :], columns(x_sb, b, j * P, P)).then_inc(s("ln_stats"), 1)
    dve.wait_ge(s("ln_stats"), TB * b + TB)
    v.memset(ve[:, :], 0.0).then_inc(s("ve_clear"), 1)
    for j in range(TB):
        v.bn_aggr(mv[:, j, :], stats[:, j, :]).then_inc(s("mv"), 1)
    dve.wait_ge(s("mv"), TB * b + TB)
    dve.wait_ge(s("ve_clear"), b + 1)
    v.tensor_scalar(ve[:, :], mv[:, :, 1], 1e-5, None, ALU.add).then_inc(s("ve"), 1)


def layernorm_apply(nc, dve, s, b, x_sb, mv, std, rstd, xn):
    v = nc.vector
    dve.wait_ge(s("std"), b + 1)
    v.reciprocal(rstd[:, :], std[:, :]).then_inc(s("rstd"), 1)
    dve.wait_ge(s("rstd"), b + 1)
    for j in range(TB):
        v.tensor_scalar(xn[:, j * P:(j + 1) * P], columns(x_sb, b, j * P, P), mv[:, j, 0:1], rstd[:, j:j + 1],
                        ALU.subtract, ALU.mult).then_inc(s("xn"), 1)


def layernorm_buffers(sb):
    return (sb("ln_stats", P, TB, 6), sb("ln_mv", P, TB, 2), sb("ln_ve", P, TB), sb("ln_std", P, TB), sb("ln_rstd", P, TB),
            sb("xn", P, BL), sb("xnT", P, BL))


def phase_delta(nc, x_sb, K, W, dram):
    with ExitStack() as ctx:
        def sb(name, *shape):
            return ctx.enter_context(nc.sbuf_tensor("delta_" + name, list(shape), F32))

        def bank(name):
            return ctx.enter_context(nc.psum_tensor("delta_" + name, [P, BL], F32))

        s = Signals(nc, "delta")
        stats, mv, ve, std, rstd, xn, xnT = layernorm_buffers(sb)
        pre = sb("pre", P, 3, KQ - 1 + BL)
        conv = sb("conv", P, 3, BL)
        beta = sb("beta", P, TB, H)
        qT = sb("qT", P, BL)
        kT = sb("kT", P, BL)
        qX = sb("qX", P, TB, H, P)
        kX = sb("kX", P, TB, H, P)
        vT = sb("vT", P, PAD + BL)
        sq = sb("sq", P, 2, BL)
        nrm = sb("nrm", P, TB, 8)
        root = sb("root", P, TB, 8)
        rn = sb("rn", P, TB, 8)
        gam = sb("gam", P, TB, H)
        rkb = sb("rkb", P, TB, H)
        k_tok = sb("k_tok", P, BL)
        vk = sb("vk", P, TB, H, 2, DK)
        A = sb("A", P, TB * H, P)
        at = sb("at", P, TB * H, P)
        E = sb("E", P, TB * H, C)
        Pm = sb("Pm", P, TB * H, C)
        Tc = sb("Tc", P, TB * H, C)
        X = sb("X", P, TB * H, P)
        u0 = sb("u0", P, TB, H, DK)
        w_tok = sb("w_tok", P, TB, H, DK)
        wT = sb("wT", P, BL)
        u = sb("u", P, TB, H, DK)
        Sbd = sb("Sbd", P, P)
        o_tok = sb("o_tok", P, BL)
        br = sb("br", P, 5, BL)
        absb = sb("absb", P, 2, BL)
        sqb = sb("sqb", P, 2, BL)
        st2 = sb("st2", P, BL)
        var = sb("var", P, BL)
        st = sb("st", P, BL)
        hid = sb("hid", P, BL)
        lg = sb("lg", P, TB, H, NBR)
        mx = sb("mx", P, TB, H)
        ex = sb("ex", P, TB, H, NBR)
        sm = sb("sm", P, TB, H)
        rs = sb("rs", P, TB, H)
        wt = sb("wt", P, TB, H, NBR)
        wtT = sb("wtT", H * NBR, BL)
        fu = sb("fu", P, BL)
        tmp = sb("tmp", P, 2, BL)
        fsq = sb("fsq", P, BL)
        lnv = sb("lnv", P, BL)
        rr = sb("rr", P, BL)
        fn = sb("fn", P, BL)
        B = [bank(f"bank{n}") for n in range(8)]

        def c3(t):
            return t.rearrange("p (a c) -> p a c", c=P)

        with nc.Block() as block:
            @block.sync
            def _(sp):
                pass

            @block.gpsimd
            def _(pool):
                for t in (qX, kX, X, pre, vT, Sbd):
                    nc.gpsimd.memset(t[:], 0.0).then_inc(s("zeroed"), 1)

            @block.tensor
            def _(pe):
                def mm(out, lhsT, rhs, start=True, stop=True, **kw):
                    return nc.tensor.matmul(out, lhsT, rhs, start=start, stop=stop, **kw)

                with pe.Fori(0, NB) as b:
                    for j in range(TB):
                        pe.wait_ge(s("xn"), b * TB + j + 1)
                        if j == 0:
                            pe.wait_ge(s("out_added"), b + 1)
                        nc.tensor.transpose(B[0][:, j * P:(j + 1) * P], xn[:, j * P:(j + 1) * P], K("ident")).then_inc(s("xnT_ps"), 1)
                    pe.wait_ge(s("xnT"), b + 1)
                    for n in range(3):
                        mm(B[1 + n][:, :], W["qkv"][:, n, :], xnT[:, :]).then_inc(s("proj"), 1)
                    for j in range(TB):
                        last = mm(B[4][:, j * 8:j * 8 + H], xnT[:, j * P:(j + 1) * P], W["b"][:, :])
                    last.then_inc(s("beta_ps"), 1)
                    pe.wait_ge(s("qk_sq"), 2 * b + 2)
                    pe.wait_ge(s("beta_tanh"), b + 1)
                    for j in range(TB):
                        for n in range(2):
                            last = mm(B[4][:, 64 + j * 8 + n * H:64 + j * 8 + (n + 1) * H],
                                      sq[:, n, j * P:(j + 1) * P], K("same32").rearrange("p (h c) -> p h c", c=DK)[:, :, 0])
                    last.then_inc(s("norms_ps"), 1)
                    pe.wait_ge(s("kT"), b + 1)
                    pe.wait_ge(s("pre_in"), 3 * b + 3)
                    for j in range(TB):
                        nc.tensor.transpose(B[1][:, j * P:(j + 1) * P], kT[:, j * P:(j + 1) * P], K("ident")).then_inc(s("k_tok_ps"), 1)
                    pe.wait_ge(s("vT"), b + 1)
                    for j in range(TB):
                        nc.tensor.transpose(B[2][:, j * P:(j + 1) * P], vT[:, PAD + j * P:PAD + (j + 1) * P], K("ident")).then_inc(s("v_tok_ps"), 1)
                    pe.wait_ge(s("kX"), 4 * b + 4)
                    pe.wait_ge(s("qX"), 4 * b + 4)
                    for j in range(TB):
                        if j:
                            pe.wait_ge(s("A"), b * TB + j)
                        mm(B[3][:, :], kT[:, j * P:(j + 1) * P], kX[:, j].rearrange("p h t -> p (h t)")).then_inc(s("gram"), 1)
                        if j:
                            pe.wait_ge(s("attn"), b * TB + j)
                        mm(B[5][:, :], kT[:, j * P:(j + 1) * P], qX[:, j].rearrange("p h t -> p (h t)")).then_inc(s("attn_ps"), 1)
                    for r in range(4):
                        pe.wait_ge(s("E"), 5 * b + r + 1)
                        pe.wait_ge(s("attn"), b * TB + TB)
                        for n in range(TB * H):
                            last = mm(B[3][:, n * C:(n + 1) * C], A[:, n, :], E[:, n, :])
                        last.then_inc(s("UE"), 1)
                        pe.wait_ge(s("Pm"), 4 * b + r + 1)
                        pe.wait_ge(s("X"), 20 * b + 4 * r + 4)
                        for n in range(TB * H):
                            last = mm(B[5][:, n * C:(n + 1) * C], X[:, n, :], Pm[:, n, :])
                        last.then_inc(s("EUE"), 1)
                    pe.wait_ge(s("X"), 20 * b + 20)
                    pe.wait_ge(s("vk"), 2 * b + 2)
                    for n in range(TB * H):
                        last = mm(B[1 + n // 8][:, (n % 8) * 64:(n % 8) * 64 + 64], X[:, n, :],
                                  vk[:, n // H, n % H].rearrange("p a c -> p (a c)"))
                    last.then_inc(s("uw_ps"), 1)
                    pe.wait_ge(s("w_tok"), b + 1)
                    for j in range(TB):
                        nc.tensor.transpose(B[3][:, j * P:(j + 1) * P], w_tok[:, j].rearrange("p h c -> p (h c)"), K("ident")).then_inc(s("wT_ps"), 1)
                    pe.wait_ge(s("wT"), b + 1)
                    pe.wait_ge(s("u0"), b + 1)
                    for c in range(CB):
                        j, q = c // 4, slice((c % 4) * C, (c % 4 + 1) * C)
                        t = slice(c * C, (c + 1) * C)
                        cs = slice(j * P, (j + 1) * P)
                        pe.wait_ge(s("state"), b * CB + c + 1)
                        mm(B[5][q, 0:P], wT[:, t], Sbd[:, :], tile_position=(0, q.start)).then_inc(s("wS"), 1)
                        mm(B[7][q, cs], qT[:, t], Sbd[:, :], tile_position=(0, q.start), stop=False, skip_group_check=True).then_inc(s("qS"), 1)
                        pe.wait_ge(s("u"), b * CB + c + 1)
                        mm(B[6][:, 0:P], k_tok[q, cs], u[q, j].rearrange("p h c -> p (h c)"),
                           tile_position=(q.start, 0)).then_inc(s("kU"), 1)
                        if c % 4 == 3:
                            for h in range(H):
                                last = mm(B[7][:, j * P + h * DK:j * P + (h + 1) * DK], at[:, j * H + h, :], u[:, j, h, :],
                                          start=False, stop=True, skip_group_check=True)
                            last.then_inc(s("o_ps"), 1)
                    pe.wait_ge(s("o_tok"), b + 1)
                    for j in range(TB):
                        nc.tensor.transpose(B[1][:, j * P:(j + 1) * P], o_tok[:, j * P:(j + 1) * P], K("ident")).then_inc(s("oT_ps"), 1)
                    for n in range(NBR):
                        x = br[:, n, :] if n < 5 else vT[:, PAD:]
                        if n < 5:
                            pe.wait_ge(s(f"branch{n}"), b + 1)
                        mm(B[2][:, :], K("meanX")[:, NBR - 1 - n:NBR - 1 - n + P], x, start=(n == 0), stop=False)
                        pe.wait_ge(s("abs"), NBR * b + n + 1)
                        mm(B[2][:, :], K("meanA")[:, NBR - 1 - n:NBR - 1 - n + P], absb[:, n % 2, :], start=False, stop=False)
                        pe.wait_ge(s("square"), NBR * b + n + 1)
                        mm(B[2][:, :], K("sumQ")[:, NBR - 1 - n:NBR - 1 - n + P], sqb[:, n % 2, :], start=False, stop=(n == NBR - 1)).then_inc(s("sums"), 1)
                    pe.wait_ge(s("st2"), b + 1)
                    mm(B[3][:, :], K("less_mean2"), st2[:, :]).then_inc(s("mean2"), 1)
                    pe.wait_ge(s("st"), 2 * b + 2)
                    mm(B[5][:, :], W["m1x"][:, :], xnT[:, :], stop=False)
                    mm(B[5][:, :], W["m1s"][:, :], st[:, :], start=False).then_inc(s("hid_ps"), 1)
                    pe.wait_ge(s("hid"), b + 1)
                    for j in range(TB):
                        mm(B[4][:, 128 + j * 24:128 + (j + 1) * 24], hid[:, j * P:(j + 1) * P], W["m2"][:, :], stop=False)
                        last = mm(B[4][:, 128 + j * 24:128 + (j + 1) * 24], W["ones"][0:1, :], W["b2"][0:1, :], start=False)
                    last.then_inc(s("logits"), 1)
                    pe.wait_ge(s("wt"), b + 1)
                    for j in range(TB):
                        nc.tensor.transpose(B[6][0:H * NBR, j * P:(j + 1) * P], wt[:, j].rearrange("p h b -> p (h b)"), K("ident")).then_inc(s("wtT_ps"), 1)
                    pe.wait_ge(s("wtT"), b + 1)
                    for n in range(NBR):
                        if n >= 2:
                            pe.wait_ge(s("mixed"), NBR * b + n - 1)
                        mm(B[(2, 3)[n % 2]][:, :], K(f"spread{n}")[0:H * NBR, :], wtT[:, :]).then_inc(s("spread"), 1)
                    pe.wait_ge(s("fsq"), b + 1)
                    mm(B[5][:, :], K("head_mean"), fsq[:, :]).then_inc(s("ms"), 1)
                    pe.wait_ge(s("fn"), b + 1)
                    for j in range(TB):
                        last = mm(B[0][:, j * P:(j + 1) * P], fn[:, j * P:(j + 1) * P], W["o"][:, :])
                    last.then_inc(s("out_ps"), 1)

            @block.scalar
            def _(act):
                a = nc.scalar.activation
                act.wait_ge(s("zeroed"), 6)
                with act.Fori(0, NB) as b:
                    act.wait_ge(s("ve"), b + 1)
                    a(std[:, :], ve[:, :], ACT.Sqrt).then_inc(s("std"), 1)
                    act.wait_ge(s("xnT_ps"), TB * b + TB)
                    a(xnT[:, :], B[0][:, :], ACT.Copy).then_inc(s("xnT"), 1)
                    for n in range(3):
                        act.wait_ge(s("proj"), 3 * b + n + 1)
                        act.wait_ge(s("halo"), 3 * b + 1)
                        a(pre[:, n, KQ - 1:], B[1 + n][:, :], ACT.Copy).then_inc(s("pre_in"), 1)
                    act.wait_ge(s("beta_ps"), b + 1)
                    a(beta[:, :, :], B[4][:, 0:TB * 8].rearrange("p (j h) -> p j h", h=8)[:, :, 0:H], ACT.Tanh, scale=0.5).then_inc(s("beta_tanh"), 1)
                    for n, (plain, spread, name) in enumerate(((qT, qX, "q"), (kT, kX, "k"))):
                        act.wait_ge(s("conv"), 3 * b + n + 1)
                        a(plain[:, :], conv[:, n, :], ACT.Silu).then_inc(s(name + "T"), 1)
                        for h in range(H):
                            r = slice(h * DK, (h + 1) * DK)
                            a(spread[r, :, h, :], c3(conv[r, n, :]), ACT.Silu).then_inc(s(name + "X"), 1)
                    act.wait_ge(s("conv"), 3 * b + 3)
                    a(vT[:, PAD:], conv[:, 2, :], ACT.Silu).then_inc(s("vT"), 1)
                    for n, (plain, name) in enumerate(((qT, "q"), (kT, "k"))):
                        act.wait_ge(s(name + "T"), b + 1)
                        a(sq[:, n, :], plain[:, :], ACT.Square).then_inc(s("qk_sq"), 1)
                    act.wait_ge(s("nrm"), b + 1)
                    a(root[:, :, :], nrm[:, :, :], ACT.Sqrt).then_inc(s("root"), 1)
                    act.wait_ge(s("k_tok_ps"), TB * b + TB)
                    a(k_tok[:, :], B[1][:, :], ACT.Copy).then_inc(s("k_tok"), 1)
                    for r in range(5):
                        src = Tc if r < 4 else E
                        if r < 4:
                            act.wait_ge(s("Tc"), 4 * b + r + 1)
                            if r:
                                act.wait_ge(s("EUE"), 4 * b + r)
                        else:
                            act.wait_ge(s("E"), 5 * b + 5)
                            act.wait_ge(s("EUE"), 4 * b + 4)
                        for g in range(4):
                            q = slice(g * C, (g + 1) * C)
                            a(X[q, :, q], src[q, :, :], ACT.Copy).then_inc(s("X"), 1)
                    act.wait_ge(s("uw_ps"), b + 1)
                    for n in range(2):
                        uw = B[1 + n][:, :].rearrange("p (j h a c) -> p j h a c", j=2, h=H, a=2)
                        for j in range(2):
                            last = a(w_tok[:, 2 * n + j], uw[:, j, :, 1, :], ACT.Copy)
                    last.then_inc(s("w_tok"), 1)
                    for n in range(2):
                        uw = B[1 + n][:, :].rearrange("p (j h a c) -> p j h a c", j=2, h=H, a=2)
                        for j in range(2):
                            last = a(u0[:, 2 * n + j], uw[:, j, :, 0, :], ACT.Copy)
                    last.then_inc(s("u0"), 1)
                    act.wait_ge(s("wT_ps"), TB * b + TB)
                    a(wT[:, :], B[3][:, :], ACT.Copy).then_inc(s("wT"), 1)
                    a(br[:, 0, :], vT[:, PAD:], ACT.Copy, scale=W["fir"][:, 0:1]).then_inc(s("branch0"), 1)
                    for n in range(NBR):
                        if n == 4:
                            act.wait_ge(s("oT_ps"), TB * b + TB)
                            a(br[:, 4, :], B[1][:, :], ACT.Copy).then_inc(s("branch4"), 1)
                        x = br[:, n, :] if n < 5 else vT[:, PAD:]
                        if n < 5:
                            act.wait_ge(s(f"branch{n}"), b + 1)
                        if n >= 2:
                            act.wait_ge(s("sums"), NBR * b + n - 1)
                        a(absb[:, n % 2, :], x, ACT.Abs).then_inc(s("abs"), 1)
                        a(sqb[:, n % 2, :], x, ACT.Square).then_inc(s("square"), 1)
                    act.wait_ge(s("sums"), NBR * b + NBR)
                    a(st2[:, :], B[2][:, :], ACT.Square).then_inc(s("st2"), 1)
                    a(st[0:64, :], B[2][0:64, :], ACT.Copy).then_inc(s("st"), 1)
                    act.wait_ge(s("var"), 2 * b + 2)
                    a(st[64:P, :], var[64:P, :], ACT.Sqrt).then_inc(s("st"), 1)
                    act.wait_ge(s("hid_ps"), b + 1)
                    a(hid[:, :], B[5][:, :], ACT.Gelu, bias=W["b1"][:, 0:1]).then_inc(s("hid"), 1)
                    act.wait_ge(s("lg"), 3 * b + 3)
                    a(ex[:, :, :, :], lg[:, :, :, :], ACT.Exp).then_inc(s("ex"), 1)
                    act.wait_ge(s("wtT_ps"), TB * b + TB)
                    a(wtT[:, :], B[6][0:H * NBR, :], ACT.Copy).then_inc(s("wtT"), 1)
                    act.wait_ge(s("fu"), 6 * b + 6)
                    a(fsq[:, :], fu[:, :], ACT.Square).then_inc(s("fsq"), 1)
                    act.wait_ge(s("ms"), b + 1)
                    a(lnv[:, :], B[5][:, :], ACT.Ln, bias=K("eps5")).then_inc(s("lnv"), 1)
                    act.wait_ge(s("lnv"), b + 1)
                    a(rr[:, :], lnv[:, :], ACT.Exp, scale=-0.5).then_inc(s("rr"), 1)

            @block.vector
            def _(dve):
                v = nc.vector
                dve.sem_inc(s("out_added"), 1)
                dve.sem_inc(s("halo"), 1)
                dve.wait_ge(s("zeroed"), 6)
                v.tensor_copy(Sbd[:, :], Sbd[:, :]).then_inc(s("state"), 1)
                with dve.Fori(0, NB) as b:
                    layernorm_moments(nc, dve, s, b, x_sb, stats, mv, ve)
                    layernorm_apply(nc, dve, s, b, x_sb, mv, std, rstd, xn)
                    for n in range(3):
                        dve.wait_ge(s("pre_in"), 3 * b + n + 1)
                        v.tensor_scalar(conv[:, n, :], pre[:, n, 0:BL], W["taps"][:, n, 0:1], None, ALU.mult).then_inc(s("tap"), 1)
                        for k in range(1, KQ):
                            dve.wait_ge(s("tap"), 9 * b + 3 * n + k)
                            ins = v.scalar_tensor_tensor(conv[:, n, :], pre[:, n, k:k + BL], W["taps"][:, n, k:k + 1], conv[:, n, :],
                                                         ALU.mult, ALU.add)
                            ins.then_inc(s("conv" if k == KQ - 1 else "tap"), 1)
                    dve.wait_ge(s("conv"), 3 * b + 3)
                    for n in range(3):
                        v.tensor_copy(pre[:, n, 0:KQ - 1], pre[:, n, BL:BL + KQ - 1]).then_inc(s("halo"), 1)
                    dve.wait_ge(s("beta_tanh"), b + 1)
                    v.tensor_scalar(beta[:, :, :], beta[:, :, :], 0.5, 0.5, ALU.mult, ALU.add).then_inc(s("beta"), 1)
                    dve.wait_ge(s("norms_ps"), b + 1)
                    v.tensor_scalar(nrm[:, :, :], B[4][:, 64:64 + TB * 8].rearrange("p (j h) -> p j h", h=8), 1e-6, None, ALU.add).then_inc(s("nrm"), 1)
                    dve.wait_ge(s("root"), b + 1)
                    v.reciprocal(rn[:, :, :], root[:, :, :]).then_inc(s("rn"), 1)
                    dve.wait_ge(s("rn"), b + 1)
                    dve.wait_ge(s("beta"), b + 1)
                    v.tensor_tensor(rkb[:, :, :], beta[:, :, :], rn[:, :, H:2 * H], ALU.mult).then_inc(s("rkb"), 1)
                    dve.wait_ge(s("rkb"), b + 1)
                    v.tensor_tensor(gam[:, :, :], rkb[:, :, :], rn[:, :, H:2 * H], ALU.mult).then_inc(s("gam"), 1)
                    dve.wait_ge(s("gam"), b + 1)

                    def heads(t):
                        return t.rearrange("p (g c) -> p g c", c=DK)

                    def per_head(t):
                        return t.rearrange("p j h -> p (j h)").unsqueeze(2).to_broadcast([P, TB * H, DK])

                    vk3 = vk[:, :, :, :, :].rearrange("p j h a c -> p (j h) a c")
                    dve.wait_ge(s("k_tok_ps"), TB * b + TB)
                    dve.wait_ge(s("k_tok"), b + 1)
                    v.tensor_tensor(vk3[:, :, 1, :], heads(B[1][:, :]), per_head(gam[:, :, :]), ALU.mult).then_inc(s("vk"), 1)
                    dve.wait_ge(s("v_tok_ps"), TB * b + TB)
                    v.tensor_tensor(vk3[:, :, 0, :], heads(B[2][:, :]), per_head(rkb[:, :, :]), ALU.mult).then_inc(s("vk"), 1)
                    for j in range(TB):
                        dve.wait_ge(s("gram"), TB * b + j + 1)
                        for h in range(H):
                            last = v.scalar_tensor_tensor(A[:, j * H + h, :], B[3][:, h * P:(h + 1) * P], gam[:, j, h:h + 1], K("lower"),
                                                          ALU.mult, ALU.mult)
                        last.then_inc(s("A"), 1)
                        dve.wait_ge(s("attn_ps"), TB * b + j + 1)
                        v.tensor_tensor(at[:, j * H:(j + 1) * H, :], c3(B[5][:, :]),
                                        K("upper").unsqueeze(1).to_broadcast([P, H, P]), ALU.mult).then_inc(s("attn"), 1)
                    dve.wait_ge(s("A"), TB * b + TB)
                    for g in range(4):
                        q = slice(g * C, (g + 1) * C)
                        last = v.transpose(Tc[q, :, :], A[q, :, q])
                    last.then_inc(s("AT"), 1)
                    dve.wait_ge(s("AT"), b + 1)

                    def all_heads(m):
                        return m.unsqueeze(1).to_broadcast([P, TB * H, C])

                    v.tensor_tensor(Pm[:, :, :], Tc[:, :, :], all_heads(K("level1")), ALU.mult).then_inc(s("E0"), 1)
                    dve.wait_ge(s("E0"), b + 1)
                    v.tensor_tensor(E[:, :, :], Pm[:, :, :], all_heads(K("eye32")), ALU.add).then_inc(s("E"), 1)
                    for r in range(4):
                        m = 2 << r
                        dve.wait_ge(s("E"), 5 * b + r + 1)
                        v.transpose(Tc[:, :, :].rearrange("p n c -> p (n c)"), E[:, :, :].rearrange("p n c -> p (n c)")).then_inc(s("Tc"), 1)
                        dve.wait_ge(s("UE"), 4 * b + r + 1)
                        v.tensor_tensor(Pm[:, :, :], B[3][:, :].rearrange("p (n c) -> p n c", c=C), all_heads(K(f"level{m}")), ALU.mult).then_inc(s("Pm"), 1)
                        dve.wait_ge(s("EUE"), 4 * b + r + 1)
                        if r == 3:
                            dve.wait_ge(s("Tc"), 4 * b + 4)
                        v.tensor_tensor(E[:, :, :], E[:, :, :], B[5][:, :].rearrange("p (n c) -> p n c", c=C), ALU.add).then_inc(s("E"), 1)
                    dve.wait_ge(s("u0"), b + 1)
                    for c in range(CB):
                        j, q = c // 4, slice((c % 4) * C, (c % 4 + 1) * C)
                        dve.wait_ge(s("wS"), CB * b + c + 1)
                        v.tensor_tensor(u[q, j], u0[q, j], B[5][q, 0:P].rearrange("p (h c) -> p h c", c=DK), ALU.subtract).then_inc(s("u"), 1)
                        dve.wait_ge(s("kU"), CB * b + c + 1)
                        dve.wait_ge(s("qS"), CB * b + c + 1)
                        v.tensor_tensor(tmp[:, 0, 0:P], B[6][:, 0:P], K("same32"), ALU.mult).then_inc(s("kU_own"), 1)
                        dve.wait_ge(s("kU_own"), CB * b + c + 1)
                        v.tensor_tensor(Sbd[:, :], Sbd[:, :], tmp[:, 0, 0:P], ALU.add).then_inc(s("state"), 1)
                    dve.wait_ge(s("o_ps"), TB * b + TB)
                    v.tensor_tensor(o_tok[:, :].rearrange("p (j h c) -> p j h c", j=TB, c=DK), B[7][:, :].rearrange("p (j h c) -> p j h c", j=TB, c=DK),
                                    rn[:, :, 0:H].unsqueeze(3).to_broadcast([P, TB, H, DK]), ALU.mult).then_inc(s("o_tok"), 1)
                    tap = len(FIRS[:1])
                    for n, taps in enumerate(FIRS):
                        if n == 0:
                            continue
                        total = sum(FIRS[1:]) - len(FIRS[1:])
                        done = sum(FIRS[1:n]) - len(FIRS[1:n])
                        v.tensor_scalar(br[:, n, :], vT[:, PAD - taps + 1:PAD - taps + 1 + BL], W["fir"][:, tap:tap + 1], None, ALU.mult).then_inc(s("fir_tap"), 1)
                        for k in range(1, taps):
                            dve.wait_ge(s("fir_tap"), total * b + done + k)
                            ins = v.scalar_tensor_tensor(br[:, n, :], vT[:, PAD - taps + 1 + k:PAD - taps + 1 + k + BL], W["fir"][:, tap + k:tap + k + 1],
                                                         br[:, n, :], ALU.mult, ALU.add)
                            ins.then_inc(s(f"branch{n}" if k == taps - 1 else "fir_tap"), 1)
                        tap += taps
                    dve.wait_ge(s("st2"), b + 1)
                    v.tensor_copy(var[64:P, :], B[2][64:P, :]).then_inc(s("var0"), 1)
                    dve.wait_ge(s("mean2"), b + 1)
                    dve.wait_ge(s("var0"), b + 1)
                    v.tensor_tensor(var[64:P, :], var[64:P, :], B[3][64:P, :], ALU.add).then_inc(s("var"), 1)
                    dve.wait_ge(s("var"), 2 * b + 1)
                    v.tensor_scalar(var[64:P, :], var[64:P, :], 0.0, None, ALU.max).then_inc(s("var"), 1)
                    dve.wait_ge(s("logits"), b + 1)
                    v.tensor_tensor(lg[:, :, :, :], B[4][:, 128:128 + TB * 24].rearrange("p (j h n) -> p j h n", j=TB, h=H),
                                    W["itemp"][:, :].unsqueeze(1).unsqueeze(3).to_broadcast([P, TB, H, NBR]), ALU.mult).then_inc(s("lg"), 1)
                    dve.wait_ge(s("lg"), 3 * b + 1)
                    v.tensor_reduce(mx[:, :, :], lg[:, :, :, :], AX.X, ALU.max).then_inc(s("lg"), 1)
                    dve.wait_ge(s("lg"), 3 * b + 2)
                    v.tensor_tensor(lg[:, :, :, :], lg[:, :, :, :], mx[:, :, :].unsqueeze(3).to_broadcast([P, TB, H, NBR]), ALU.subtract).then_inc(s("lg"), 1)
                    dve.wait_ge(s("ex"), b + 1)
                    v.tensor_reduce(sm[:, :, :], ex[:, :, :, :], AX.X, ALU.add).then_inc(s("sm"), 1)
                    dve.wait_ge(s("sm"), b + 1)
                    v.reciprocal(rs[:, :, :], sm[:, :, :]).then_inc(s("rs"), 1)
                    dve.wait_ge(s("rs"), b + 1)
                    v.tensor_tensor(wt[:, :, :, :], ex[:, :, :, :], rs[:, :, :].unsqueeze(3).to_broadcast([P, TB, H, NBR]), ALU.mult).then_inc(s("wt"), 1)
                    for n in range(NBR):
                        x = br[:, n, :] if n < 5 else vT[:, PAD:]
                        dve.wait_ge(s("spread"), NBR * b + n + 1)
                        if n >= 2:
                            dve.wait_ge(s("fu"), 6 * b + n)
                        dst = fu[:, :] if n == 0 else tmp[:, n % 2, :]
                        ins = v.tensor_tensor(dst, x, B[(2, 3)[n % 2]][:, :], ALU.mult)
                        ins.then_inc(s("mixed"), 1)
                        if n == 0:
                            v.tensor_copy(Pm[:, 0, :], Pm[:, 0, :]).then_inc(s("fu"), 1)
                        else:
                            dve.wait_ge(s("mixed"), NBR * b + n + 1)
                            v.tensor_tensor(fu[:, :], fu[:, :], tmp[:, n % 2, :], ALU.add).then_inc(s("fu"), 1)
                    dve.wait_ge(s("fu"), 6 * b + 6)
                    v.tensor_copy(vT[:, 0:PAD], vT[:, BL:BL + PAD]).then_inc(s("v_halo"), 1)
                    dve.wait_ge(s("rr"), b + 1)
                    v.scalar_tensor_tensor(fn[:, :], fu[:, :], W["onorm"][:, 0:1], rr[:, :], ALU.mult, ALU.mult).then_inc(s("fn"), 1)
                    dve.wait_ge(s("out_ps"), b + 1)
                    v.tensor_tensor(columns(x_sb, b, 0), columns(x_sb, b, 0), B[0][:, :], ALU.add).then_inc(s("out_added"), 1)
        s.clear()


NL, RL = 8, 8


def phase_lora(nc, x_sb, K, W):
    with ExitStack() as ctx:
        def sb(name, *shape, dt=F32):
            return ctx.enter_context(nc.sbuf_tensor("lora_" + name, list(shape), dt))

        s = Signals(nc, "lora")
        stats, mv, ve, std, rstd, xn, xnT = layernorm_buffers(sb)
        mid = sb("mid", P, TB, RL)
        lg = sb("lg", P, TB, NL)
        mx = sb("mx", P, TB)
        ex = sb("ex", P, TB, NL)
        sm = sb("sm", P, TB)
        rs = sb("rs", P, TB)
        gate = sb("gate", P, TB, NL, dt=mybir.dt.bfloat16)
        outer = sb("outer", P, TB, P)
        outerT = sb("outerT", NL * RL, BL)
        B = [ctx.enter_context(nc.psum_tensor(f"lora_bank{n}", [P, BL], F32)) for n in range(4)]

        with nc.Block() as block:
            @block.tensor
            def _(pe):
                pe.sem_inc(s("y"), 1)
                with pe.Fori(0, NB) as b:
                    pe.wait_ge(s("xn"), TB * b + TB)
                    for j in range(TB):
                        nc.tensor.transpose(B[0][:, j * P:(j + 1) * P], xn[:, j * P:(j + 1) * P], K("ident")).then_inc(s("xnT_ps"), 1)
                    pe.wait_ge(s("xnT"), b + 1)
                    for j in range(TB):
                        c = slice(j * 16, (j + 1) * 16)
                        nc.tensor.matmul(B[1][:, c], xnT[:, j * P:(j + 1) * P], W["mid_route"][:, :], start=True, stop=False)
                        last = nc.tensor.matmul(B[1][:, c], W["ones"][:, :], W["mid_route_b"][:, :], start=False, stop=True)
                    last.then_inc(s("small"), 1)
                    pe.wait_ge(s("outer"), b + 1)
                    for j in range(TB):
                        nc.tensor.transpose(B[2][:, j * P:(j + 1) * P], outer[:, j, :], K("ident")).then_inc(s("outerT_ps"), 1)
                    pe.wait_ge(s("outerT"), b + 1)
                    pe.wait_ge(s("added"), b + 1)
                    for j in range(TB):
                        c = slice(j * P, (j + 1) * P)
                        nc.tensor.matmul(B[3][:, c], xnT[:, c], W["base"][:, :], start=True, stop=False)
                        nc.tensor.matmul(B[3][:, c], W["ones"][:, :], W["base_b"][:, :], start=False, stop=False)
                        last = nc.tensor.matmul(B[3][:, c], outerT[:, c], W["lora_b"][:, :], start=False, stop=True)
                    last.then_inc(s("y"), 1)

            @block.scalar
            def _(act):
                a = nc.scalar.activation
                with act.Fori(0, NB) as b:
                    act.wait_ge(s("ve"), b + 1)
                    a(std[:, :], ve[:, :], ACT.Sqrt).then_inc(s("std"), 1)
                    act.wait_ge(s("xnT_ps"), TB * b + TB)
                    act.wait_ge(s("y"), b + 1)
                    a(xnT[:, :], B[0][:, :], ACT.Copy).then_inc(s("xnT"), 1)
                    act.wait_ge(s("shifted"), b + 1)
                    a(ex[:, :, :], lg[:, :, :], ACT.Exp).then_inc(s("ex"), 1)
                    act.wait_ge(s("outerT_ps"), TB * b + TB)
                    a(outerT[:, :], B[2][0:NL * RL, :], ACT.Copy).then_inc(s("outerT"), 1)

            @block.vector
            def _(dve):
                v = nc.vector
                dve.sem_inc(s("added"), 1)
                v.memset(outer[:, :, :], 0.0).then_inc(s("outer_zero"), 1)
                dve.wait_ge(s("outer_zero"), 1)
                with dve.Fori(0, NB) as b:
                    layernorm_moments(nc, dve, s, b, x_sb, stats, mv, ve)
                    layernorm_apply(nc, dve, s, b, x_sb, mv, std, rstd, xn)
                    small = B[1][:, 0:TB * 16].rearrange("p (j c) -> p j c", c=16)
                    dve.wait_ge(s("small"), b + 1)
                    v.tensor_copy(mid[:, :, :], small[:, :, 0:RL]).then_inc(s("mid"), 1)
                    v.tensor_copy(lg[:, :, :], small[:, :, RL:16]).then_inc(s("lg"), 1)
                    dve.wait_ge(s("lg"), b + 1)
                    v.tensor_reduce(mx[:, :], lg[:, :, :], AX.X, ALU.max).then_inc(s("mx"), 1)
                    dve.wait_ge(s("mx"), b + 1)
                    v.tensor_tensor(lg[:, :, :], lg[:, :, :], mx[:, :].unsqueeze(2).to_broadcast([P, TB, NL]), ALU.subtract).then_inc(s("shifted"), 1)
                    dve.wait_ge(s("ex"), b + 1)
                    v.tensor_reduce(sm[:, :], ex[:, :, :], AX.X, ALU.add).then_inc(s("sm"), 1)
                    dve.wait_ge(s("sm"), b + 1)
                    v.reciprocal(rs[:, :], sm[:, :]).then_inc(s("rs"), 1)
                    dve.wait_ge(s("rs"), b + 1)
                    v.tensor_tensor(gate[:, :, :], ex[:, :, :], rs[:, :].unsqueeze(2).to_broadcast([P, TB, NL]), ALU.mult).then_inc(s("gate"), 1)
                    dve.wait_ge(s("gate"), b + 1)
                    dve.wait_ge(s("mid"), b + 1)
                    for j in range(TB):
                        last = v.tensor_tensor(outer[:, j, 0:NL * RL].rearrange("p (e r) -> p e r", r=RL), gate[:, j, :].unsqueeze(2).to_broadcast([P, NL, RL]),
                                               mid[:, j, :].unsqueeze(1).to_broadcast([P, NL, RL]), ALU.mult)
                    last.then_inc(s("outer"), 1)
                    dve.wait_ge(s("y"), b + 2)
                    v.tensor_tensor(columns(x_sb, b, 0), columns(x_sb, b, 0), B[3][:, :], ALU.add).then_inc(s("added"), 1)
        s.clear()


HL, DL = 16, 8
GH = 4
VE = DL + 1


def phase_linear(nc, x_sb, K, W):
    with ExitStack() as ctx:
        def sb(name, *shape):
            return ctx.enter_context(nc.sbuf_tensor("linear_" + name, list(shape), F32))

        s = Signals(nc, "linear")
        stats, mv, ve, std, rstd, xn, xnT = layernorm_buffers(sb)
        qT = sb("qT", P, BL)
        kT = sb("kT", P, BL)
        qX = sb("qX", P, GH, BL)
        k_tok = sb("k_tok", P, BL)
        v1 = sb("v1", P, TB, HL, VE)
        sc = sb("sc", P, 2, HL, P)
        own = sb("own", P, HL * VE)
        state = sb("state", P, HL * VE)
        den = sb("den", P, TB, HL)
        rden = sb("rden", P, TB, HL)
        a_tok = sb("a_tok", P, BL)
        aT = sb("aT", P, BL)
        B = [ctx.enter_context(nc.psum_tensor(f"linear_bank{n}", [P, BL], F32)) for n in range(8)]

        with nc.Block() as block:
            @block.gpsimd
            def _(pool):
                nc.gpsimd.memset(state[:], 0.0).then_inc(s("state"), 1)
                nc.gpsimd.memset(v1[:], 1.0).then_inc(s("v_ones"), 1)

            @block.tensor
            def _(pe):
                mm = nc.tensor.matmul
                with pe.Fori(0, NB) as b:
                    pe.wait_ge(s("xn"), TB * b + TB)
                    for j in range(TB):
                        nc.tensor.transpose(B[0][:, j * P:(j + 1) * P], xn[:, j * P:(j + 1) * P], K("ident")).then_inc(s("xnT_ps"), 1)
                    pe.wait_ge(s("xnT"), b + 1)
                    pe.wait_ge(s("added"), b + 1)
                    for n in range(2):
                        mm(B[1 + n][:, :], W["lin_qkv"][:, n, :], xnT[:, :], start=True, stop=True).then_inc(s("qk_ps"), 1)
                    for n in range(2):
                        for j in range(TB):
                            c = slice(j * P, (j + 1) * P)
                            mm(B[3 + n][:, c], xnT[:, c], W["lin_qkv"][:, 1 + n, :], start=True, stop=False)
                            last = mm(B[3 + n][:, c], W["ones"][:, :], W["lin_b"][:, (1 + n) * P:(2 + n) * P], start=False, stop=True)
                        last.then_inc(s("kv_ps"), 1)
                    pe.wait_ge(s("kT"), b + 1)
                    pe.wait_ge(s("qX"), GH * b + GH)
                    pe.wait_ge(s("k_tok"), b + 1)
                    pe.wait_ge(s("v1"), b + 1)
                    for j in range(TB):
                        c = slice(j * P, (j + 1) * P)
                        pe.wait_ge(s("sc"), 4 * TB * b + 4 * j + 1)
                        for g in range(4):
                            r = slice(g * 32, (g + 1) * 32)
                            mm(B[1 + g][:, :].rearrange("p (h t) -> p h t", t=P), kT[r, c], qX[r, :, c], start=True, stop=True,
                               tile_position=(g * 32, 0)).then_inc(s("sc_ps"), 1)
                        o = B[5 + j // 2][:, (j % 2) * 256:(j % 2) * 256 + HL * VE]
                        pe.wait_ge(s("state"), TB * b + j + 1)
                        mm(o, qT[:, c], state[:, :], start=True, stop=False, skip_group_check=True).then_inc(s("inter"), 1)
                        mm(B[7][:, 0:HL * VE], k_tok[:, c], v1[:, j].rearrange("p h e -> p (h e)"), start=True, stop=True).then_inc(s("kv"), 1)
                        for g in range(4):
                            pe.wait_ge(s("sc"), 4 * TB * b + 4 * j + g + 2)
                            for i in range(GH):
                                h = g * GH + i
                                last = mm(o[:, h * VE:(h + 1) * VE], sc[:, j % 2, h, :], v1[:, j, h, :], start=False, stop=True, skip_group_check=True)
                        last.then_inc(s("o_ps"), 1)
                    pe.wait_ge(s("a_tok"), b + 1)
                    for j in range(TB):
                        nc.tensor.transpose(B[0][:, j * P:(j + 1) * P], a_tok[:, j * P:(j + 1) * P], K("ident")).then_inc(s("aT_ps"), 1)
                    pe.wait_ge(s("aT"), b + 1)
                    for j in range(TB):
                        c = slice(j * P, (j + 1) * P)
                        mm(B[1][:, c], aT[:, c], W["lin_out"][:, :], start=True, stop=False)
                        last = mm(B[1][:, c], W["ones"][:, :], W["lin_out_b"][:, :], start=False, stop=True)
                    last.then_inc(s("y"), 1)

            @block.scalar
            def _(act):
                a = nc.scalar.activation
                act.wait_ge(s("v_ones"), 1)
                with act.Fori(0, NB) as b:
                    act.wait_ge(s("ve"), b + 1)
                    a(std[:, :], ve[:, :], ACT.Sqrt).then_inc(s("std"), 1)
                    act.wait_ge(s("xnT_ps"), TB * b + TB)
                    a(xnT[:, :], B[0][:, :], ACT.Copy).then_inc(s("xnT"), 1)
                    act.wait_ge(s("kv_ps"), 2 * b + 2)
                    a(v1[:, :, :, 0:DL].rearrange("p j h e -> p (j h) e"), B[4][:, :].rearrange("p (g e) -> p g e", e=DL), ACT.Copy).then_inc(s("v1"), 1)
                    act.wait_ge(s("aT_ps"), TB * b + TB)
                    a(aT[:, :], B[0][:, :], ACT.Copy).then_inc(s("aT"), 1)

            @block.vector
            def _(dve):
                v = nc.vector
                dve.sem_inc(s("added"), 1)
                dve.sem_inc(s("sc"), 1)
                with dve.Fori(0, NB) as b:
                    layernorm_moments(nc, dve, s, b, x_sb, stats, mv, ve)
                    layernorm_apply(nc, dve, s, b, x_sb, mv, std, rstd, xn)
                    for n, (t, name) in enumerate(((qT, "qT"), (kT, "kT"))):
                        dve.wait_ge(s("qk_ps"), 2 * b + n + 1)
                        v.tensor_scalar(t[:, :], B[1 + n][:, :], W["lin_b_eps"][:, n:n + 1], 1e-6, ALU.add, ALU.max).then_inc(s(name), 1)
                    dve.wait_ge(s("qT"), b + 1)
                    for i in range(GH):
                        v.tensor_scalar(qX[:, i, :], qT[:, :], K("head_of4")[:, i:i + 1], None, ALU.mult).then_inc(s("qX"), 1)
                    dve.wait_ge(s("kv_ps"), 2 * b + 1)
                    v.tensor_scalar(k_tok[:, :], B[3][:, :], 1e-6, 1e-6, ALU.add, ALU.max).then_inc(s("k_tok"), 1)
                    dve.wait_ge(s("k_tok"), b + 1)
                    dve.wait_ge(s("v1"), b + 1)
                    for j in range(TB):
                        for g in range(4):
                            dve.wait_ge(s("sc_ps"), 4 * TB * b + 4 * j + g + 1)
                            v.tensor_tensor(sc[:, j % 2, g * GH:(g + 1) * GH, :], B[1 + g][:, :].rearrange("p (h t) -> p h t", t=P),
                                            K("causal").unsqueeze(1).to_broadcast([P, GH, P]), ALU.mult).then_inc(s("sc"), 1)
                        dve.wait_ge(s("kv"), TB * b + j + 1)
                        v.tensor_tensor(own[:, :], B[7][:, 0:HL * VE], K("head_own"), ALU.mult).then_inc(s("own"), 1)
                        dve.wait_ge(s("own"), TB * b + j + 1)
                        dve.wait_ge(s("inter"), TB * b + j + 1)
                        v.tensor_tensor(state[:, :], state[:, :], own[:, :], ALU.add).then_inc(s("state"), 1)
                    dve.wait_ge(s("o_ps"), TB * b + TB)

                    def pair(n):
                        return B[5 + n][:, :].rearrange("p (j c) -> p j c", j=2)[:, :, 0:HL * VE].rearrange("p j (h e) -> p j h e", e=VE)

                    for n in range(2):
                        last = v.tensor_scalar(den[:, 2 * n:2 * n + 2, :], pair(n)[:, :, :, DL], 1e-6, None, ALU.max)
                    last.then_inc(s("den"), 1)
                    dve.wait_ge(s("den"), b + 1)
                    v.reciprocal(rden[:, :, :], den[:, :, :]).then_inc(s("rden"), 1)
                    dve.wait_ge(s("rden"), b + 1)
                    for j in range(TB):
                        last = v.tensor_tensor(a_tok[:, j * P:(j + 1) * P].rearrange("p (h e) -> p h e", e=DL), pair(j // 2)[:, j % 2, :, 0:DL],
                                               rden[:, j, :].unsqueeze(2).to_broadcast([P, HL, DL]), ALU.mult)
                    last.then_inc(s("a_tok"), 1)
                    dve.wait_ge(s("y"), b + 1)
                    v.tensor_tensor(columns(x_sb, b, 0), columns(x_sb, b, 0), B[1][:, :], ALU.add).then_inc(s("added"), 1)
        s.clear()


HC = [(c, min(P, HID - c)) for c in range(0, HID, P)]


def phase_experts(nc, x_sb, K, W, weights_loaded, out):
    with ExitStack() as ctx:
        def sb(name, *shape):
            return ctx.enter_context(nc.sbuf_tensor("experts_" + name, list(shape), F32))

        s = Signals(nc, "experts")
        stats, mv, ve, std, rstd, xn, xnT = layernorm_buffers(sb)
        lg = sb("lg", P, TB, EXP)
        mx = sb("mx", P, TB)
        ex = sb("ex", P, TB, EXP)
        sm = sb("sm", P, TB)
        rs = sb("rs", P, TB)
        p = sb("p", P, TB, EXP)
        over = sb("over", P, TB, EXP, EXP)
        ties = sb("ties", P, TB, EXP, EXP)
        rank = sb("rank", P, TB, EXP)
        cw = sb("cw", P, TB, EXP)
        h1 = sb("h1", P, 2, BL)
        h = sb("h", P, 2, BL)
        B = [ctx.enter_context(nc.psum_tensor(f"experts_bank{n}", [P, BL], F32)) for n in range(8)]
        y_dram = out.rearrange("a (t p) d -> p (a t) d", p=P)
        STEPS = [(e, n) for e in range(EXP) for n in range(len(HC))]
        NS = len(STEPS)

        with nc.Block() as block:
            @block.sync
            def _(sp):
                with sp.Fori(0, NB) as b:
                    sp.wait_ge(s("added"), EXP * b + EXP + 1)
                    sp.dma_start(y_dram[:, bass.ds(b * TB, TB), :], columns(x_sb, b, 0).rearrange("p (t d) -> p t d", d=D)).then_inc(s("stored"), 16)
                sp.wait_ge(s("stored"), 16 * NB)

            @block.tensor
            def _(pe):
                mm = nc.tensor.matmul
                pe.wait_ge(weights_loaded[0], weights_loaded[1])
                with pe.Fori(0, NB) as b:
                    pe.wait_ge(s("xn"), TB * b + TB)
                    for j in range(TB):
                        nc.tensor.transpose(B[6][:, j * P:(j + 1) * P], xn[:, j * P:(j + 1) * P], K("ident")).then_inc(s("xnT_ps"), 1)
                    pe.wait_ge(s("xnT"), b + 1)
                    for j in range(TB):
                        last = mm(B[7][:, j * EXP:(j + 1) * EXP], xnT[:, j * P:(j + 1) * P], W["gate"][:, 0:EXP], start=True, stop=True)
                    last.then_inc(s("gate_ps"), 1)

                    def up(i):
                        e, n = STEPS[i]
                        c, m = HC[n]
                        pe.wait_ge(s("h1"), NS * b + i - 1) if i >= 2 else pe.wait_ge(s("h"), NS * b + 1)
                        mm(B[i % 2][0:m, :], W["w1"][:, e, c:c + m], xnT[:, :], start=True, stop=True).then_inc(s("h1_ps"), 1)
                        if i >= 2:
                            pe.wait_ge(s("h"), NS * b + i)
                        mm(B[2 + i % 2][0:m, :], W["w3"][:, e, c:c + m], xnT[:, :], start=True, stop=True).then_inc(s("h3_ps"), 1)

                    def down(i):
                        e, n = STEPS[i]
                        m = HC[n][1]
                        pe.wait_ge(s("h"), NS * b + i + 2)
                        if n == 0:
                            pe.wait_ge(s("added"), EXP * b + max(e, 1))
                        for j in range(TB):
                            last = mm(B[4 + e % 2][:, j * P:(j + 1) * P], h[0:m, i % 2, j * P:(j + 1) * P], W["w2"][0:m, e, n, :],
                                      start=(n == 0 and j == 0), stop=(n == len(HC) - 1), skip_group_check=True)
                        last.then_inc(s("y_part"), 1)

                    up(0)
                    for i in range(NS):
                        if i + 1 < NS:
                            up(i + 1)
                        down(i)

            @block.scalar
            def _(act):
                a = nc.scalar.activation
                with act.Fori(0, NB) as b:
                    act.wait_ge(s("ve"), b + 1)
                    a(std[:, :], ve[:, :], ACT.Sqrt).then_inc(s("std"), 1)
                    act.wait_ge(s("xnT_ps"), TB * b + TB)
                    a(xnT[:, :], B[6][:, :], ACT.Copy).then_inc(s("xnT"), 1)
                    act.wait_ge(s("shifted"), b + 1)
                    a(ex[:, :, :], lg[:, :, :], ACT.Exp).then_inc(s("ex"), 1)
                    for i, (e, n) in enumerate(STEPS):
                        m = HC[n][1]
                        act.wait_ge(s("h1_ps"), NS * b + i + 1)
                        if i >= 2:
                            act.wait_ge(s("h"), NS * b + i)
                        a(h1[0:m, i % 2, :], B[i % 2][0:m, :], ACT.Silu).then_inc(s("h1"), 1)

            @block.vector
            def _(dve):
                v = nc.vector
                dve.sem_inc(s("added"), 1)
                dve.sem_inc(s("h"), 1)
                with dve.Fori(0, NB) as b:
                    layernorm_moments(nc, dve, s, b, x_sb, stats, mv, ve)
                    layernorm_apply(nc, dve, s, b, x_sb, mv, std, rstd, xn)
                    dve.wait_ge(s("gate_ps"), b + 1)
                    v.tensor_copy(lg[:, :, :], B[7][:, 0:TB * EXP].rearrange("p (j e) -> p j e", e=EXP)).then_inc(s("lg"), 1)
                    dve.wait_ge(s("lg"), b + 1)
                    v.tensor_reduce(mx[:, :], lg[:, :, :], AX.X, ALU.max).then_inc(s("mx"), 1)
                    dve.wait_ge(s("mx"), b + 1)
                    v.tensor_tensor(lg[:, :, :], lg[:, :, :], mx[:, :].unsqueeze(2).to_broadcast([P, TB, EXP]), ALU.subtract).then_inc(s("shifted"), 1)
                    dve.wait_ge(s("ex"), b + 1)
                    v.tensor_reduce(sm[:, :], ex[:, :, :], AX.X, ALU.add).then_inc(s("sm"), 1)
                    dve.wait_ge(s("sm"), b + 1)
                    v.reciprocal(rs[:, :], sm[:, :]).then_inc(s("rs"), 1)
                    dve.wait_ge(s("rs"), b + 1)
                    v.tensor_tensor(p[:, :, :], ex[:, :, :], rs[:, :].unsqueeze(2).to_broadcast([P, TB, EXP]), ALU.mult).then_inc(s("p"), 1)
                    dve.wait_ge(s("p"), b + 1)
                    for j in range(TB):
                        theirs = p[:, j, :].unsqueeze(1).to_broadcast([P, EXP, EXP])
                        mine = p[:, j, :].unsqueeze(2).to_broadcast([P, EXP, EXP])
                        v.tensor_tensor(over[:, j], theirs, mine, ALU.is_gt).then_inc(s("compared"), 1)
                        v.tensor_tensor(ties[:, j], theirs, mine, ALU.is_equal).then_inc(s("compared"), 1)
                    dve.wait_ge(s("compared"), 2 * TB * b + 2 * TB)
                    v.tensor_tensor(ties[:, :].rearrange("p j e f -> p j (e f)"), ties[:, :].rearrange("p j e f -> p j (e f)"),
                                    K("earlier").unsqueeze(1).to_broadcast([P, TB, EXP * EXP]), ALU.mult).then_inc(s("ties"), 1)
                    dve.wait_ge(s("ties"), b + 1)
                    v.tensor_tensor(over[:, :], over[:, :], ties[:, :], ALU.add).then_inc(s("over"), 1)
                    dve.wait_ge(s("over"), b + 1)
                    v.tensor_reduce(rank[:, :, :], over[:, :, :, :], AX.X, ALU.add).then_inc(s("rank"), 1)
                    dve.wait_ge(s("rank"), b + 1)
                    v.scalar_tensor_tensor(cw[:, :, :], rank[:, :, :], 1.5, p[:, :, :], ALU.is_lt, ALU.mult).then_inc(s("cw"), 1)
                    dve.wait_ge(s("cw"), 2 * b + 1)
                    v.tensor_reduce(sm[:, :], cw[:, :, :], AX.X, ALU.add).then_inc(s("sm2"), 1)
                    dve.wait_ge(s("sm2"), b + 1)
                    v.reciprocal(rs[:, :], sm[:, :]).then_inc(s("rs2"), 1)
                    dve.wait_ge(s("rs2"), b + 1)
                    v.tensor_tensor(cw[:, :, :], cw[:, :, :], rs[:, :].unsqueeze(2).to_broadcast([P, TB, EXP]), ALU.mult).then_inc(s("cw"), 1)

                    def add(e):
                        dve.wait_ge(s("y_part"), NS * b + (e + 1) * len(HC))
                        dve.wait_ge(s("cw"), 2 * b + 2)
                        if e:
                            dve.wait_ge(s("added"), EXP * b + e + 1)
                        for j in range(TB):
                            last = v.scalar_tensor_tensor(columns(x_sb, b, j * P, P), B[4 + e % 2][:, j * P:(j + 1) * P], cw[:, j, e:e + 1],
                                                          columns(x_sb, b, j * P, P), ALU.mult, ALU.add)
                        last.then_inc(s("added"), 1)

                    for i, (e, n) in enumerate(STEPS):
                        m = HC[n][1]
                        dve.wait_ge(s("h1"), NS * b + i + 1)
                        dve.wait_ge(s("h3_ps"), NS * b + i + 1)
                        if i >= 2:
                            dve.wait_ge(s("y_part"), NS * b + i - 1)
                        v.tensor_tensor(h[0:m, i % 2, :], h1[0:m, i % 2, :], B[2 + i % 2][0:m, :], ALU.mult).then_inc(s("h"), 1)
                        if n == 1 and e:
                            add(e - 1)
                    add(EXP - 1)


def build_program(nc, args, out, phases=9, dump=None):
    with ExitStack() as ctx:
        def sb(name, *shape):
            return ctx.enter_context(nc.sbuf_tensor(name, list(shape), F32))

        s = Signals(nc, "setup")
        x_sb = sb("x_sb", P, NT * P)
        consts = sb("consts", P, CONSTS.shape[1])

        def K(name):
            a, n = CONST_AT[name]
            return consts[:, a:a + n]

        W = {"qkv": sb("w_qkv", P, 3, P), "b": sb("w_b", P, H), "taps": sb("w_taps", P, 3, KQ), "fir": sb("w_fir", P, sum(FIRS)),
             "m1x": sb("w_m1x", P, P), "m1s": sb("w_m1s", P, P), "m2": sb("w_m2", P, H * NBR), "b1": sb("w_b1", P, 1),
             "b2": sb("w_b2", 1, H * NBR), "ones": sb("w_ones", 1, P), "itemp": sb("w_itemp", P, H), "onorm": sb("w_onorm", P, 1),
             "o": sb("w_o", P, P),
                 "mid_route": sb("w_mid_route", P, 16), "mid_route_b": sb("w_mid_route_b", 1, 16), "base": sb("w_base", P, P),
             "base_b": sb("w_base_b", 1, P), "lora_b": sb("w_lora_b", NL * RL, P), "lin_qkv": sb("w_lin_qkv", P, 3, P),
             "lin_b": sb("w_lin_b", 1, 3 * P), "lin_b_eps": sb("w_lin_b_eps", P, 2), "lin_out": sb("w_lin_out", P, P),
             "lin_out_b": sb("w_lin_out_b", 1, P), "gate": sb("w_gate", P, NE),
             "w1": sb("w_1", P, EXP, HID), "w3": sb("w_3", P, EXP, HID), "w2": sb("w_2", P, EXP, len(HC), P)}
        rows = sb("rows", P, 6, P)
        rows8 = sb("rows8", NE, 2, P)
        setup = ExitStack()
        turned = setup.enter_context(nc.psum_tensor("turned", [P, 2, BL], F32))
        t0, t1, t2 = sb("t0", P, H), sb("t1", P, H), sb("t2", P, H)
        loads = []

        def load(dst, src):
            loads.append((dst, src))

        load(x_sb[:, :].rearrange("p (t d) -> p t d", d=D), args["L0_attn_hidden_states"].rearrange("a (t p) d -> p (a t) d", p=P))
        load(consts[:, :], args["consts"])
        for n, name in enumerate(("q", "k", "v")):
            load(W["qkv"][:, n, :], args[f"L0_attn_{name}_w"])
            load(W["taps"][:, n, :], args[f"L0_attn_{name}c_w"].rearrange("d a k -> d (a k)"))
        load(W["b"][:, :], args["L0_attn_b_w"])
        at = 0
        for n in FIRS:
            load(W["fir"][:, at:at + n], args[f"L0_attn_fir_w{n}"].rearrange("d a k -> d (a k)"))
            at += n
        load(W["m1x"][:, :], args["L0_attn_mlp_w1"][0:D, :])
        by_kind = args["L0_attn_mlp_w1"][D:D + H * NBR * 4, :].rearrange("(r k) n -> k r n", k=4)
        for kind, row in ((0, 0), (2, 32), (1, 64), (3, 96)):
            load(W["m1s"][row:row + H * NBR, :], by_kind[kind])
        load(W["m2"][:, :], args["L0_attn_mlp_w2"])
        load(W["b1"][:, :], args["L0_attn_mlp_b1"].rearrange("(n a) -> n a", a=1))
        load(W["b2"][:, :], args["L0_attn_mlp_b2"].rearrange("(a n) -> a n", a=1))
        load(t0[:, :], args["L0_attn_gate_log_temp"].rearrange("(a n) -> a n", a=1).to_broadcast([P, H]))
        for h in range(H):
            load(W["onorm"][h * DK:(h + 1) * DK, :], args["L0_attn_onorm_w"].rearrange("(n a) -> n a", a=1))
        load(W["o"][:, :], args["L0_attn_o_w"])
        load(rows[:, 0, :], args["L0_ffn_base_w"])
        load(rows[:, 1:4, :], args["L1_attn_qkv_w"].rearrange("(n o) i -> o n i", o=P))
        load(rows[:, 4, :], args["L1_attn_out_w"])
        load(rows8[:, 0, :], args["L0_ffn_router_w"])
        load(rows8[:, 1, :], args["L1_ffn_gate_w"])
        load(W["mid_route"][:, 0:RL], args["L0_ffn_lora_A"])
        load(W["mid_route_b"][:, RL:16], args["L0_ffn_router_b"].rearrange("(a n) -> a n", a=1))
        load(W["base_b"][:, :], args["L0_ffn_base_b"].rearrange("(a n) -> a n", a=1))
        load(W["lora_b"][:, :], args["L0_ffn_lora_B"].rearrange("e r d -> (e r) d"))
        load(W["lin_b"][:, :], args["L1_attn_qkv_b"].rearrange("(a n) -> a n", a=1))
        for n in range(2):
            load(W["lin_b_eps"][:, n:n + 1], args["L1_attn_qkv_b"][n * P:(n + 1) * P].rearrange("(p a) -> p a", a=1))
        load(W["lin_out_b"][:, :], args["L1_attn_out_b"].rearrange("(a n) -> a n", a=1))

        whole = HID // P
        late = [(W[n][:, e, :], args[f"L1_ffn_{n}"][e]) for e in range(EXP) for n in ("w1", "w3")]
        late += [(W["w2"][:, e, 0:whole, :], args["L1_ffn_w2"][e, 0:whole * P, :].rearrange("(c k) d -> k c d", k=P)) for e in range(EXP)]
        late += [(W["w2"][0:HID - whole * P, e, whole, :], args["L1_ffn_w2"][e, whole * P:HID, :]) for e in range(EXP)]

        with nc.Block() as block:
            @block.vector
            def _(dve):
                nc.vector.memset(W["ones"][:, :], 1.0).then_inc(s("ones"), 1)
                nc.vector.memset(W["mid_route_b"][:, :], 0.0).then_inc(s("m1s_zero"), 1)
                nc.vector.memset(W["m1s"][:, :], 0.0).then_inc(s("m1s_zero"), 1)
                dve.wait_ge(s("loads"), 16 * len(loads))
                dve.wait_ge(s("log1p"), 3)
                nc.vector.tensor_scalar(t2[:, :], t0[:, :], 0.0, 0.5, ALU.max, ALU.add).then_inc(s("temp"), 1)
                dve.wait_ge(s("temp"), 1)
                nc.vector.tensor_tensor(t2[:, :], t2[:, :], t1[:, :], ALU.add).then_inc(s("temp"), 1)
                dve.wait_ge(s("temp"), 2)
                nc.vector.reciprocal(W["itemp"][:, :], t2[:, :]).then_inc(s("temp"), 1)
                dve.wait_ge(s("temp"), 3)
                nc.vector.tensor_scalar(W["lora_b"][:, :], W["lora_b"][:, :], 2.0, None, ALU.mult).then_inc(s("weights"), 1)
                nc.vector.tensor_scalar(W["lin_b_eps"][:, :], W["lin_b_eps"][:, :], 1e-6, None, ALU.add).then_inc(s("weights"), 1)
                dve.wait_ge(s("turned"), 7)
                nc.vector.tensor_copy(W["base"][:, :], turned[:, 0, 0:P]).then_inc(s("weights"), 1)
                nc.vector.tensor_copy(W["lin_qkv"][:, :, :], turned[:, 0, P:4 * P].rearrange("p (n o) -> p n o", o=P)).then_inc(s("weights"), 1)
                nc.vector.tensor_copy(W["lin_out"][:, :], turned[:, 1, 0:P]).then_inc(s("weights"), 1)
                nc.vector.tensor_copy(W["mid_route"][:, RL:16], turned[:, 1, P:P + NE]).then_inc(s("weights"), 1)
                nc.vector.tensor_copy(W["gate"][:, :], turned[:, 1, 2 * P:2 * P + NE]).then_inc(s("weights"), 1)
                dve.wait_ge(s("weights"), 7)

            @block.tensor
            def _(pe):
                pe.wait_ge(s("loads"), 16 * len(loads))
                for n in range(5):
                    nc.tensor.transpose(turned[:, n // 4, (n % 4) * P:(n % 4 + 1) * P], rows[:, n, :], K("ident")).then_inc(s("turned"), 1)
                for n in range(2):
                    nc.tensor.transpose(turned[:, 1, (n + 1) * P:(n + 1) * P + NE], rows8[:, n, :], K("ident")[0:NE, 0:NE]).then_inc(s("turned"), 1)

            @block.scalar
            def _(act):
                act.wait_ge(s("loads"), 16 * len(loads))
                nc.scalar.activation(t1[:, :], t0[:, :], ACT.Abs).then_inc(s("log1p"), 1)
                act.wait_ge(s("log1p"), 1)
                nc.scalar.activation(t1[:, :], t1[:, :], ACT.Exp, scale=-1.0).then_inc(s("log1p"), 1)
                act.wait_ge(s("log1p"), 2)
                nc.scalar.activation(t1[:, :], t1[:, :], ACT.Ln, bias=1.0).then_inc(s("log1p"), 1)

            @block.sync
            def _(sp):
                sp.wait_ge(s("m1s_zero"), 2)
                for dst, src in loads:
                    sp.dma_start(dst, src).then_inc(s("loads"), 16)
                for dst, src in late:
                    sp.dma_start(dst, src).then_inc(s("expert_weights"), 16)
                sp.wait_ge(s("loads"), 16 * len(loads))

        setup.close()
        if phases != -1:
            phase_delta(nc, x_sb, K, W, args)
        if phases >= 2:
            phase_lora(nc, x_sb, K, W)
        if phases >= 3:
            phase_linear(nc, x_sb, K, W)
        if phases >= 4:
            phase_experts(nc, x_sb, K, W, (s("expert_weights"), 16 * len(late)), out)
        else:
            with nc.Block() as block:
                @block.sync
                def _(sp):
                    sp.wait_ge(s("expert_weights"), 16 * len(late))
                    sp.dma_start(out.rearrange("a (t p) d -> p (a t) d", p=P), x_sb[:, :].rearrange("p (t d) -> p t d", d=D)).then_inc(s("stored"), 16)
                    sp.wait_ge(s("stored"), 16)


def kernel(**inputs):
    import concourse.bacc as bacc
    from concourse.bass_utils import run_bass_kernel_spmd

    nc = bacc.Bacc("TRN2", target_bir_lowering=False, num_devices=1)
    arrays, args = {}, {}
    for name, a in list(inputs.items()) + [("consts", CONSTS)]:
        a = np.ascontiguousarray(a)
        arrays[f"in_{name}_dram"] = a
        args[name] = nc.dram_tensor(f"in_{name}_dram", a.shape, mybir.dt.from_np(a.dtype), kind="ExternalInput").ap()
    out = nc.dram_tensor("out_0_dram", (1, L, D), F32, kind="ExternalOutput").ap()
    build_program(nc, args, out)
    r = run_bass_kernel_spmd(nc, [arrays], core_ids=[0])
    return r.results[0]["out_0_dram"]
```

```python
from contextlib import ExitStack

import numpy as np
import concourse.bass as bass
from concourse import mybir

ACT = mybir.ActivationFunctionType
ALU = mybir.AluOpType
AX = mybir.AxisListType
F32 = mybir.dt.float32

P = 128
L, D = 2048, 128
NT = L // P
TB = 4
BL = TB * P
NB = L // BL
H, DK = 4, 32
C = 32
CB = BL // C
NBR = 6
KQ = 4
FIRS = (1, 3, 7, 31)
PAD = max(FIRS) - 1
EXP, HID = 4, 704
NE = 8
NL, RL = 8, 8
HL, DL = 16, 8
GH = 4
VE = DL + 1
HC = [(c, min(P, HID - c)) for c in range(0, HID, P)]
UNITS = [(e, n) for e in range(EXP) for n in range(len(HC))]
NU = len(UNITS)
TAPS = [(n, k) for n in range(1, len(FIRS)) for k in range(FIRS[n])]


def const_columns():
    p = np.arange(P)
    i, j = p[:, None], p[None, :]
    same = (i // C) == (j // C)
    cols = {}
    cols["ident"] = np.eye(P)
    cols["same32"] = same * 1.0
    cols["lower"] = (same & (i > j)) * 1.0
    cols["upper"] = (same & (i <= j)) * 1.0
    cols["causal"] = (i <= j) * 1.0
    jj = np.arange(C)[None, :]
    ii = (p % C)[:, None]
    for m in (1, 2, 4, 8, 16):
        at = (ii // (2 * m) == jj // (2 * m)) & ((ii // m) % 2 == 0) & ((jj // m) % 2 == 1)
        cols[f"level{m}"] = at * -1.0
    cols["eye32"] = (ii == jj) * 1.0
    head = p // DK
    w = P + NBR - 1
    for name, rows in (("meanX", {0: 1 / DK}), ("meanA", {32: 1 / DK}), ("sumQ", {64: 1 / (DK - 1), 96: 1.0})):
        a = np.zeros((P, w))
        for off, val in rows.items():
            a[p, NBR - 1 + off + head * NBR] = val
        cols[name] = a
    a = np.zeros((P, P))
    r = np.arange(H * NBR)
    a[r, 64 + r] = -DK / (DK - 1)
    cols["less_mean2"] = a
    for b in range(NBR):
        a = np.zeros((P, P))
        for h in range(H):
            a[h * NBR + b, h * DK:(h + 1) * DK] = 1.0
        cols[f"spread{b}"] = a
    cols["head_mean"] = same / DK
    cols["head_own"] = np.kron((np.arange(P)[:, None] // 8 == np.arange(16)[None, :]) * 1.0, np.ones((1, 9)))
    cols["head_of4"] = ((p[:, None] % 32) // 8 == np.arange(4)[None, :]) * 1.0
    cols["earlier"] = np.tile((np.arange(EXP)[None, :] < np.arange(EXP)[:, None]).reshape(1, -1) * 1.0, (P, 1))
    for n, v in (("eps5", 1e-5), ("eps6", 1e-6)):
        cols[n] = np.full((P, 1), v)
    at, where = 0, {}
    for n, a in cols.items():
        where[n] = (at, a.shape[1])
        at += a.shape[1]
    return np.concatenate(list(cols.values()), 1).astype(np.float32), where


CONSTS, CONST_AT = const_columns()


class Signals:

    def __init__(self, nc, phase):
        self.nc, self.phase, self.of = nc, phase, {}

    def __call__(self, name):
        if name not in self.of:
            self.of[name] = self.nc.alloc_semaphore(name=f"{self.phase}_{name}")
        return self.of[name]

    def clear_but(self, *kept):
        self.nc.clear_and_free_semaphores([x for n, x in self.of.items() if n not in kept])
        self.nc.all_engine_barrier()


def columns(t, b, n, width=BL):
    return t[:, bass.ds(b * BL + n, width)]


def layernorm_moments(nc, dve, s, i, b, x_sb, a, added=None):
    v = nc.vector
    if added:
        dve.wait_ge(*added)
    v.memset(a.ve[:, :], 0.0).then_inc(s("ve_clear"), 1)
    for j in range(TB):
        v.bn_stats(a.stats[:, j, :], columns(x_sb, b, j * P, P)).then_inc(s("ln_stats"), 1)
    dve.wait_ge(s("ln_stats"), TB * i + TB)
    v.memset(a.rstd[:, :], 0.0).then_inc(s("rstd_clear"), 1)
    for j in range(TB):
        v.bn_aggr(a.mv[:, j, :], a.stats[:, j, :]).then_inc(s("mv"), 1)
    dve.wait_ge(s("mv"), TB * i + TB)
    dve.wait_ge(s("ve_clear"), i + 1)
    v.tensor_scalar(a.ve[:, :], a.mv[:, :, 1], 1e-5, None, ALU.add).then_inc(s("ve"), 1)


def layernorm_apply(nc, dve, s, i, b, x_sb, a):
    v = nc.vector
    dve.wait_ge(s("std"), i + 1)
    dve.wait_ge(s("rstd_clear"), i + 1)
    v.reciprocal(a.rstd[:, :], a.std[:, :]).then_inc(s("rstd"), 1)
    dve.wait_ge(s("rstd"), i + 1)
    for j in range(TB):
        v.tensor_scalar(a.xn[:, j * P:(j + 1) * P], columns(x_sb, b, j * P, P), a.mv[:, j, 0:1], a.rstd[:, j:j + 1],
                        ALU.subtract, ALU.mult).then_inc(s("xn"), 1)


def layernorm_turn(nc, pe, s, i, xn, bank, ident):
    pe.wait_ge(s("xn"), TB * i + TB)
    for j in range(TB):
        last = nc.tensor.transpose(bank[:, j * P:(j + 1) * P], xn[:, j * P:(j + 1) * P], ident)
    last.then_inc(s("xnT_ps"), 1)


class Arrays:

    def __init__(self, nc, ctx, prefix):
        self.nc, self.ctx, self.prefix = nc, ctx, prefix

    def new(self, name, *shape, dt=F32):
        return self.ctx.enter_context(self.nc.sbuf_tensor(f"{self.prefix}_{name}", list(shape), dt))


def layernorm_arrays(a):
    a.stats = a.new("stats", P, TB, 6)
    a.mv = a.new("mv", P, TB, 2)
    a.ve = a.new("ve", P, TB)
    a.std = a.new("std", P, TB)
    a.rstd = a.new("rstd", P, TB)
    a.xn = a.new("xn", P, BL)
    a.xnT = a.new("xnT", P, BL)


def delta_arrays(a):
    layernorm_arrays(a)
    a.pre = a.new("pre", P, 3, KQ - 1 + BL)
    a.conv = a.new("conv", P, 3, BL)
    a.beta = a.new("beta", P, TB, H)
    a.qT = a.new("qT", P, BL)
    a.kT = a.new("kT", P, BL)
    a.vT = a.new("vT", P, PAD + BL)
    a.sq = a.new("sq", P, 2, BL)
    a.nrm = a.new("nrm", P, TB, 8)
    a.root = a.new("root", P, TB, 8)
    a.rn = a.new("rn", P, TB, 8)
    a.gam = a.new("gam", P, TB, H)
    a.rkb = a.new("rkb", P, TB, H)
    a.k_tok = a.new("k_tok", P, BL)
    a.vk = a.new("vk", P, TB, H, 2, DK)
    a.A = a.new("A", P, TB * H, P)
    a.at = a.new("at", P, TB * H, P)
    a.E = a.new("E", P, TB * H, C)
    a.Pm = a.new("Pm", P, TB * H, C)
    a.Tc = a.new("Tc", P, TB * H, C)
    a.X = a.new("X", P, TB * H, P)
    a.u0 = a.new("u0", P, TB, H, DK)
    a.w_tok = a.new("w_tok", P, TB, H, DK)
    a.wT = a.new("wT", P, BL)
    a.u = a.new("u", P, TB, H, DK)
    a.state = a.new("state", P, P)
    a.own = a.new("own", P, P)
    a.br = a.new("br", P, 5, BL)
    a.absb = a.new("absb", P, 2, BL)
    a.hid = a.new("hid", P, BL)
    a.lg = a.new("lg", P, TB, H, NBR)
    a.mx = a.new("mx", P, TB, H)
    a.ex = a.new("ex", P, TB, H, NBR)
    a.sm = a.new("sm", P, TB, H)
    a.rs = a.new("rs", P, TB, H)
    a.wt = a.new("wt", P, TB, H, NBR)
    a.sqb = a.sq
    a.part = a.absb
    a.o_tok = a.w_tok[:, :, :, :].rearrange("p j h c -> p (j h c)")
    a.st2 = a.hid
    a.var = a.Tc[:, :, :].rearrange("p n c -> p (n c)")
    a.st = a.Pm[:, :, :].rearrange("p n c -> p (n c)")
    a.fu = a.E[:, :, :].rearrange("p n c -> p (n c)")
    a.wtT = a.u0[0:H * NBR, :, :, :].rearrange("p j h c -> p (j h c)")


STATS_AT = {5: 2, 0: 4, 1: 6, 2: 10, 3: 25}
STATS_ORDER = [5, 0, 1, 2, 3, 4]
TAPS_PER_HALF = 2

DELTA_STEPS = ([2.5, 2, 2, 4, 3, 3, 3, 3, 3] + [2.5] * (H + 1) + [2] + [3] * 8 + [3, 2] + [1.6] * (2 * CB)
               + [3, 3, 2, 2, 4, 3, 4, 3] + [1.5] * NBR + [2, 2, 2])


def head_bank(h):
    return (h + 3) % 4


def delta_pe(nc, pe, s, b, a, B, K, W):
    def mm(out, lhsT, rhs, start=True, stop=True, **kw):
        return nc.tensor.matmul(out, lhsT, rhs, start=start, stop=stop, **kw)

    def by_head(h, t):
        r = slice(h * DK, (h + 1) * DK)
        for j in range(TB):
            c = slice(j * P, (j + 1) * P)
            last = mm(B[head_bank(h)][:, c], a.kT[r, c], t[r, c], tile_position=(r.start, 0))
        return last

    ident = K("ident")
    yield
    yield
    pe.wait_ge(s("out_added"), b + 1)
    layernorm_turn(nc, pe, s, b, a.xn, B[0], ident)
    yield
    pe.wait_ge(s("xnT"), b + 1)
    pe.wait_ge(s("fu"), (NBR - 1) * b + 1)
    for n in range(3):
        mm(B[1 + n][:, :], W["qkv"][:, n, :], a.xnT[:, :]).then_inc(s("proj"), 1)
    for j in range(TB):
        last = mm(B[0][:, j * 8:j * 8 + H], a.xnT[:, j * P:(j + 1) * P], W["b"][:, :])
    last.then_inc(s("beta_ps"), 1)
    yield
    yield
    yield
    yield
    pe.wait_ge(s("qk_sq"), 2 * b + 2)
    pe.wait_ge(s("beta_tanh"), b + 1)
    for j in range(TB):
        for n in range(2):
            last = mm(B[0][:, 64 + j * 8 + n * H:64 + j * 8 + (n + 1) * H],
                      a.sq[:, n, j * P:(j + 1) * P], K("same32").rearrange("p (h c) -> p h c", c=DK)[:, :, 0])
    last.then_inc(s("norms_ps"), 1)
    pe.wait_ge(s("kT"), b + 1)
    for j in range(TB):
        last = nc.tensor.transpose(B[1][:, j * P:(j + 1) * P], a.kT[:, j * P:(j + 1) * P], ident)
    last.then_inc(s("k_tok_ps"), 1)
    pe.wait_ge(s("vT"), b + 1)
    for j in range(TB):
        last = nc.tensor.transpose(B[2][:, j * P:(j + 1) * P], a.vT[:, PAD + j * P:PAD + (j + 1) * P], ident)
    last.then_inc(s("v_tok_ps"), 1)
    yield
    yield
    for h in range(H + 1):
        if h < H:
            if h == 1:
                pe.wait_ge(s("nrm"), b + 1)
            if h >= 2:
                pe.wait_ge(s("vk"), 2 * b + h - 1)
            by_head(h, a.kT).then_inc(s("gram"), 1)
        if h:
            pe.wait_ge(s("A"), H * b + h)
            by_head(h - 1, a.qT).then_inc(s("attn_ps"), 1)
        yield
    yield
    for r in range(4):
        pe.wait_ge(s("E"), 5 * b + r + 1)
        if r == 0:
            pe.wait_ge(s("attn"), b * H + H)
        for n in range(TB * H):
            last = mm(B[3][:, n * C:(n + 1) * C], a.A[:, n, :], a.E[:, n, :])
        last.then_inc(s("UE"), 1)
        yield
        pe.wait_ge(s("Pm"), 4 * b + r + 1)
        pe.wait_ge(s("X"), 20 * b + 4 * r + 4)
        for n in range(TB * H):
            last = mm(B[1][:, n * C:(n + 1) * C], a.X[:, n, :], a.Pm[:, n, :])
        last.then_inc(s("EUE"), 1)
        yield
    pe.wait_ge(s("X"), 20 * b + 20)
    pe.wait_ge(s("vk"), 2 * b + 2)
    for n in range(TB * H):
        last = mm(B[2 + n // 8][:, (n % 8) * 64:(n % 8) * 64 + 64], a.X[:, n, :],
                  a.vk[:, n // H, n % H].rearrange("p a c -> p (a c)"))
    last.then_inc(s("uw_ps"), 1)
    yield
    pe.wait_ge(s("w_tok"), b + 1)
    for j in range(TB):
        last = nc.tensor.transpose(B[1][:, j * P:(j + 1) * P], a.w_tok[:, j].rearrange("p h c -> p (h c)"), ident)
    last.then_inc(s("wT_ps"), 1)
    yield

    def branch_sums(n):
        x = a.br[:, n, :] if n < 5 else a.vT[:, PAD:]
        i = STATS_ORDER.index(n)
        pe.wait_ge(s("square"), NBR * b + i + 1)
        if n < 5:
            pe.wait_ge(s(f"branch{n}"), b + 1)
        mm(B[2][:, :], K("meanX")[:, NBR - 1 - n:NBR - 1 - n + P], x, start=(i == 0), stop=False)
        mm(B[2][:, :], K("meanA")[:, NBR - 1 - n:NBR - 1 - n + P], a.absb[:, i % 2, :], start=False, stop=False)
        mm(B[2][:, :], K("sumQ")[:, NBR - 1 - n:NBR - 1 - n + P], a.sqb[:, i % 2, :], start=False, stop=(i == NBR - 1)).then_inc(s("sums"), 1)

    pe.wait_ge(s("wT"), b + 1)
    pe.wait_ge(s("u0"), b + 1)
    for half in range(2 * CB):
        c = half // 2
        j, q = c // 4, slice((c % 4) * C, (c % 4 + 1) * C)
        t = slice(c * C, (c + 1) * C)
        cs = slice(j * P, (j + 1) * P)
        if half % 2 == 0:
            pe.wait_ge(s("state"), b * CB + c + 1)
            mm(B[1][q, 0:P], a.wT[:, t], a.state[:, :], tile_position=(0, q.start)).then_inc(s("wS"), 1)
            mm(B[0][q, cs], a.qT[:, t], a.state[:, :], tile_position=(0, q.start), stop=False, skip_group_check=True).then_inc(s("qS"), 1)
        else:
            pe.wait_ge(s("u"), b * CB + c + 1)
            mm(B[3][:, 0:P], a.k_tok[q, cs], a.u[q, j].rearrange("p h c -> p (h c)"),
               tile_position=(q.start, 0)).then_inc(s("kU"), 1)
            if c % 4 == 3:
                for h in range(H):
                    last = mm(B[0][:, j * P + h * DK:j * P + (h + 1) * DK], a.at[:, j * H + h, :], a.u[:, j, h, :],
                              start=False, stop=True, skip_group_check=True)
                last.then_inc(s("o_ps"), 1)
        for n, when in STATS_AT.items():
            if half == when + 1:
                branch_sums(n)
        yield
    yield
    pe.wait_ge(s("o_tok"), b + 1)
    for j in range(TB):
        last = nc.tensor.transpose(B[1][:, j * P:(j + 1) * P], a.o_tok[:, j * P:(j + 1) * P], ident)
    last.then_inc(s("oT_ps"), 1)
    yield
    branch_sums(4)
    yield
    pe.wait_ge(s("st2"), b + 1)
    mm(B[3][:, :], K("less_mean2"), a.st2[:, :]).then_inc(s("mean2"), 1)
    mm(B[1][:, :], W["m1x"][:, :], a.xnT[:, :], stop=False)
    yield
    pe.wait_ge(s("st"), 2 * b + 2)
    mm(B[1][:, :], W["m1s"][:, :], a.st[:, :], start=False).then_inc(s("hid_ps"), 1)
    yield
    pe.wait_ge(s("hid"), b + 1)
    for j in range(TB):
        mm(B[0][:, j * 24:(j + 1) * 24], a.hid[:, j * P:(j + 1) * P], W["m2"][:, :], stop=False)
        last = mm(B[0][:, j * 24:(j + 1) * 24], W["ones"][0:1, :], W["b2"][0:1, :], start=False)
    last.then_inc(s("logits"), 1)
    yield
    yield
    pe.wait_ge(s("wt"), b + 1)
    for j in range(TB):
        last = nc.tensor.transpose(B[3][0:H * NBR, j * P:(j + 1) * P], a.wt[:, j].rearrange("p h b -> p (h b)"), ident)
    last.then_inc(s("wtT_ps"), 1)
    yield
    pe.wait_ge(s("wtT"), b + 1)
    for n in range(NBR):
        if n >= 2:
            pe.wait_ge(s("mixed"), NBR * b + n - 1)
        mm(B[2 + n % 2][:, :], K(f"spread{n}")[0:H * NBR, :], a.wtT[:, :]).then_inc(s("spread"), 1)
        yield
    pe.wait_ge(s("fsq"), b + 1)
    mm(B[1][:, :], K("head_mean"), a.sq[:, 0, :]).then_inc(s("ms"), 1)
    yield
    yield
    pe.wait_ge(s("fn"), b + 1)
    for j in range(TB):
        last = mm(B[0][:, j * P:(j + 1) * P], a.conv[:, 0, j * P:(j + 1) * P], W["o"][:, :])
    last.then_inc(s("out_ps"), 1)
    yield


def delta_act(nc, act, s, b, a, B, K, W):
    f = nc.scalar.activation
    act.wait_ge(s("ve"), b + 1)
    f(a.std[:, :], a.ve[:, :], ACT.Sqrt).then_inc(s("std"), 1)
    yield
    yield
    act.wait_ge(s("xnT_ps"), b + 1)
    f(a.xnT[:, :], B[0][:, :], ACT.Copy).then_inc(s("xnT"), 1)
    yield
    act.wait_ge(s("halo"), b + 1)
    for n in range(3):
        act.wait_ge(s("proj"), 3 * b + n + 1)
        f(a.pre[:, n, KQ - 1:], B[1 + n][:, :], ACT.Copy).then_inc(s("pre_in"), 1)
    yield
    act.wait_ge(s("beta_ps"), b + 1)
    f(a.beta[:, :, :], B[0][:, 0:TB * 8].rearrange("p (j h) -> p j h", h=8)[:, :, 0:H], ACT.Tanh, scale=0.5).then_inc(s("beta_tanh"), 1)
    for n, (plain, name) in enumerate(((a.qT, "q"), (a.kT, "k"))):
        act.wait_ge(s("conv"), 3 * b + n + 1)
        f(plain[:, :], a.conv[:, n, :], ACT.Silu).then_inc(s(name + "T"), 1)
        act.wait_ge(s(name + "T"), b + 1)
        f(a.sq[:, n, :], plain[:, :], ACT.Square).then_inc(s("qk_sq"), 1)
        yield
    act.wait_ge(s("conv"), 3 * b + 3)
    f(a.vT[:, PAD:], a.conv[:, 2, :], ACT.Silu).then_inc(s("vT"), 1)
    yield
    act.wait_ge(s("nrm"), b + 1)
    f(a.root[:, :, :], a.nrm[:, :, :], ACT.Sqrt).then_inc(s("root"), 1)
    act.wait_ge(s("k_tok_ps"), b + 1)
    f(a.k_tok[:, :], B[1][:, :], ACT.Copy).then_inc(s("k_tok"), 1)
    yield
    act.wait_ge(s("vT"), b + 1)
    f(a.br[:, 0, :], a.vT[:, PAD:], ACT.Copy, scale=W["fir"][:, 0:1]).then_inc(s("branch0"), 1)
    yield
    for h in range(H + 1):
        yield
    yield
    for r in range(5):
        src = a.Tc if r < 4 else a.E
        if r < 4:
            act.wait_ge(s("Tc"), 4 * b + r + 1)
        else:
            act.wait_ge(s("E"), 5 * b + 5)
        for g in range(4):
            q = slice(g * C, (g + 1) * C)
            f(a.X[q, :, q], src[q, :, :], ACT.Copy).then_inc(s("X"), 1)
        if r < 4:
            yield
            yield
    act.wait_ge(s("uw_ps"), b + 1)
    for part, t, name in ((1, a.w_tok, "w_tok"), (0, a.u0, "u0")):
        for n in range(2):
            uw = B[2 + n][:, :].rearrange("p (g a c) -> p g a c", g=2 * H, a=2)
            last = f(t[:, 2 * n:2 * n + 2].rearrange("p j h c -> p (j h) c"), uw[:, :, part, :], ACT.Copy)
        last.then_inc(s(name), 1)
    yield
    act.wait_ge(s("wT_ps"), b + 1)
    f(a.wT[:, :], B[1][:, :], ACT.Copy).then_inc(s("wT"), 1)
    yield

    def branch_magnitudes(n):
        i = STATS_ORDER.index(n)
        x = a.br[:, n, :] if n < 5 else a.vT[:, PAD:]
        if n < 5:
            act.wait_ge(s(f"branch{n}"), b + 1)
        if i >= 2:
            act.wait_ge(s("sums"), NBR * b + i - 1)
        f(a.absb[:, i % 2, :], x, ACT.Abs)
        f(a.sqb[:, i % 2, :], x, ACT.Square).then_inc(s("square"), 1)

    for half in range(2 * CB):
        for n, when in STATS_AT.items():
            if half == when:
                branch_magnitudes(n)
        yield
    yield
    act.wait_ge(s("oT_ps"), b + 1)
    f(a.br[:, 4, :], B[1][:, :], ACT.Copy).then_inc(s("branch4"), 1)
    yield
    branch_magnitudes(4)
    yield
    act.wait_ge(s("sums"), NBR * b + NBR)
    f(a.st2[:, :], B[2][:, :], ACT.Square).then_inc(s("st2"), 1)
    f(a.st[0:64, :], B[2][0:64, :], ACT.Copy).then_inc(s("st"), 1)
    yield
    act.wait_ge(s("var"), 2 * b + 2)
    f(a.st[64:P, :], a.var[64:P, :], ACT.Sqrt).then_inc(s("st"), 1)
    yield
    act.wait_ge(s("hid_ps"), b + 1)
    f(a.hid[:, :], B[1][:, :], ACT.Gelu, bias=W["b1"][:, 0:1]).then_inc(s("hid"), 1)
    yield
    act.wait_ge(s("lg"), 3 * b + 3)
    f(a.ex[:, :, :, :], a.lg[:, :, :, :], ACT.Exp).then_inc(s("ex"), 1)
    yield
    act.wait_ge(s("wtT_ps"), b + 1)
    f(a.wtT[:, :], B[3][0:H * NBR, :], ACT.Copy).then_inc(s("wtT"), 1)
    yield
    for n in range(NBR):
        yield
    act.wait_ge(s("fu"), (NBR - 1) * b + NBR)
    f(a.sq[:, 0, :], a.fu[:, :], ACT.Square).then_inc(s("fsq"), 1)
    yield
    act.wait_ge(s("ms"), b + 1)
    f(a.sq[:, 1, :], B[1][:, :], ACT.Ln, bias=K("eps5")).then_inc(s("lnv"), 1)
    act.wait_ge(s("lnv"), b + 1)
    f(a.conv[:, 1, :], a.sq[:, 1, :], ACT.Exp, scale=-0.5).then_inc(s("rr"), 1)
    yield
    yield


def delta_dve(nc, dve, s, b, a, B, K, W, x_sb):
    v = nc.vector
    layernorm_moments(nc, dve, s, b, b, x_sb, a)
    yield
    layernorm_apply(nc, dve, s, b, b, x_sb, a)
    yield
    yield
    yield
    for n in range(3):
        dve.wait_ge(s("pre_in"), 3 * b + n + 1)
        v.tensor_scalar(a.conv[:, n, :], a.pre[:, n, 0:BL], W["taps"][:, n, 0:1], None, ALU.mult).then_inc(s("tap"), 1)
        for k in range(1, KQ):
            dve.wait_ge(s("tap"), 9 * b + 3 * n + k)
            ins = v.scalar_tensor_tensor(a.conv[:, n, :], a.pre[:, n, k:k + BL], W["taps"][:, n, k:k + 1], a.conv[:, n, :],
                                         ALU.mult, ALU.add)
            ins.then_inc(s("conv" if k == KQ - 1 else "tap"), 1)
        if n == 2:
            dve.wait_ge(s("conv"), 3 * b + 3)
            v.tensor_copy(a.pre[:, :, 0:KQ - 1], a.pre[:, :, BL:BL + KQ - 1]).then_inc(s("halo"), 1)
            dve.wait_ge(s("beta_tanh"), b + 1)
            v.tensor_scalar(a.beta[:, :, :], a.beta[:, :, :], 0.5, 0.5, ALU.mult, ALU.add).then_inc(s("beta"), 1)
        yield
    dve.wait_ge(s("norms_ps"), b + 1)
    v.tensor_scalar(a.nrm[:, :, :], B[0][:, 64:64 + TB * 8].rearrange("p (j h) -> p j h", h=8), 1e-6, None, ALU.add).then_inc(s("nrm"), 1)
    yield
    dve.wait_ge(s("root"), b + 1)
    v.reciprocal(a.rn[:, :, :], a.root[:, :, :]).then_inc(s("rn"), 1)
    dve.wait_ge(s("rn"), b + 1)
    dve.wait_ge(s("beta"), b + 1)
    v.tensor_tensor(a.rkb[:, :, :], a.beta[:, :, :], a.rn[:, :, H:2 * H], ALU.mult).then_inc(s("rkb"), 1)
    dve.wait_ge(s("rkb"), b + 1)
    v.tensor_tensor(a.gam[:, :, :], a.rkb[:, :, :], a.rn[:, :, H:2 * H], ALU.mult).then_inc(s("gam"), 1)
    dve.wait_ge(s("gam"), b + 1)

    def heads(t):
        return t.rearrange("p (g c) -> p g c", c=DK)

    def per_head(t):
        return t.rearrange("p j h -> p (j h)").unsqueeze(2).to_broadcast([P, TB * H, DK])

    def all_heads(m):
        return m.unsqueeze(1).to_broadcast([P, TB * H, C])

    vk = a.vk[:, :, :, :, :].rearrange("p j h a c -> p (j h) a c")
    dve.wait_ge(s("k_tok"), b + 1)
    v.tensor_tensor(vk[:, :, 1, :], heads(B[1][:, :]), per_head(a.gam[:, :, :]), ALU.mult).then_inc(s("vk"), 1)
    dve.wait_ge(s("v_tok_ps"), b + 1)
    v.tensor_tensor(vk[:, :, 0, :], heads(B[2][:, :]), per_head(a.rkb[:, :, :]), ALU.mult).then_inc(s("vk"), 1)
    yield
    def of_head(t, h):
        return t[:, :, :].rearrange("p (j h) c -> p j h c", h=H)[:, :, h, :]

    for h in range(H + 1):
        if h < H:
            dve.wait_ge(s("gram"), H * b + h + 1)
            for j in range(TB):
                last = v.scalar_tensor_tensor(a.A[:, j * H + h, :], B[head_bank(h)][:, j * P:(j + 1) * P], a.gam[:, j, h:h + 1],
                                              K("lower"), ALU.mult, ALU.mult)
            last.then_inc(s("A"), 1)
        if h:
            dve.wait_ge(s("attn_ps"), H * b + h)
            v.tensor_tensor(of_head(a.at, h - 1), B[head_bank(h - 1)][:, :].rearrange("p (j c) -> p j c", c=P),
                            K("upper").unsqueeze(1).to_broadcast([P, TB, P]), ALU.mult).then_inc(s("attn"), 1)
        yield
    dve.wait_ge(s("A"), H * b + H)
    for g in range(4):
        q = slice(g * C, (g + 1) * C)
        last = v.transpose(a.Tc[q, :, :], a.A[q, :, q])
    last.then_inc(s("AT"), 1)
    dve.wait_ge(s("AT"), b + 1)
    v.tensor_tensor(a.Pm[:, :, :], a.Tc[:, :, :], all_heads(K("level1")), ALU.mult).then_inc(s("E0"), 1)
    dve.wait_ge(s("E0"), b + 1)
    v.tensor_tensor(a.E[:, :, :], a.Pm[:, :, :], all_heads(K("eye32")), ALU.add).then_inc(s("E"), 1)
    yield
    for r in range(4):
        dve.wait_ge(s("E"), 5 * b + r + 1)
        v.transpose(a.Tc[:, :, :].rearrange("p n c -> p (n c)"), a.E[:, :, :].rearrange("p n c -> p (n c)")).then_inc(s("Tc"), 1)
        dve.wait_ge(s("UE"), 4 * b + r + 1)
        v.tensor_tensor(a.Pm[:, :, :], B[3][:, :].rearrange("p (n c) -> p n c", c=C), all_heads(K(f"level{2 << r}")), ALU.mult).then_inc(s("Pm"), 1)
        yield
        dve.wait_ge(s("EUE"), 4 * b + r + 1)
        dve.wait_ge(s("Tc"), 4 * b + r + 1)
        v.tensor_tensor(a.E[:, :, :], a.E[:, :, :], B[1][:, :].rearrange("p (n c) -> p n c", c=C), ALU.add).then_inc(s("E"), 1)
        yield
    yield
    yield
    first_tap = [sum(FIRS[:n]) for n in range(len(FIRS))]
    chained = len(TAPS) - len(FIRS[1:])

    def fir_tap(i):
        n, k = TAPS[i]
        at = PAD - FIRS[n] + 1 + k
        w = W["fir"][:, first_tap[n] + k:first_tap[n] + k + 1]
        if k == 0:
            ins = v.tensor_scalar(a.br[:, n, :], a.vT[:, at:at + BL], w, None, ALU.mult)
        else:
            dve.wait_ge(s("fir_tap"), chained * b + i - n + 1)
            ins = v.scalar_tensor_tensor(a.br[:, n, :], a.vT[:, at:at + BL], w, a.br[:, n, :], ALU.mult, ALU.add)
        ins.then_inc(s(f"branch{n}" if k == FIRS[n] - 1 else "fir_tap"), 1)

    tap = 0
    for half in range(2 * CB):
        c = half // 2
        j, q = c // 4, slice((c % 4) * C, (c % 4 + 1) * C)
        if half % 2 == 0:
            dve.wait_ge(s("wS"), CB * b + c + 1)
            if c == 0:
                dve.wait_ge(s("u0"), b + 1)
            v.tensor_tensor(a.u[q, j], a.u0[q, j], B[1][q, 0:P].rearrange("p (h c) -> p h c", c=DK), ALU.subtract).then_inc(s("u"), 1)
        else:
            dve.wait_ge(s("kU"), CB * b + c + 1)
            v.tensor_tensor(a.own[:, :], B[3][:, 0:P], K("same32"), ALU.mult).then_inc(s("kU_own"), 1)
            dve.wait_ge(s("kU_own"), CB * b + c + 1)
            dve.wait_ge(s("qS"), CB * b + c + 1)
            v.tensor_tensor(a.state[:, :], a.state[:, :], a.own[:, :], ALU.add).then_inc(s("state"), 1)
        for _ in range(TAPS_PER_HALF):
            if tap < len(TAPS):
                fir_tap(tap)
                tap += 1
        yield
    dve.wait_ge(s("o_ps"), TB * b + TB)
    v.tensor_tensor(a.o_tok[:, :].rearrange("p (g c) -> p g c", c=DK), heads(B[0][:, :]),
                    a.rn[:, :, 0:H].unsqueeze(3).to_broadcast([P, TB, H, DK]), ALU.mult).then_inc(s("o_tok"), 1)
    yield
    yield
    yield
    dve.wait_ge(s("st2"), b + 1)
    v.tensor_copy(a.var[64:P, :], B[2][64:P, :]).then_inc(s("var0"), 1)
    dve.wait_ge(s("mean2"), b + 1)
    dve.wait_ge(s("var0"), b + 1)
    v.tensor_tensor(a.var[64:P, :], a.var[64:P, :], B[3][64:P, :], ALU.add).then_inc(s("var"), 1)
    dve.wait_ge(s("var"), 2 * b + 1)
    v.tensor_scalar(a.var[64:P, :], a.var[64:P, :], 0.0, None, ALU.max).then_inc(s("var"), 1)
    yield
    yield
    dve.wait_ge(s("logits"), b + 1)
    v.tensor_tensor(a.lg[:, :, :, :], B[0][:, 0:TB * 24].rearrange("p (j h n) -> p j h n", j=TB, h=H),
                    W["itemp"][:, :].unsqueeze(1).unsqueeze(3).to_broadcast([P, TB, H, NBR]), ALU.mult).then_inc(s("lg"), 1)
    dve.wait_ge(s("lg"), 3 * b + 1)
    v.tensor_reduce(a.mx[:, :, :], a.lg[:, :, :, :], AX.X, ALU.max).then_inc(s("lg"), 1)
    dve.wait_ge(s("lg"), 3 * b + 2)
    v.tensor_tensor(a.lg[:, :, :, :], a.lg[:, :, :, :], a.mx[:, :, :].unsqueeze(3).to_broadcast([P, TB, H, NBR]), ALU.subtract).then_inc(s("lg"), 1)
    yield
    dve.wait_ge(s("ex"), b + 1)
    v.tensor_reduce(a.sm[:, :, :], a.ex[:, :, :, :], AX.X, ALU.add).then_inc(s("sm"), 1)
    dve.wait_ge(s("sm"), b + 1)
    v.reciprocal(a.rs[:, :, :], a.sm[:, :, :]).then_inc(s("rs"), 1)
    dve.wait_ge(s("rs"), b + 1)
    v.tensor_tensor(a.wt[:, :, :, :], a.ex[:, :, :, :], a.rs[:, :, :].unsqueeze(3).to_broadcast([P, TB, H, NBR]), ALU.mult).then_inc(s("wt"), 1)
    yield
    yield
    for n in range(NBR):
        x = a.br[:, n, :] if n < 5 else a.vT[:, PAD:]
        dve.wait_ge(s("spread"), NBR * b + n + 1)
        if n > 2:
            dve.wait_ge(s("fu"), (NBR - 1) * b + n - 1)
        v.tensor_tensor(a.fu[:, :] if n == 0 else a.part[:, n % 2, :], x, B[2 + n % 2][:, :], ALU.mult).then_inc(s("mixed"), 1)
        if n:
            dve.wait_ge(s("mixed"), NBR * b + n + 1)
            dve.wait_ge(s("fu"), (NBR - 1) * b + n)
            v.tensor_tensor(a.fu[:, :], a.fu[:, :], a.part[:, n % 2, :], ALU.add).then_inc(s("fu"), 1)
        if n == NBR - 1:
            v.tensor_copy(a.vT[:, 0:PAD], a.vT[:, BL:BL + PAD]).then_inc(s("v_halo"), 1)
        yield
    yield
    yield
    dve.wait_ge(s("rr"), b + 1)
    v.scalar_tensor_tensor(a.conv[:, 0, :], a.fu[:, :], W["onorm"][:, 0:1], a.conv[:, 1, :], ALU.mult, ALU.mult).then_inc(s("fn"), 1)
    dve.wait_ge(s("out_ps"), b + 1)
    v.tensor_tensor(columns(x_sb, b, 0), columns(x_sb, b, 0), B[0][:, :], ALU.add).then_inc(s("out_added"), 1)
    yield


def rest_arrays(a):
    layernorm_arrays(a)
    a.mid = a.new("mid", P, TB, RL)
    a.lg = a.new("lg", P, TB, NL)
    a.mx = a.new("mx", P, TB)
    a.ex = a.new("ex", P, TB, NL)
    a.sm = a.new("sm", P, TB)
    a.rs = a.new("rs", P, TB)
    a.gate = a.new("gate", P, TB, NL, dt=mybir.dt.bfloat16)
    a.outer = a.new("outer", P, TB, P)
    a.outerT = a.new("outerT", NL * RL, BL)
    a.qT = a.new("qT", P, BL)
    a.kT = a.new("kT", P, BL)
    a.qX = a.new("qX", P, GH, BL)
    a.k_tok = a.new("k_tok", P, BL)
    a.v1 = a.new("v1", P, TB, HL, VE)
    a.sc = a.new("sc", P, 4, GH, P)
    a.own = a.new("own", P, HL * VE)
    a.state = a.new("state", P, HL * VE)
    a.den = a.new("den", P, 2, HL)
    a.rden = a.new("rden", P, 2, HL)
    a.a_tok = a.new("a_tok", P, BL)
    a.aT = a.new("aT", P, BL)
    a.p = a.new("p", P, TB, EXP)
    a.over = a.new("over", P, TB, EXP, EXP)
    a.ties = a.new("ties", P, TB, EXP, EXP)
    a.rank = a.new("rank", P, TB, EXP)
    a.cw = a.new("cw", P, TB, EXP)
    a.h1 = a.new("h1", P, 2, BL)
    a.h = a.new("h", P, 2, BL)


LN_STEPS = [2.5, 2, 2]
REST_STEPS = (LN_STEPS + [3, 3, 2, 2] + LN_STEPS + [5] + [1.7] * (4 * TB) + [2, 2, 2, 2]
              + LN_STEPS + [3, 3] + [2.6] * (NU + 1) + [1])


def rest_pe(nc, pe, s, b, a, B, K, W):
    mm = nc.tensor.matmul
    ident = K("ident")
    yield
    yield
    layernorm_turn(nc, pe, s, 3 * b, a.xn, B[3], ident)
    yield
    pe.wait_ge(s("xnT"), 3 * b + 1)
    for j in range(TB):
        c = slice(j * 16, (j + 1) * 16)
        mm(B[0][:, c], a.xnT[:, j * P:(j + 1) * P], W["mid_route"][:, :], start=True, stop=False)
        last = mm(B[0][:, c], W["ones"][:, :], W["mid_route_b"][:, :], start=False, stop=True)
    last.then_inc(s("small"), 1)
    yield
    yield
    pe.wait_ge(s("outer"), b + 1)
    for j in range(TB):
        last = nc.tensor.transpose(B[1][:, j * P:(j + 1) * P], a.outer[:, j, :], ident)
    last.then_inc(s("outerT_ps"), 1)
    yield
    pe.wait_ge(s("outerT"), b + 1)
    for j in range(TB):
        c = slice(j * P, (j + 1) * P)
        mm(B[2][:, c], a.xnT[:, c], W["base"][:, :], start=True, stop=False)
        mm(B[2][:, c], W["ones"][:, :], W["base_b"][:, :], start=False, stop=False)
        last = mm(B[2][:, c], a.outerT[:, c], W["lora_b"][:, :], start=False, stop=True)
    last.then_inc(s("y1"), 1)
    yield
    yield
    yield
    layernorm_turn(nc, pe, s, 3 * b + 1, a.xn, B[3], ident)
    yield
    pe.wait_ge(s("xnT"), 3 * b + 2)
    for n in range(2):
        mm(B[n][:, :], W["lin_qkv"][:, n, :], a.xnT[:, :], start=True, stop=True).then_inc(s("qk_ps"), 1)
    for n in range(2):
        for j in range(TB):
            c = slice(j * P, (j + 1) * P)
            mm(B[2 + n][:, c], a.xnT[:, c], W["lin_qkv"][:, 1 + n, :], start=True, stop=False)
            last = mm(B[2 + n][:, c], W["ones"][:, :], W["lin_b"][:, (1 + n) * P:(2 + n) * P], start=False, stop=True)
        last.then_inc(s("kv_ps"), 1)
    yield

    def own_keys(i):
        j, g = i // 4, i % 4
        pe.wait_ge(s("sc"), 4 * TB * b + i + 1)
        for n in range(GH):
            h = g * GH + n
            o = B[2 + j % 2][:, h * VE:(h + 1) * VE]
            last = mm(o, a.sc[:, g, n, :], a.v1[:, j, h, :], start=False, stop=True, skip_group_check=True)
        last.then_inc(s("o_ps"), 1)

    pe.wait_ge(s("kT"), b + 1)
    pe.wait_ge(s("qX"), GH * b + GH)
    pe.wait_ge(s("k_tok"), b + 1)
    pe.wait_ge(s("v1"), b + 1)
    for i in range(4 * TB):
        j, g = i // 4, i % 4
        c = slice(j * P, (j + 1) * P)
        r = slice(g * 32, (g + 1) * 32)
        if i >= 2:
            pe.wait_ge(s("sc"), 4 * TB * b + i - 1)
        mm(B[g % 2][:, :].rearrange("p (h t) -> p h t", t=P), a.kT[r, c], a.qX[r, :, c], start=True, stop=True,
           tile_position=(g * 32, 0)).then_inc(s("sc_ps"), 1)
        if i:
            own_keys(i - 1)
        if g == 0:
            pe.wait_ge(s("state"), TB * b + j + 1)
            mm(B[2 + j % 2][:, 0:HL * VE], a.qT[:, c], a.state[:, :], start=True, stop=False, skip_group_check=True).then_inc(s("inter"), 1)
        if g == 2:
            if j:
                pe.wait_ge(s("a_tok"), TB * b + j)
            mm(B[3 - j % 2][:, 0:HL * VE], a.k_tok[:, c], a.v1[:, j].rearrange("p h e -> p (h e)"), start=True, stop=True).then_inc(s("kv"), 1)
        yield
    own_keys(4 * TB - 1)
    yield
    pe.wait_ge(s("a_tok"), TB * b + TB)
    pe.wait_ge(s("state"), TB * b + TB + 1)
    for j in range(TB):
        last = nc.tensor.transpose(B[3][:, j * P:(j + 1) * P], a.a_tok[:, j * P:(j + 1) * P], ident)
    last.then_inc(s("aT_ps"), 1)
    yield
    pe.wait_ge(s("aT"), b + 1)
    for j in range(TB):
        c = slice(j * P, (j + 1) * P)
        mm(B[0][:, c], a.aT[:, c], W["lin_out"][:, :], start=True, stop=False)
        last = mm(B[0][:, c], W["ones"][:, :], W["lin_out_b"][:, :], start=False, stop=True)
    last.then_inc(s("y2"), 1)
    yield
    yield
    yield
    yield
    layernorm_turn(nc, pe, s, 3 * b + 2, a.xn, B[3], ident)
    yield
    pe.wait_ge(s("xnT"), 3 * b + 3)
    for j in range(TB):
        last = mm(B[2][:, j * EXP:(j + 1) * EXP], a.xnT[:, j * P:(j + 1) * P], W["gate"][:, 0:EXP], start=True, stop=True)
    last.then_inc(s("gate_ps"), 1)
    yield
    yield

    def up(i):
        e, n = UNITS[i]
        c, m = HC[n]
        if i:
            pe.wait_ge(s("h1"), NU * b + i)
        mm(B[0][0:m, :], W["w1"][:, e, c:c + m], a.xnT[:, :], start=True, stop=True).then_inc(s("h1_ps"), 1)
        if i:
            pe.wait_ge(s("h"), NU * b + i)
        mm(B[1][0:m, :], W["w3"][:, e, c:c + m], a.xnT[:, :], start=True, stop=True).then_inc(s("h3_ps"), 1)

    def down(i):
        e, n = UNITS[i]
        m = HC[n][1]
        pe.wait_ge(s("h"), NU * b + i + 1)
        if n == 0:
            if e >= 2:
                pe.wait_ge(s("y3_added"), EXP * b + e - 1)
            else:
                pe.wait_ge(s("cw"), 2 * b + 2)
        for j in range(TB):
            last = mm(B[2 + e % 2][:, j * P:(j + 1) * P], a.h[0:m, i % 2, j * P:(j + 1) * P], W["w2"][0:m, e, n, :],
                      start=(n == 0 and j == 0), stop=(n == len(HC) - 1), skip_group_check=True)
        last.then_inc(s("y_part"), 1)

    for i in range(NU + 1):
        if i < NU:
            up(i)
        if i:
            down(i - 1)
        yield
    yield


def rest_act(nc, act, s, b, a, B, K, W):
    f = nc.scalar.activation

    def norm(i):
        act.wait_ge(s("ve"), i + 1)
        f(a.std[:, :], a.ve[:, :], ACT.Sqrt).then_inc(s("std"), 1)
        yield
        yield
        act.wait_ge(s("xnT_ps"), i + 1)
        f(a.xnT[:, :], B[3][:, :], ACT.Copy).then_inc(s("xnT"), 1)
        yield

    yield from norm(3 * b)
    act.wait_ge(s("shifted"), 2 * b + 1)
    f(a.ex[:, :, :], a.lg[:, :, :], ACT.Exp).then_inc(s("ex"), 1)
    yield
    yield
    act.wait_ge(s("outerT_ps"), b + 1)
    f(a.outerT[:, :], B[1][0:NL * RL, :], ACT.Copy).then_inc(s("outerT"), 1)
    yield
    yield
    yield from norm(3 * b + 1)
    act.wait_ge(s("kv_ps"), 2 * b + 2)
    f(a.v1[:, :, :, 0:DL].rearrange("p j h e -> p (j h) e"), B[3][:, :].rearrange("p (g e) -> p g e", e=DL), ACT.Copy).then_inc(s("v1"), 1)
    yield
    for i in range(4 * TB):
        yield
    yield
    act.wait_ge(s("aT_ps"), b + 1)
    f(a.aT[:, :], B[3][:, :], ACT.Copy).then_inc(s("aT"), 1)
    yield
    yield
    yield
    yield from norm(3 * b + 2)
    act.wait_ge(s("shifted"), 2 * b + 2)
    f(a.ex[:, :, 0:EXP], a.lg[:, :, 0:EXP], ACT.Exp).then_inc(s("ex"), 1)
    yield
    yield
    for i in range(NU + 1):
        if i < NU:
            m = HC[UNITS[i][1]][1]
            act.wait_ge(s("h1_ps"), NU * b + i + 1)
            if i >= 2:
                act.wait_ge(s("h"), NU * b + i - 1)
            f(a.h1[0:m, i % 2, :], B[0][0:m, :], ACT.Silu).then_inc(s("h1"), 1)
        yield
    yield


def rest_dve(nc, dve, s, b, a, B, K, W, x_sb, x_in):
    v = nc.vector

    def norm(i, *added):
        layernorm_moments(nc, dve, s, i, b, x_sb, a, added)
        yield
        layernorm_apply(nc, dve, s, i, b, x_sb, a)
        yield
        yield

    def softmax(i, src, n):
        lg = a.lg[:, :, 0:n]
        v.tensor_copy(lg, src).then_inc(s("lg"), 1)
        dve.wait_ge(s("lg"), i + 1)
        v.tensor_reduce(a.mx[:, :], lg, AX.X, ALU.max).then_inc(s("mx"), 1)
        dve.wait_ge(s("mx"), i + 1)
        v.tensor_tensor(lg, lg, a.mx[:, :].unsqueeze(2).to_broadcast([P, TB, n]), ALU.subtract).then_inc(s("shifted"), 1)
        yield
        dve.wait_ge(s("ex"), i + 1)
        v.tensor_reduce(a.sm[:, :], a.ex[:, :, 0:n], AX.X, ALU.add).then_inc(s("sm"), 1)
        dve.wait_ge(s("sm"), i + 1)
        v.reciprocal(a.rs[:, :], a.sm[:, :]).then_inc(s("rs"), 1)
        dve.wait_ge(s("rs"), i + 1)

    yield from norm(3 * b, x_in, b + 2)
    small = B[0][:, 0:TB * 16].rearrange("p (j c) -> p j c", c=16)
    dve.wait_ge(s("small"), b + 1)
    v.tensor_copy(a.mid[:, :, :], small[:, :, 0:RL]).then_inc(s("mid"), 1)
    yield from softmax(2 * b, small[:, :, RL:16], NL)
    v.tensor_tensor(a.gate[:, :, :], a.ex[:, :, :], a.rs[:, :].unsqueeze(2).to_broadcast([P, TB, NL]), ALU.mult).then_inc(s("gate"), 1)
    dve.wait_ge(s("gate"), b + 1)
    dve.wait_ge(s("mid"), b + 1)
    for j in range(TB):
        last = v.tensor_tensor(a.outer[:, j, 0:NL * RL].rearrange("p (e r) -> p e r", r=RL), a.gate[:, j, :].unsqueeze(2).to_broadcast([P, NL, RL]),
                               a.mid[:, j, :].unsqueeze(1).to_broadcast([P, NL, RL]), ALU.mult)
    last.then_inc(s("outer"), 1)
    yield
    yield
    dve.wait_ge(s("y1"), b + 1)
    v.tensor_tensor(columns(x_sb, b, 0), columns(x_sb, b, 0), B[2][:, :], ALU.add).then_inc(s("y1_added"), 1)
    yield
    yield from norm(3 * b + 1, s("y1_added"), b + 1)
    for n, (t, name) in enumerate(((a.qT, "qT"), (a.kT, "kT"))):
        dve.wait_ge(s("qk_ps"), 2 * b + n + 1)
        v.tensor_scalar(t[:, :], B[n][:, :], W["lin_b_eps"][:, n:n + 1], 1e-6, ALU.add, ALU.max).then_inc(s(name), 1)
    dve.wait_ge(s("qT"), b + 1)
    for i in range(GH):
        v.tensor_scalar(a.qX[:, i, :], a.qT[:, :], K("head_of4")[:, i:i + 1], None, ALU.mult).then_inc(s("qX"), 1)
    dve.wait_ge(s("kv_ps"), 2 * b + 1)
    v.tensor_scalar(a.k_tok[:, :], B[2][:, :], 1e-6, 1e-6, ALU.add, ALU.max).then_inc(s("k_tok"), 1)
    yield

    def divide(j):
        o = B[2 + j % 2][:, 0:HL * VE].rearrange("p (h e) -> p h e", e=VE)
        dve.wait_ge(s("o_ps"), 4 * TB * b + 4 * j + 4)
        v.tensor_scalar(a.den[:, j % 2, :], o[:, :, DL], 1e-6, None, ALU.max).then_inc(s("den"), 1)
        dve.wait_ge(s("den"), TB * b + j + 1)
        v.reciprocal(a.rden[:, j % 2, :], a.den[:, j % 2, :]).then_inc(s("rden"), 1)
        dve.wait_ge(s("rden"), TB * b + j + 1)
        v.tensor_tensor(a.a_tok[:, j * P:(j + 1) * P].rearrange("p (h e) -> p h e", e=DL), o[:, :, 0:DL],
                        a.rden[:, j % 2, :].unsqueeze(2).to_broadcast([P, HL, DL]), ALU.mult).then_inc(s("a_tok"), 1)

    for i in range(4 * TB):
        j, g = i // 4, i % 4
        dve.wait_ge(s("sc_ps"), 4 * TB * b + i + 1)
        if i >= 4:
            dve.wait_ge(s("o_ps"), 4 * TB * b + i - 3)
        v.tensor_tensor(a.sc[:, g], B[g % 2][:, :].rearrange("p (h t) -> p h t", t=P),
                        K("causal").unsqueeze(1).to_broadcast([P, GH, P]), ALU.mult).then_inc(s("sc"), 1)
        if g == 3:
            dve.wait_ge(s("kv"), TB * b + j + 1)
            v.tensor_tensor(a.own[:, :], B[3 - j % 2][:, 0:HL * VE], K("head_own"), ALU.mult).then_inc(s("own"), 1)
            dve.wait_ge(s("own"), TB * b + j + 1)
            dve.wait_ge(s("inter"), TB * b + j + 1)
            v.tensor_tensor(a.state[:, :], a.state[:, :], a.own[:, :], ALU.add).then_inc(s("state"), 1)
        if g == 1 and j:
            divide(j - 1)
        yield
    divide(TB - 1)
    yield
    yield
    yield
    dve.wait_ge(s("y2"), b + 1)
    v.tensor_tensor(columns(x_sb, b, 0), columns(x_sb, b, 0), B[0][:, :], ALU.add).then_inc(s("y2_added"), 1)
    yield
    yield from norm(3 * b + 2, s("y2_added"), b + 1)
    dve.wait_ge(s("gate_ps"), b + 1)
    yield from softmax(2 * b + 1, B[2][:, 0:TB * EXP].rearrange("p (j e) -> p j e", e=EXP), EXP)
    v.tensor_tensor(a.p[:, :, :], a.ex[:, :, 0:EXP], a.rs[:, :].unsqueeze(2).to_broadcast([P, TB, EXP]), ALU.mult).then_inc(s("p"), 1)
    dve.wait_ge(s("p"), b + 1)
    for j in range(TB):
        theirs = a.p[:, j, :].unsqueeze(1).to_broadcast([P, EXP, EXP])
        mine = a.p[:, j, :].unsqueeze(2).to_broadcast([P, EXP, EXP])
        v.tensor_tensor(a.over[:, j], theirs, mine, ALU.is_gt)
        last = v.tensor_tensor(a.ties[:, j], theirs, mine, ALU.is_equal)
    last.then_inc(s("choose"), 1)
    ties = a.ties[:, :].rearrange("p j e f -> p j (e f)")
    dve.wait_ge(s("choose"), 4 * b + 1)
    v.tensor_tensor(ties, ties, K("earlier").unsqueeze(1).to_broadcast([P, TB, EXP * EXP]), ALU.mult).then_inc(s("choose"), 1)
    dve.wait_ge(s("choose"), 4 * b + 2)
    v.tensor_tensor(a.over[:, :], a.over[:, :], a.ties[:, :], ALU.add).then_inc(s("choose"), 1)
    dve.wait_ge(s("choose"), 4 * b + 3)
    v.tensor_reduce(a.rank[:, :, :], a.over[:, :, :, :], AX.X, ALU.add).then_inc(s("choose"), 1)
    dve.wait_ge(s("choose"), 4 * b + 4)
    v.scalar_tensor_tensor(a.cw[:, :, :], a.rank[:, :, :], 1.5, a.p[:, :, :], ALU.is_lt, ALU.mult).then_inc(s("cw"), 1)
    dve.wait_ge(s("cw"), 2 * b + 1)
    v.tensor_reduce(a.sm[:, :], a.cw[:, :, :], AX.X, ALU.add).then_inc(s("cw_sum"), 1)
    dve.wait_ge(s("cw_sum"), 2 * b + 1)
    v.reciprocal(a.rs[:, :], a.sm[:, :]).then_inc(s("cw_sum"), 1)
    dve.wait_ge(s("cw_sum"), 2 * b + 2)
    v.tensor_tensor(a.cw[:, :, :], a.cw[:, :, :], a.rs[:, :].unsqueeze(2).to_broadcast([P, TB, EXP]), ALU.mult).then_inc(s("cw"), 1)
    yield

    def add(e):
        dve.wait_ge(s("y_part"), NU * b + (e + 1) * len(HC))
        dve.wait_ge(s("cw"), 2 * b + 2)
        if e:
            dve.wait_ge(s("y3_added"), EXP * b + e)
        for j in range(TB):
            last = v.scalar_tensor_tensor(columns(x_sb, b, j * P, P), B[2 + e % 2][:, j * P:(j + 1) * P], a.cw[:, j, e:e + 1],
                                          columns(x_sb, b, j * P, P), ALU.mult, ALU.add)
        last.then_inc(s("y3_added"), 1)

    for i in range(NU + 1):
        if i < NU:
            e, n = UNITS[i]
            m = HC[n][1]
            dve.wait_ge(s("h1"), NU * b + i + 1)
            dve.wait_ge(s("h3_ps"), NU * b + i + 1)
            if i >= 2:
                dve.wait_ge(s("y_part"), NU * b + i - 1)
            v.tensor_tensor(a.h[0:m, i % 2, :], a.h1[0:m, i % 2, :], B[1][0:m, :], ALU.mult).then_inc(s("h"), 1)
            if n == 1 and e:
                add(e - 1)
        yield
    add(EXP - 1)
    yield


def merged(first, second):
    streams = [(first, DELTA_STEPS), (second, REST_STEPS)]
    order = []
    for n, (_, steps) in enumerate(streams):
        whole, behind = sum(steps), 0.0
        for t in steps:
            order.append(((behind + t / 2) / whole, n))
            behind += t
    for _, n in sorted(order):
        next(streams[n][0])
    for stream, _ in streams:
        assert next(stream, None) is None and next(stream, "ended") == "ended"


def alone(stream, steps):
    assert sum(1 for _ in stream) == len(steps)


def main_phase(nc, x_sb, K, W, x_loaded, weights_loaded, out):
    with ExitStack() as ctx:
        d, r = Arrays(nc, ctx, "delta"), Arrays(nc, ctx, "rest")
        delta_arrays(d)
        rest_arrays(r)
        banks = [ctx.enter_context(nc.psum_tensor(f"bank{n}", [P, BL], F32)) for n in range(8)]
        DB, RB = banks[:4], banks[4:]
        sd, sr = Signals(nc, "delta"), Signals(nc, "rest")
        y_dram = out.rearrange("a (t p) d -> p (a t) d", p=P)

        with nc.Block() as block:
            @block.gpsimd
            def _(pool):
                for t in (d.X, d.pre, d.vT, d.state, r.outer, r.state):
                    nc.gpsimd.memset(t[:], 0.0).then_inc(sd("zeroed"), 1)
                nc.gpsimd.memset(r.v1[:], 1.0).then_inc(sd("zeroed"), 1)

            @block.sync
            def _(sp):
                with sp.Fori(0, NB) as b:
                    sp.wait_ge(sr("y3_added"), EXP * b + EXP)
                    sp.dma_start(y_dram[:, bass.ds(b * TB, TB), :], columns(x_sb, b, 0).rearrange("p (t d) -> p t d", d=D)).then_inc(sr("stored"), 16)
                sp.wait_ge(sr("stored"), 16 * NB)

            @block.tensor
            def _(pe):
                pe.wait_ge(sd("zeroed"), 7)
                alone(delta_pe(nc, pe, sd, 0, d, DB, K, W), DELTA_STEPS)
                pe.wait_ge(weights_loaded[0], weights_loaded[1])
                with pe.Fori(1, NB) as b:
                    merged(delta_pe(nc, pe, sd, b, d, DB, K, W), rest_pe(nc, pe, sr, b - 1, r, RB, K, W))
                alone(rest_pe(nc, pe, sr, NB - 1, r, RB, K, W), REST_STEPS)

            @block.scalar
            def _(act):
                act.wait_ge(sd("zeroed"), 7)
                alone(delta_act(nc, act, sd, 0, d, DB, K, W), DELTA_STEPS)
                with act.Fori(1, NB) as b:
                    merged(delta_act(nc, act, sd, b, d, DB, K, W), rest_act(nc, act, sr, b - 1, r, RB, K, W))
                alone(rest_act(nc, act, sr, NB - 1, r, RB, K, W), REST_STEPS)

            @block.vector
            def _(dve):
                for name in ("out_added", "halo", "fu", "state"):
                    dve.sem_inc(sd(name), 1)
                dve.sem_inc(sr("state"), 1)
                dve.wait_ge(sd("zeroed"), 7)
                alone(delta_dve(nc, dve, sd, 0, d, DB, K, W, x_sb), DELTA_STEPS)
                with dve.Fori(1, NB) as b:
                    merged(delta_dve(nc, dve, sd, b, d, DB, K, W, x_sb), rest_dve(nc, dve, sr, b - 1, r, RB, K, W, x_sb, sd("out_added")))
                alone(rest_dve(nc, dve, sr, NB - 1, r, RB, K, W, x_sb, sd("out_added")), REST_STEPS)


def build_program(nc, args, out):
    with ExitStack() as ctx:
        def sb(name, *shape):
            return ctx.enter_context(nc.sbuf_tensor(name, list(shape), F32))

        s = Signals(nc, "setup")
        x_sb = sb("x_sb", P, NT * P)
        consts = sb("consts", P, CONSTS.shape[1])

        def K(name):
            a, n = CONST_AT[name]
            return consts[:, a:a + n]

        W = {"qkv": sb("w_qkv", P, 3, P), "b": sb("w_b", P, H), "taps": sb("w_taps", P, 3, KQ), "fir": sb("w_fir", P, sum(FIRS)),
             "m1x": sb("w_m1x", P, P), "m1s": sb("w_m1s", P, P), "m2": sb("w_m2", P, H * NBR), "b1": sb("w_b1", P, 1),
             "b2": sb("w_b2", 1, H * NBR), "ones": sb("w_ones", 1, P), "itemp": sb("w_itemp", P, H), "onorm": sb("w_onorm", P, 1),
             "o": sb("w_o", P, P),
                 "mid_route": sb("w_mid_route", P, 16), "mid_route_b": sb("w_mid_route_b", 1, 16), "base": sb("w_base", P, P),
             "base_b": sb("w_base_b", 1, P), "lora_b": sb("w_lora_b", NL * RL, P), "lin_qkv": sb("w_lin_qkv", P, 3, P),
             "lin_b": sb("w_lin_b", 1, 3 * P), "lin_b_eps": sb("w_lin_b_eps", P, 2), "lin_out": sb("w_lin_out", P, P),
             "lin_out_b": sb("w_lin_out_b", 1, P), "gate": sb("w_gate", P, NE),
             "w1": sb("w_1", P, EXP, HID), "w3": sb("w_3", P, EXP, HID), "w2": sb("w_2", P, EXP, len(HC), P)}
        setup = ExitStack()

        def passing(name, *shape):
            return setup.enter_context(nc.sbuf_tensor(name, list(shape), F32))

        rows, rows8 = passing("rows", P, 6, P), passing("rows8", NE, 2, P)
        turned = setup.enter_context(nc.psum_tensor("turned", [P, 2, BL], F32))
        t0, t1, t2 = passing("t0", P, H), passing("t1", P, H), passing("t2", P, H)
        loads = []

        def load(dst, src):
            loads.append((dst, src))

        load(x_sb[:, :].rearrange("p (t d) -> p t d", d=D), args["L0_attn_hidden_states"].rearrange("a (t p) d -> p (a t) d", p=P))
        load(consts[:, :], args["consts"])
        for n, name in enumerate(("q", "k", "v")):
            load(W["qkv"][:, n, :], args[f"L0_attn_{name}_w"])
            load(W["taps"][:, n, :], args[f"L0_attn_{name}c_w"].rearrange("d a k -> d (a k)"))
        load(W["b"][:, :], args["L0_attn_b_w"])
        at = 0
        for n in FIRS:
            load(W["fir"][:, at:at + n], args[f"L0_attn_fir_w{n}"].rearrange("d a k -> d (a k)"))
            at += n
        load(W["m1x"][:, :], args["L0_attn_mlp_w1"][0:D, :])
        by_kind = args["L0_attn_mlp_w1"][D:D + H * NBR * 4, :].rearrange("(r k) n -> k r n", k=4)
        for kind, row in ((0, 0), (2, 32), (1, 64), (3, 96)):
            load(W["m1s"][row:row + H * NBR, :], by_kind[kind])
        load(W["m2"][:, :], args["L0_attn_mlp_w2"])
        load(W["b1"][:, :], args["L0_attn_mlp_b1"].rearrange("(n a) -> n a", a=1))
        load(W["b2"][:, :], args["L0_attn_mlp_b2"].rearrange("(a n) -> a n", a=1))
        load(t0[:, :], args["L0_attn_gate_log_temp"].rearrange("(a n) -> a n", a=1).to_broadcast([P, H]))
        for h in range(H):
            load(W["onorm"][h * DK:(h + 1) * DK, :], args["L0_attn_onorm_w"].rearrange("(n a) -> n a", a=1))
        load(W["o"][:, :], args["L0_attn_o_w"])
        load(rows[:, 0, :], args["L0_ffn_base_w"])
        load(rows[:, 1:4, :], args["L1_attn_qkv_w"].rearrange("(n o) i -> o n i", o=P))
        load(rows[:, 4, :], args["L1_attn_out_w"])
        load(rows8[:, 0, :], args["L0_ffn_router_w"])
        load(rows8[:, 1, :], args["L1_ffn_gate_w"])
        load(W["mid_route"][:, 0:RL], args["L0_ffn_lora_A"])
        load(W["mid_route_b"][:, RL:16], args["L0_ffn_router_b"].rearrange("(a n) -> a n", a=1))
        load(W["base_b"][:, :], args["L0_ffn_base_b"].rearrange("(a n) -> a n", a=1))
        load(W["lora_b"][:, :], args["L0_ffn_lora_B"].rearrange("e r d -> (e r) d"))
        load(W["lin_b"][:, :], args["L1_attn_qkv_b"].rearrange("(a n) -> a n", a=1))
        for n in range(2):
            load(W["lin_b_eps"][:, n:n + 1], args["L1_attn_qkv_b"][n * P:(n + 1) * P].rearrange("(p a) -> p a", a=1))
        load(W["lin_out_b"][:, :], args["L1_attn_out_b"].rearrange("(a n) -> a n", a=1))

        whole = HID // P
        late = [(W[n][:, e, :], args[f"L1_ffn_{n}"][e]) for e in range(EXP) for n in ("w1", "w3")]
        late += [(W["w2"][:, e, 0:whole, :], args["L1_ffn_w2"][e, 0:whole * P, :].rearrange("(c k) d -> k c d", k=P)) for e in range(EXP)]
        late += [(W["w2"][0:HID - whole * P, e, whole, :], args["L1_ffn_w2"][e, whole * P:HID, :]) for e in range(EXP)]

        with nc.Block() as block:
            @block.vector
            def _(dve):
                nc.vector.memset(W["ones"][:, :], 1.0).then_inc(s("ones"), 1)
                nc.vector.memset(W["mid_route_b"][:, :], 0.0).then_inc(s("m1s_zero"), 1)
                nc.vector.memset(W["m1s"][:, :], 0.0).then_inc(s("m1s_zero"), 1)
                dve.wait_ge(s("loads"), 16 * len(loads))
                dve.wait_ge(s("log1p"), 3)
                nc.vector.tensor_scalar(t2[:, :], t0[:, :], 0.0, 0.5, ALU.max, ALU.add).then_inc(s("temp"), 1)
                dve.wait_ge(s("temp"), 1)
                nc.vector.tensor_tensor(t2[:, :], t2[:, :], t1[:, :], ALU.add).then_inc(s("temp"), 1)
                dve.wait_ge(s("temp"), 2)
                nc.vector.reciprocal(W["itemp"][:, :], t2[:, :]).then_inc(s("temp"), 1)
                dve.wait_ge(s("temp"), 3)
                nc.vector.tensor_scalar(W["lora_b"][:, :], W["lora_b"][:, :], 2.0, None, ALU.mult).then_inc(s("weights"), 1)
                nc.vector.tensor_scalar(W["lin_b_eps"][:, :], W["lin_b_eps"][:, :], 1e-6, None, ALU.add).then_inc(s("weights"), 1)
                dve.wait_ge(s("turned"), 7)
                nc.vector.tensor_copy(W["base"][:, :], turned[:, 0, 0:P]).then_inc(s("weights"), 1)
                nc.vector.tensor_copy(W["lin_qkv"][:, :, :], turned[:, 0, P:4 * P].rearrange("p (n o) -> p n o", o=P)).then_inc(s("weights"), 1)
                nc.vector.tensor_copy(W["lin_out"][:, :], turned[:, 1, 0:P]).then_inc(s("weights"), 1)
                nc.vector.tensor_copy(W["mid_route"][:, RL:16], turned[:, 1, P:P + NE]).then_inc(s("weights"), 1)
                nc.vector.tensor_copy(W["gate"][:, :], turned[:, 1, 2 * P:2 * P + NE]).then_inc(s("weights"), 1)
                dve.wait_ge(s("weights"), 7)

            @block.tensor
            def _(pe):
                pe.wait_ge(s("loads"), 16 * len(loads))
                for n in range(5):
                    nc.tensor.transpose(turned[:, n // 4, (n % 4) * P:(n % 4 + 1) * P], rows[:, n, :], K("ident")).then_inc(s("turned"), 1)
                for n in range(2):
                    nc.tensor.transpose(turned[:, 1, (n + 1) * P:(n + 1) * P + NE], rows8[:, n, :], K("ident")[0:NE, 0:NE]).then_inc(s("turned"), 1)

            @block.scalar
            def _(act):
                act.wait_ge(s("loads"), 16 * len(loads))
                nc.scalar.activation(t1[:, :], t0[:, :], ACT.Abs).then_inc(s("log1p"), 1)
                act.wait_ge(s("log1p"), 1)
                nc.scalar.activation(t1[:, :], t1[:, :], ACT.Exp, scale=-1.0).then_inc(s("log1p"), 1)
                act.wait_ge(s("log1p"), 2)
                nc.scalar.activation(t1[:, :], t1[:, :], ACT.Ln, bias=1.0).then_inc(s("log1p"), 1)

            @block.sync
            def _(sp):
                sp.wait_ge(s("m1s_zero"), 2)
                for dst, src in loads:
                    sp.dma_start(dst, src).then_inc(s("loads"), 16)
                for dst, src in late:
                    sp.dma_start(dst, src).then_inc(s("expert_weights"), 16)
                sp.wait_ge(s("loads"), 16 * len(loads))

        setup.close()
        s.clear_but("expert_weights")
        main_phase(nc, x_sb, K, W, None, (s("expert_weights"), 16 * len(late)), out)


def kernel(**inputs):
    import concourse.bacc as bacc
    from concourse.bass_utils import run_bass_kernel_spmd

    nc = bacc.Bacc("TRN2", target_bir_lowering=False, num_devices=1)
    arrays, args = {}, {}
    for name, a in list(inputs.items()) + [("consts", CONSTS)]:
        a = np.ascontiguousarray(a)
        arrays[f"in_{name}_dram"] = a
        args[name] = nc.dram_tensor(f"in_{name}_dram", a.shape, mybir.dt.from_np(a.dtype), kind="ExternalInput").ap()
    out = nc.dram_tensor("out_0_dram", (1, L, D), F32, kind="ExternalOutput").ap()
    build_program(nc, args, out)
    r = run_bass_kernel_spmd(nc, [arrays], core_ids=[0])
    return r.results[0]["out_0_dram"]
```

```python
from contextlib import ExitStack

import numpy as np
import concourse.bass as bass
from concourse import mybir

ACT = mybir.ActivationFunctionType
ALU = mybir.AluOpType
AX = mybir.AxisListType
F32 = mybir.dt.float32
F32R = mybir.dt.float32r

P = 128
L, D = 2048, 128
NT = L // P
TB = 4
BL = TB * P
NB = L // BL
H, DK = 4, 32
C = 32
CB = BL // C
NBR = 6
KQ = 4
FIRS = (1, 3, 7, 31)
PAD = max(FIRS) - 1
EXP, HID = 4, 704
NE = 8
NL, RL = 8, 8
HL, DL = 16, 8
GH = 4
HC = [(c, min(P, HID - c)) for c in range(0, HID, P)]
UNITS = [(e, n) for e in range(EXP) for n in range(len(HC))]
NU = len(UNITS)
TAPS = [(n, k) for n in range(1, len(FIRS)) for k in range(FIRS[n])]


def const_columns():
    p = np.arange(P)
    i, j = p[:, None], p[None, :]
    same = (i // C) == (j // C)
    cols = {}
    cols["ident"] = np.eye(P)
    cols["same32"] = same * 1.0
    cols["causal_then_ones"] = np.concatenate([(i <= j) * 1.0, np.ones((P, BL - P))], 1)
    jj = np.arange(C)[None, :]
    ii = (p % C)[:, None]
    cols["strict_and_upto"] = np.concatenate([ii > jj, ii <= jj], 1) * 1.0
    for m in (1, 2, 4, 8, 16):
        at = (ii // (2 * m) == jj // (2 * m)) & ((ii // m) % 2 == 0) & ((jj // m) % 2 == 1)
        cols[f"level{m}"] = at * -1.0
    cols["eye32"] = (ii == jj) * 1.0
    head = p // DK
    for name, val in (("mean", 1 / DK), ("sum_less1", 1 / (DK - 1)), ("sum", 1.0)):
        cols[name] = np.zeros((P, 32 + NBR - 1))
        cols[name][p, NBR - 1 + head * NBR] = val
    a = np.zeros((P, P))
    r = np.arange(H * NBR)
    a[r, 64 + r] = -DK / (DK - 1)
    cols["less_mean2"] = a
    for b in range(NBR):
        a = np.zeros((P, P))
        for h in range(H):
            a[h * NBR + b, h * DK:(h + 1) * DK] = 1.0
        cols[f"spread{b}"] = a
    cols["head_mean"] = same / DK
    cols["same8"] = (i // DL == j // DL) * 1.0
    cols["head_of"] = (p[:, None] // DL == np.arange(HL)[None, :]) * 1.0
    cols["earlier"] = np.tile((np.arange(EXP)[None, :] < np.arange(EXP)[:, None]).reshape(1, -1) * 1.0, (P, 1))
    for n, v in (("eps5", 1e-5), ("eps6", 1e-6)):
        cols[n] = np.full((P, 1), v)
    at, where = 0, {}
    for n, a in cols.items():
        where[n] = (at, a.shape[1])
        at += a.shape[1]
    return np.concatenate(list(cols.values()), 1).astype(np.float32), where


CONSTS, CONST_AT = const_columns()


class Signals:

    def __init__(self, nc, phase):
        self.nc, self.phase, self.of = nc, phase, {}

    def __call__(self, name):
        if name not in self.of:
            self.of[name] = self.nc.alloc_semaphore(name=f"{self.phase}_{name}")
        return self.of[name]


def columns(t, b, n, width=BL):
    return t[:, bass.ds(b * BL + n, width)]


def layernorm_moments(nc, dve, s, i, b, x_sb, a, added=None):
    v = nc.vector
    if added:
        dve.wait_ge(*added)
    v.memset(a.ve[:, :], 0.0).then_inc(s("cleared"), 1)
    for j in range(TB):
        v.bn_stats(a.stats[:, j, :], columns(x_sb, b, j * P, P)).then_inc(s("ln_stats"), 1)
    dve.wait_ge(s("ln_stats"), TB * i + TB)
    v.memset(a.rstd[:, :], 0.0).then_inc(s("cleared"), 1)
    for j in range(TB):
        v.bn_aggr(a.mv[:, j, :], a.stats[:, j, :]).then_inc(s("mv"), 1)
    dve.wait_ge(s("mv"), TB * i + TB)
    dve.wait_ge(s("cleared"), 2 * i + 1)
    v.tensor_scalar(a.ve[:, :], a.mv[:, :, 1], 1e-5, None, ALU.add).then_inc(s("ve"), 1)


def layernorm_apply(nc, dve, s, i, b, x_sb, a):
    v = nc.vector
    dve.wait_ge(s("std"), i + 1)
    dve.wait_ge(s("cleared"), 2 * i + 2)
    v.reciprocal(a.rstd[:, :], a.std[:, :]).then_inc(s("rstd"), 1)
    dve.wait_ge(s("rstd"), i + 1)
    for j in range(TB):
        v.tensor_scalar(a.xn[:, j * P:(j + 1) * P], columns(x_sb, b, j * P, P), a.mv[:, j, 0:1], a.rstd[:, j:j + 1],
                        ALU.subtract, ALU.mult).then_inc(s("xn"), 1)


def layernorm_turn(nc, pe, s, i, xn, bank, ident):
    pe.wait_ge(s("xn"), TB * i + TB)
    for j in range(TB):
        last = nc.tensor.transpose(bank[:, j * P:(j + 1) * P], xn[:, j * P:(j + 1) * P], ident)
    last.then_inc(s("xnT_ps"), 1)


class Arrays:

    def __init__(self, nc, ctx, prefix):
        self.nc, self.ctx, self.prefix = nc, ctx, prefix

    def new(self, name, *shape, dt=F32):
        return self.ctx.enter_context(self.nc.sbuf_tensor(f"{self.prefix}_{name}", list(shape), dt))


def layernorm_arrays(a):
    a.stats = a.new("stats", P, TB, 6)
    a.mv = a.new("mv", P, TB, 2)
    a.ve = a.new("ve", P, TB)
    a.std = a.new("std", P, TB)
    a.rstd = a.new("rstd", P, TB)
    a.xn = a.new("xn", P, BL)
    a.xnT = a.new("xnT", P, BL)


def delta_arrays(a):
    layernorm_arrays(a)
    a.pre = a.new("pre", P, 3, KQ - 1 + BL)
    a.conv = a.new("conv", P, 3, BL)
    a.beta = a.new("beta", P, TB, H)
    a.temperature = a.new("temperature", P, 2, H)
    a.qT = a.new("qT", P, BL)
    a.kT = a.new("kT", P, BL)
    a.vT = a.new("vT", P, PAD + BL)
    a.sq = a.new("sq", P, 2, BL)
    a.nrm = a.new("nrm", P, TB, 8)
    a.root = a.new("root", P, TB, 8)
    a.rn = a.new("rn", P, TB, 8)
    a.gam = a.new("gam", P, TB, H)
    a.rkb = a.new("rkb", P, TB, H)
    a.k_tok = a.new("k_tok", P, BL)
    a.vk = a.new("vk", P, TB, H, 2, DK)
    a.A_at = a.new("A_at", P, 2, TB * H, C)
    a.A, a.at = a.A_at[:, 0], a.A_at[:, 1]
    a.E = a.new("E", P, TB * H, C)
    a.Pm = a.new("Pm", P, TB * H, C)
    a.Tc = a.new("Tc", P, TB * H, C)
    a.u0 = a.new("u0", P, TB, H, DK)
    a.w_tok = a.new("w_tok", P, TB, H, DK)
    a.wT = a.new("wT", P, BL)
    a.u = a.new("u", P, TB, H, DK)
    a.state = a.new("state", P, P)
    a.br = a.new("br", P, 5, BL)
    a.absb = a.new("absb", P, 2, BL)
    a.hid = a.new("hid", P, BL)
    a.lg = a.new("lg", P, TB, H, NBR)
    a.mx = a.new("mx", P, TB, H)
    a.ex = a.new("ex", P, TB, H, NBR)
    a.sm = a.new("sm", P, TB, H)
    a.rs = a.new("rs", P, TB, H)
    a.wt = a.new("wt", P, TB, H, NBR)
    a.sqb = a.sq
    a.part = a.absb
    a.o_tok = a.w_tok[:, :, :, :].rearrange("p j h c -> p (j h c)")
    a.st2 = a.hid
    a.var = a.Tc[:, :, :].rearrange("p n c -> p (n c)")
    a.st = a.Pm[:, :, :].rearrange("p n c -> p (n c)")
    a.fu = a.E[:, :, :].rearrange("p n c -> p (n c)")
    a.wtT = a.u0[0:H * NBR, :, :, :].rearrange("p j h c -> p (j h c)")


STATS_AT = {5: 2, 0: 4, 1: 6, 2: 10, 3: 25}
STATS_ORDER = [5, 0, 1, 2, 3, 4]
DELTA_TAPS = [2, 0, 1, 1, 1, 2, 2, 2, 0, 2, 2, 2, 2]
CHUNK_TAPS = 1

MORE_WEIGHTS_AT = 5
DELTA_STEPS = 6 + H + 1 + 8 + 2 + 2 * CB + 8 + NBR + 3


def head_bank(h):
    return (h + 3) % 4


def delta_norm_pe(nc, pe, s, b, a, B, K):
    yield
    yield
    pe.wait_ge(s("out_added"), b + 1)
    layernorm_turn(nc, pe, s, b, a.xn, B[0], K("ident"))
    yield


def delta_norm_act(nc, act, s, b, a, B):
    f = nc.scalar.activation
    act.wait_ge(s("ve"), b + 1)
    f(a.std[:, :], a.ve[:, :], ACT.Sqrt).then_inc(s("std"), 1)
    yield
    yield
    act.wait_ge(s("xnT_ps"), b + 1)
    f(a.xnT[:, :], B[0][:, :], ACT.Copy).then_inc(s("xnT"), 1)
    yield


def delta_norm_dve(nc, dve, s, b, a, x_sb):
    layernorm_moments(nc, dve, s, b, b, x_sb, a)
    yield
    layernorm_apply(nc, dve, s, b, b, x_sb, a)
    yield
    yield


def with_next_norm(block, norm):
    for n in range(DELTA_STEPS):
        next(block)
        yield
        if n >= DELTA_STEPS - 3:
            next(norm)
            yield
    assert next(block, "ended") == "ended" and next(norm, "ended") == "ended"


def delta_pe(nc, pe, s, b, a, B, K, W):
    def mm(out, lhsT, rhs, start=True, stop=True, **kw):
        return nc.tensor.matmul(out, lhsT, rhs, start=start, stop=stop, **kw)

    def chunk_products(out, lhsT, rhs, width=C):
        for n in range(TB * H):
            for g in range(P // C):
                q = slice(g * C, (g + 1) * C)
                last = mm(out(q, n), lhsT[q, n, :], rhs(q, n), tile_position=(q.start, q.start))
        return last

    def begun():
        pe.sem_inc(s("begun"), 1)

    ident = K("ident")
    pe.wait_ge(s("xnT"), b + 1)
    pe.wait_ge(s("fu"), (NBR - 1) * b + 1)
    for n in range(3):
        mm(B[1 + n][:, :], W["qkv"][:, n, :], a.xnT[:, :]).then_inc(s("proj"), 1)
    for j in range(TB):
        last = mm(B[0][:, j * 8:j * 8 + H], a.xnT[:, j * P:(j + 1) * P], W["b"][:, :])
    last.then_inc(s("beta_ps"), 1)
    yield
    yield
    yield
    yield
    pe.wait_ge(s("qk_sq"), 2 * b + 2)
    pe.wait_ge(s("beta_tanh"), b + 1)
    for j in range(TB):
        for n in range(2):
            last = mm(B[0][:, 64 + j * 8 + n * H:64 + j * 8 + (n + 1) * H],
                      a.sq[:, n, j * P:(j + 1) * P], K("same32").rearrange("p (h c) -> p h c", c=DK)[:, :, 0])
    last.then_inc(s("norms_ps"), 1)
    pe.wait_ge(s("kT"), b + 1)
    for j in range(TB):
        last = nc.tensor.transpose(B[1][:, j * P:(j + 1) * P], a.kT[:, j * P:(j + 1) * P], ident)
    last.then_inc(s("k_tok_ps"), 1)
    pe.wait_ge(s("vT"), b + 1)
    for j in range(TB):
        last = nc.tensor.transpose(B[2][:, j * P:(j + 1) * P], a.vT[:, PAD + j * P:PAD + (j + 1) * P], ident)
    last.then_inc(s("v_tok_ps"), 1)
    yield
    yield
    for h in range(H):
        if h == 1:
            pe.wait_ge(s("nrm"), b + 1)
            begun()
        if h >= 2:
            pe.wait_ge(s("vk"), 2 * b + h - 1)
            begun()
        r = slice(h * DK, (h + 1) * DK)
        for i, t in enumerate((a.kT, a.qT)):
            for c in range(CB):
                at = i * P + (c // 4) * C
                q, cs = slice((c % 4) * C, (c % 4 + 1) * C), slice(c * C, (c + 1) * C)
                last = mm(B[head_bank(h)][q, at:at + C], a.kT[r, cs], t[r, cs], tile_position=(r.start, q.start))
        last.then_inc(s("gram"), 1)
        yield
    yield
    for r in range(4):
        pe.wait_ge(s("E"), 5 * b + r + 1)
        begun()
        chunk_products(lambda q, n: B[3][q, n * C:(n + 1) * C], a.A, lambda q, n: a.E[q, n, :]).then_inc(s("UE"), 1)
        yield
        pe.wait_ge(s("Tc"), 4 * b + r + 1)
        pe.wait_ge(s("Pm"), 4 * b + r + 1)
        begun()
        chunk_products(lambda q, n: B[1][q, n * C:(n + 1) * C], a.Tc, lambda q, n: a.Pm[q, n, :]).then_inc(s("EUE"), 1)
        yield
    pe.wait_ge(s("E"), 5 * b + 5)
    begun()
    chunk_products(lambda q, n: B[2 + n // 8][q, (n % 8) * 64:(n % 8) * 64 + 64], a.E,
                   lambda q, n: a.vk[q, n // H, n % H].rearrange("p a c -> p (a c)")).then_inc(s("uw_ps"), 1)
    yield
    pe.wait_ge(s("w_tok"), b + 1)
    for j in range(TB):
        last = nc.tensor.transpose(B[1][:, j * P:(j + 1) * P], a.w_tok[:, j].rearrange("p h c -> p (h c)"), ident)
    last.then_inc(s("wT_ps"), 1)
    yield

    def branch_sums(n):
        x = a.br[:, n, :] if n < 5 else a.vT[:, PAD:]
        i = STATS_ORDER.index(n)
        pe.wait_ge(s("square"), NBR * b + i + 1)
        if n < 5:
            pe.wait_ge(s(f"branch{n}"), b + 1)
        for kind, (sum_of, t) in enumerate((("mean", x), ("mean", a.absb[:, i % 2, :]), ("sum_less1", a.sqb[:, i % 2, :]),
                                            ("sum", a.sqb[:, i % 2, :]))):
            last = mm(B[2][kind * 32:(kind + 1) * 32, :], K(sum_of)[:, NBR - 1 - n:NBR - 1 - n + 32], t, start=(i == 0),
                      stop=(i == NBR - 1), tile_position=(0, kind * 32))
        last.then_inc(s("sums"), 1)

    pe.wait_ge(s("wT"), b + 1)
    pe.wait_ge(s("u0"), b + 1)
    for half in range(2 * CB):
        c = half // 2
        j, q = c // 4, slice((c % 4) * C, (c % 4 + 1) * C)
        t = slice(c * C, (c + 1) * C)
        cs = slice(j * P, (j + 1) * P)
        if half % 2 == 0:
            pe.wait_ge(s("state"), b * CB + c + 1)
            if c == 0:
                mm(B[3][:, 0:P], ident, a.state[:, :], stop=False, skip_group_check=True)
            mm(B[1][q, 0:P], a.wT[:, t], a.state[:, :], tile_position=(0, q.start)).then_inc(s("wS"), 1)
            mm(B[0][q, cs], a.qT[:, t], a.state[:, :], tile_position=(0, q.start), stop=False, skip_group_check=True).then_inc(s("qS"), 1)
        else:
            pe.wait_ge(s("u"), b * CB + c + 1)
            mm(B[3][:, 0:P], a.k_tok[q, cs], a.u[q, j].rearrange("p h c -> p (h c)"), start=False,
               tile_position=(q.start, 0), skip_group_check=True).then_inc(s("kU"), 1)
            for h in range(H):
                last = mm(B[0][q, j * P + h * DK:j * P + (h + 1) * DK], a.at[q, j * H + h, :], a.u[q, j, h, :],
                          start=False, stop=True, tile_position=(q.start, q.start), skip_group_check=True)
            last.then_inc(s("o_ps"), 1)
        for n, when in STATS_AT.items():
            if half == when + 1:
                branch_sums(n)
        yield
    yield
    pe.wait_ge(s("o_tok"), b + 1)
    for j in range(TB):
        last = nc.tensor.transpose(B[1][:, j * P:(j + 1) * P], a.o_tok[:, j * P:(j + 1) * P], ident)
    last.then_inc(s("oT_ps"), 1)
    yield
    branch_sums(4)
    yield
    pe.wait_ge(s("st2"), b + 1)
    mm(B[3][:, :], K("less_mean2"), a.st2[:, :]).then_inc(s("mean2"), 1)
    mm(B[1][:, :], W["m1x"][:, :], a.xnT[:, :], stop=False)
    yield
    pe.wait_ge(s("st"), 2 * b + 2)
    mm(B[1][:, :], W["m1s"][:, :], a.st[:, :], start=False).then_inc(s("hid_ps"), 1)
    yield
    pe.wait_ge(s("hid"), b + 1)
    for j in range(TB):
        last = mm(B[0][:, j * 24:(j + 1) * 24], a.hid[:, j * P:(j + 1) * P], W["m2"][:, :])
    last.then_inc(s("logits"), 1)
    yield
    yield
    pe.wait_ge(s("wt"), b + 1)
    for j in range(TB):
        last = nc.tensor.transpose(B[3][0:H * NBR, j * P:(j + 1) * P], a.wt[:, j].rearrange("p h b -> p (h b)"), ident)
    last.then_inc(s("wtT_ps"), 1)
    yield
    pe.wait_ge(s("wtT"), b + 1)
    for n in range(NBR):
        if n >= 2:
            pe.wait_ge(s("mixed"), NBR * b + n - 1)
        mm(B[2 + n % 2][:, :], K(f"spread{n}")[0:H * NBR, :], a.wtT[:, :]).then_inc(s("spread"), 1)
        yield
    pe.wait_ge(s("fsq"), b + 1)
    mm(B[1][:, :], K("head_mean"), a.sq[:, 0, :]).then_inc(s("ms"), 1)
    yield
    yield
    pe.wait_ge(s("fn"), b + 1)
    for j in range(TB):
        last = mm(B[0][:, j * P:(j + 1) * P], a.conv[:, 0, j * P:(j + 1) * P], W["o"][:, :])
    last.then_inc(s("out_ps"), 1)
    yield


def delta_act(nc, act, s, b, a, B, K, W):
    f = nc.scalar.activation
    act.wait_ge(s("halo"), b + 1)
    for n in range(3):
        act.wait_ge(s("proj"), 3 * b + n + 1)
        f(a.pre[:, n, KQ - 1:], B[1 + n][:, :], ACT.Copy).then_inc(s("pre_in"), 1)
    yield
    act.wait_ge(s("beta_ps"), b + 1)
    f(a.beta[:, :, :], B[0][:, 0:TB * 8].rearrange("p (j h) -> p j h", h=8)[:, :, 0:H], ACT.Tanh, scale=0.5).then_inc(s("beta_tanh"), 1)
    for n, (plain, name) in enumerate(((a.qT, "q"), (a.kT, "k"))):
        act.wait_ge(s("conv"), 3 * b + n + 1)
        f(plain[:, :], a.conv[:, n, :], ACT.Silu).then_inc(s(name + "T"), 1)
        act.wait_ge(s(name + "T"), b + 1)
        f(a.sq[:, n, :], plain[:, :], ACT.Square).then_inc(s("qk_sq"), 1)
        yield
    act.wait_ge(s("conv"), 3 * b + 3)
    f(a.vT[:, PAD:], a.conv[:, 2, :], ACT.Silu).then_inc(s("vT"), 1)
    yield
    act.wait_ge(s("nrm"), b + 1)
    f(a.root[:, :, :], a.nrm[:, :, :], ACT.Sqrt).then_inc(s("root"), 1)
    act.wait_ge(s("k_tok_ps"), b + 1)
    f(a.k_tok[:, :], B[1][:, :], ACT.Copy).then_inc(s("k_tok"), 1)
    yield
    act.wait_ge(s("vT"), b + 1)
    f(a.br[:, 0, :], a.vT[:, PAD:], ACT.Copy, scale=W["fir"][:, 0:1]).then_inc(s("branch0"), 1)
    yield
    for h in range(H):
        yield
    yield
    for r in range(4):
        yield
        yield
    act.wait_ge(s("uw_ps"), b + 1)
    for part, t, name in ((1, a.w_tok, "w_tok"), (0, a.u0, "u0")):
        for n in range(2):
            uw = B[2 + n][:, :].rearrange("p (g a c) -> p g a c", g=2 * H, a=2)
            last = f(t[:, 2 * n:2 * n + 2].rearrange("p j h c -> p (j h) c"), uw[:, :, part, :], ACT.Copy)
        last.then_inc(s(name), 1)
    yield
    act.wait_ge(s("wT_ps"), b + 1)
    f(a.wT[:, :], B[1][:, :], ACT.Copy).then_inc(s("wT"), 1)
    yield

    def branch_magnitudes(n):
        i = STATS_ORDER.index(n)
        x = a.br[:, n, :] if n < 5 else a.vT[:, PAD:]
        if n < 5:
            act.wait_ge(s(f"branch{n}"), b + 1)
        if i >= 2:
            act.wait_ge(s("sums"), NBR * b + i - 1)
        f(a.absb[:, i % 2, :], x, ACT.Abs)
        f(a.sqb[:, i % 2, :], x, ACT.Square).then_inc(s("square"), 1)

    for half in range(2 * CB):
        for n, when in STATS_AT.items():
            if half == when:
                branch_magnitudes(n)
        yield
    yield
    act.wait_ge(s("oT_ps"), b + 1)
    f(a.br[:, 4, :], B[1][:, :], ACT.Copy).then_inc(s("branch4"), 1)
    yield
    branch_magnitudes(4)
    yield
    act.wait_ge(s("sums"), NBR * b + NBR)
    f(a.st2[:, :], B[2][:, :], ACT.Square).then_inc(s("st2"), 1)
    f(a.st[0:64, :], B[2][0:64, :], ACT.Copy).then_inc(s("st"), 1)
    yield
    act.wait_ge(s("var"), 3 * b + 3)
    f(a.st[64:P, :], a.var[64:P, :], ACT.Sqrt).then_inc(s("st"), 1)
    yield
    act.wait_ge(s("hid_ps"), b + 1)
    f(a.hid[:, :], B[1][:, :], ACT.Gelu, bias=W["b1"][:, 0:1]).then_inc(s("hid"), 1)
    yield
    act.wait_ge(s("lg"), 4 * b + 4)
    f(a.ex[:, :, :, :], a.lg[:, :, :, :], ACT.Exp).then_inc(s("ex"), 1)
    yield
    act.wait_ge(s("wtT_ps"), b + 1)
    f(a.wtT[:, :], B[3][0:H * NBR, :], ACT.Copy).then_inc(s("wtT"), 1)
    yield
    for n in range(NBR):
        yield
    act.wait_ge(s("fu"), (NBR - 1) * b + NBR)
    f(a.sq[:, 0, :], a.fu[:, :], ACT.Square).then_inc(s("fsq"), 1)
    yield
    act.wait_ge(s("ms"), b + 1)
    f(a.sq[:, 1, :], B[1][:, :], ACT.Ln, bias=K("eps5")).then_inc(s("lnv"), 1)
    act.wait_ge(s("lnv"), b + 1)
    f(a.conv[:, 1, :], a.sq[:, 1, :], ACT.Exp, scale=-0.5).then_inc(s("rr"), 1)
    yield
    yield


def delta_dve(nc, dve, s, b, a, B, K, W, x_sb):
    v = nc.vector
    yield
    for n in range(3):
        dve.wait_ge(s("pre_in"), 3 * b + n + 1)
        v.tensor_scalar(a.conv[:, n, :], a.pre[:, n, 0:BL], W["taps"][:, n, 0:1], None, ALU.mult).then_inc(s("tap"), 1)
        for k in range(1, KQ):
            dve.wait_ge(s("tap"), 9 * b + 3 * n + k)
            ins = v.scalar_tensor_tensor(a.conv[:, n, :], a.pre[:, n, k:k + BL], W["taps"][:, n, k:k + 1], a.conv[:, n, :],
                                         ALU.mult, ALU.add)
            ins.then_inc(s("conv" if k == KQ - 1 else "tap"), 1)
        if n == 2:
            dve.wait_ge(s("conv"), 3 * b + 3)
            v.tensor_copy(a.pre[:, :, 0:KQ - 1], a.pre[:, :, BL:BL + KQ - 1]).then_inc(s("halo"), 1)
            dve.wait_ge(s("beta_tanh"), b + 1)
            v.tensor_scalar(a.beta[:, :, :], a.beta[:, :, :], 0.5, 0.5, ALU.mult, ALU.add).then_inc(s("beta"), 1)
        yield
    first_tap = [sum(FIRS[:n]) for n in range(len(FIRS))]
    chained = len(TAPS) - len(FIRS[1:])

    def fir_tap(i):
        n, k = TAPS[i]
        at = PAD - FIRS[n] + 1 + k
        w = W["fir"][:, first_tap[n] + k:first_tap[n] + k + 1]
        if k == 0:
            ins = v.tensor_scalar(a.br[:, n, :], a.vT[:, at:at + BL], w, None, ALU.mult)
        else:
            dve.wait_ge(s("fir_tap"), chained * b + i - n + 1)
            ins = v.scalar_tensor_tensor(a.br[:, n, :], a.vT[:, at:at + BL], w, a.br[:, n, :], ALU.mult, ALU.add)
        ins.then_inc(s(f"branch{n}" if k == FIRS[n] - 1 else "fir_tap"), 1)

    def fir_taps(slot):
        done = sum(DELTA_TAPS[:slot]) + CHUNK_TAPS * max(0, slot - len(DELTA_TAPS))
        here = DELTA_TAPS[slot] if slot < len(DELTA_TAPS) else CHUNK_TAPS
        for i in range(done, min(done + here, len(TAPS))):
            if i == 0:
                dve.wait_ge(s("vT"), b + 1)
            fir_tap(i)


    dve.wait_ge(s("norms_ps"), b + 1)
    v.tensor_scalar(a.nrm[:, :, :], B[0][:, 64:64 + TB * 8].rearrange("p (j h) -> p j h", h=8), 1e-6, None, ALU.add).then_inc(s("nrm"), 1)
    yield
    dve.wait_ge(s("root"), b + 1)
    v.reciprocal(a.rn[:, :, :], a.root[:, :, :]).then_inc(s("scale"), 1)
    dve.wait_ge(s("scale"), 3 * b + 1)
    dve.wait_ge(s("beta"), b + 1)
    v.tensor_tensor(a.rkb[:, :, :], a.beta[:, :, :], a.rn[:, :, H:2 * H], ALU.mult).then_inc(s("scale"), 1)
    dve.wait_ge(s("scale"), 3 * b + 2)
    v.tensor_tensor(a.gam[:, :, :], a.rkb[:, :, :], a.rn[:, :, H:2 * H], ALU.mult).then_inc(s("scale"), 1)
    dve.wait_ge(s("scale"), 3 * b + 3)

    def heads(t):
        return t.rearrange("p (g c) -> p g c", c=DK)

    def per_head(t):
        return t.rearrange("p j h -> p (j h)").unsqueeze(2).to_broadcast([P, TB * H, DK])

    def all_heads(m):
        return m.unsqueeze(1).to_broadcast([P, TB * H, C])

    vk = a.vk[:, :, :, :, :].rearrange("p j h a c -> p (j h) a c")
    dve.wait_ge(s("k_tok"), b + 1)
    v.tensor_tensor(vk[:, :, 1, :], heads(B[1][:, :]), per_head(a.gam[:, :, :]), ALU.mult).then_inc(s("vk"), 1)
    dve.wait_ge(s("v_tok_ps"), b + 1)
    v.tensor_tensor(vk[:, :, 0, :], heads(B[2][:, :]), per_head(a.rkb[:, :, :]), ALU.mult).then_inc(s("vk"), 1)
    yield
    A_at = a.A_at[:, :, :, :].rearrange("p k (j h) c -> p k j h c", h=H)
    masks = K("strict_and_upto").rearrange("p (k c) -> p k c", c=C).unsqueeze(2).to_broadcast([P, 2, TB, C])
    for h in range(H):
        dve.wait_ge(s("gram"), H * b + h + 1)
        v.tensor_tensor(A_at[:, :, :, h, :], B[head_bank(h)][:, 0:2 * P].rearrange("p (k j c) -> p k j c", k=2, c=C), masks,
                        ALU.mult).then_inc(s("A_at"), 1)
        fir_taps(h)
        yield
    dve.wait_ge(s("A_at"), H * b + H)
    v.tensor_tensor(a.A, a.A, per_head(a.gam[:, :, :]), ALU.mult).then_inc(s("pairs"), 1)
    dve.wait_ge(s("pairs"), 3 * b + 1)
    v.transpose(a.Tc[:, :, :].rearrange("p n c -> p (n c)"), a.A.rearrange("p n c -> p (n c)")).then_inc(s("pairs"), 1)
    dve.wait_ge(s("pairs"), 3 * b + 2)
    v.tensor_tensor(a.Pm[:, :, :], a.Tc[:, :, :], all_heads(K("level1")), ALU.mult).then_inc(s("pairs"), 1)
    dve.wait_ge(s("pairs"), 3 * b + 3)
    v.tensor_tensor(a.E[:, :, :], a.Pm[:, :, :], all_heads(K("eye32")), ALU.add).then_inc(s("E"), 1)
    fir_taps(H)
    yield
    for r in range(4):
        dve.wait_ge(s("E"), 5 * b + r + 1)
        v.transpose(a.Tc[:, :, :].rearrange("p n c -> p (n c)"), a.E[:, :, :].rearrange("p n c -> p (n c)")).then_inc(s("Tc"), 1)
        dve.wait_ge(s("UE"), 4 * b + r + 1)
        v.tensor_tensor(a.Pm[:, :, :], B[3][:, :].rearrange("p (n c) -> p n c", c=C), all_heads(K(f"level{2 << r}")), ALU.mult).then_inc(s("Pm"), 1)
        fir_taps(H + 1 + 2 * r)
        yield
        dve.wait_ge(s("EUE"), 4 * b + r + 1)
        dve.wait_ge(s("Tc"), 4 * b + r + 1)
        v.tensor_tensor(a.E[:, :, :], a.E[:, :, :], B[1][:, :].rearrange("p (n c) -> p n c", c=C), ALU.add).then_inc(s("E"), 1)
        fir_taps(H + 2 + 2 * r)
        yield
    yield
    yield
    for half in range(2 * CB):
        c = half // 2
        j, q = c // 4, slice((c % 4) * C, (c % 4 + 1) * C)
        if half % 2 == 0:
            dve.wait_ge(s("wS"), CB * b + c + 1)
            if c == 0:
                dve.wait_ge(s("u0"), b + 1)
            v.tensor_tensor(a.u[q, j], a.u0[q, j], B[1][q, 0:P].rearrange("p (h c) -> p h c", c=DK), ALU.subtract).then_inc(s("u"), 1)
        else:
            dve.wait_ge(s("kU"), CB * b + c + 1)
            dve.wait_ge(s("qS"), CB * b + c + 1)
            v.tensor_tensor(a.state[:, :], B[3][:, 0:P], K("same32"), ALU.mult).then_inc(s("state"), 1)
        fir_taps(len(DELTA_TAPS) + half)
        yield
    dve.wait_ge(s("o_ps"), CB * b + CB)
    v.tensor_tensor(a.o_tok[:, :].rearrange("p (g c) -> p g c", c=DK), heads(B[0][:, :]),
                    a.rn[:, :, 0:H].unsqueeze(3).to_broadcast([P, TB, H, DK]), ALU.mult).then_inc(s("o_tok"), 1)
    yield
    yield
    yield
    dve.wait_ge(s("st2"), b + 1)
    v.tensor_copy(a.var[64:P, :], B[2][64:P, :]).then_inc(s("var"), 1)
    dve.wait_ge(s("mean2"), b + 1)
    dve.wait_ge(s("var"), 3 * b + 1)
    v.tensor_tensor(a.var[64:P, :], a.var[64:P, :], B[3][64:P, :], ALU.add).then_inc(s("var"), 1)
    dve.wait_ge(s("var"), 3 * b + 2)
    v.tensor_scalar(a.var[64:P, :], a.var[64:P, :], 0.0, None, ALU.max).then_inc(s("var"), 1)
    yield
    yield
    dve.wait_ge(s("logits"), b + 1)
    v.tensor_tensor(a.lg[:, :, :, :], B[0][:, 0:TB * 24].rearrange("p (j h n) -> p j h n", j=TB, h=H),
                    W["itemp"][:, :].unsqueeze(1).unsqueeze(3).to_broadcast([P, TB, H, NBR]), ALU.mult).then_inc(s("lg"), 1)
    dve.wait_ge(s("lg"), 4 * b + 1)
    v.tensor_tensor(a.lg[:, :, :, :], a.lg[:, :, :, :], W["b2"][:, :, :].unsqueeze(1).to_broadcast([P, TB, H, NBR]), ALU.add).then_inc(s("lg"), 1)
    dve.wait_ge(s("lg"), 4 * b + 2)
    v.tensor_reduce(a.mx[:, :, :], a.lg[:, :, :, :], AX.X, ALU.max).then_inc(s("lg"), 1)
    dve.wait_ge(s("lg"), 4 * b + 3)
    v.tensor_tensor(a.lg[:, :, :, :], a.lg[:, :, :, :], a.mx[:, :, :].unsqueeze(3).to_broadcast([P, TB, H, NBR]), ALU.subtract).then_inc(s("lg"), 1)
    yield
    dve.wait_ge(s("ex"), b + 1)
    v.tensor_reduce(a.sm[:, :, :], a.ex[:, :, :, :], AX.X, ALU.add).then_inc(s("sum"), 1)
    dve.wait_ge(s("sum"), 2 * b + 1)
    v.reciprocal(a.rs[:, :, :], a.sm[:, :, :]).then_inc(s("sum"), 1)
    dve.wait_ge(s("sum"), 2 * b + 2)
    v.tensor_tensor(a.wt[:, :, :, :], a.ex[:, :, :, :], a.rs[:, :, :].unsqueeze(3).to_broadcast([P, TB, H, NBR]), ALU.mult).then_inc(s("wt"), 1)
    yield
    yield
    for n in range(NBR):
        x = a.br[:, n, :] if n < 5 else a.vT[:, PAD:]
        dve.wait_ge(s("spread"), NBR * b + n + 1)
        if n > 2:
            dve.wait_ge(s("fu"), (NBR - 1) * b + n - 1)
        v.tensor_tensor(a.fu[:, :] if n == 0 else a.part[:, n % 2, :], x, B[2 + n % 2][:, :], ALU.mult).then_inc(s("mixed"), 1)
        if n:
            dve.wait_ge(s("mixed"), NBR * b + n + 1)
            dve.wait_ge(s("fu"), (NBR - 1) * b + n)
            v.tensor_tensor(a.fu[:, :], a.fu[:, :], a.part[:, n % 2, :], ALU.add).then_inc(s("fu"), 1)
        if n == NBR - 1:
            v.tensor_copy(a.vT[:, 0:PAD], a.vT[:, BL:BL + PAD])
        yield
    yield
    yield
    dve.wait_ge(s("rr"), b + 1)
    v.scalar_tensor_tensor(a.conv[:, 0, :], a.fu[:, :], W["onorm"][:, 0:1], a.conv[:, 1, :], ALU.mult, ALU.mult).then_inc(s("fn"), 1)
    dve.wait_ge(s("out_ps"), b + 1)
    v.tensor_tensor(columns(x_sb, b, 0), columns(x_sb, b, 0), B[0][:, :], ALU.add).then_inc(s("out_added"), 1)
    yield


def rest_arrays(a):
    layernorm_arrays(a)
    a.mid = a.new("mid", P, TB, RL)
    a.lg = a.new("lg", P, TB, NL)
    a.mx = a.new("mx", P, TB)
    a.ex = a.new("ex", P, TB, NL)
    a.sm = a.new("sm", P, TB)
    a.rs = a.new("rs", P, TB)
    a.gate = a.new("gate", P, TB, NL, dt=mybir.dt.bfloat16)
    a.outer = a.new("outer", P, TB, P)
    a.outerT = a.new("outerT", NL * RL + 1, BL)
    a.qT = a.new("qT", P, BL)
    a.kT = a.new("kT", P, BL)
    a.q_wide = a.new("q_wide", P, 4, GH, P)
    a.k_tok = a.new("k_tok", P, BL)
    a.v_tok = a.new("v_tok", P, BL)
    a.v_wide = a.new("v_wide", P, TB, HL, 32)
    a.keys_before = a.new("keys_before", P, 1)
    a.q_keys = a.new("q_keys", P, BL)
    a.sc = a.new("sc", P, 4, GH, P)
    a.own = a.new("own", P, TB, P)
    a.states = a.new("states", P, TB, P)
    a.den = a.q_keys
    a.rden = a.new("rden", P, BL)
    a.aT = a.new("aT", P, BL)
    a.p = a.new("p", P, TB, EXP)
    a.over = a.new("over", P, TB, EXP, EXP)
    a.ties = a.new("ties", P, TB, EXP, EXP)
    a.rank = a.new("rank", P, TB, EXP)
    a.cw = a.new("cw", P, TB, EXP)
    a.h1, a.h = (a.sc[:, n:n + 2].rearrange("p n h t -> p n (h t)") for n in (0, 2))
    a.x_lead, a.x_rest = a.new("x_lead", P, BL, dt=F32R), a.new("x_rest", P, BL, dt=F32R)


REST_STEPS = (3 + 4) + (3 + 1) + 4 * TB + 3 + (3 + 2) + (NU + 1) + 1
PLACES = [
    0, 0, 1, 1, 2, 2, 4, 4, 5, 6, 8, 11, 11, 12, 12, 12, 13, 13, 14, 14, 14, 14, 14, 14, 15, 15, 16, 17, 19,
    19, 19, 20, 21, 22, 26, 28, 31, 32, 34, 36, 38, 40, 42, 44, 46, 47, 49, 51, 52, 53, 55, 56, 57, 59, 60,
    61, 63, 65, 67, 72, 72
]


KEYS_AT, DEN_AT, STATES_AT, BIAS_AT = 1, 3, 5, 8


def rest_pe(nc, pe, s, b, a, B, K, W):
    mm = nc.tensor.matmul
    ident = K("ident")
    yield
    yield
    layernorm_turn(nc, pe, s, 3 * b, a.xn, B[3], ident)
    yield
    pe.wait_ge(s("xnT"), 3 * b + 1)
    for j in range(TB):
        last = mm(B[0][:, j * 16:(j + 1) * 16], a.xnT[:, j * P:(j + 1) * P], W["mid_route"][:, :], start=True, stop=True)
    last.then_inc(s("small"), 1)
    yield
    yield
    pe.wait_ge(s("outer"), b + 1)
    for j in range(TB):
        last = nc.tensor.transpose(B[1][:, j * P:(j + 1) * P], a.outer[:, j, :], ident)
    last.then_inc(s("outerT_ps"), 1)
    yield
    pe.wait_ge(s("outerT"), b + 1)
    for j in range(TB):
        c = slice(j * P, (j + 1) * P)
        mm(B[2][:, c], a.xnT[:, c], W["base"][:, :], start=True, stop=False)
        last = mm(B[2][:, c], a.outerT[:, c], W["lora_b"][:, :], start=False, stop=True)
    last.then_inc(s("y1"), 1)
    yield
    yield
    yield
    layernorm_turn(nc, pe, s, 3 * b + 1, a.xn, B[3], ident)
    yield
    pe.wait_ge(s("xnT"), 3 * b + 2)
    for n in (1, 0):
        mm(B[n][:, :], W["lin_qkv"][:, n, :], a.xnT[:, :], start=True, stop=True).then_inc(s("qk_ps"), 1)
    for j in range(TB):
        c = slice(j * P, (j + 1) * P)
        last = mm(B[3][:, c], a.xnT[:, c], W["lin_qkv"][:, 2, :], start=True, stop=True)
    last.then_inc(s("v_ps"), 1)
    pe.wait_ge(s("kT"), b + 1)
    for j in range(TB):
        last = nc.tensor.transpose(B[2][:, j * P:(j + 1) * P], a.kT[:, j * P:(j + 1) * P], ident)
    last.then_inc(s("k_ps"), 1)
    yield

    def own_keys(i):
        j, g = i // 4, i % 4
        pe.wait_ge(s("sc"), 4 * TB * b + i + 1)
        if i == 0:
            pe.wait_ge(s("v_wide"), GH * b + GH)
        for n in range(GH):
            last = mm(B[3][g * 32:(g + 1) * 32, j * P:(j + 1) * P], a.v_wide[:, j, g * GH + n, :], a.sc[:, g, n, :],
                      start=(n == 0), stop=False, tile_position=(0, g * 32), skip_group_check=True)
        last.then_inc(s("own_keys"), 1)
        if g == GH - 1:
            pe.wait_ge(s("states"), TB * b + j + 1)
            c = slice(j * P, (j + 1) * P)
            mm(B[3][:, c], a.states[:, j, :], a.qT[:, c], start=False, stop=True, skip_group_check=True).then_inc(s("num"), 1)

    for i in range(4 * TB):
        j, g = i // 4, i % 4
        c = slice(j * P, (j + 1) * P)
        if i >= 2:
            pe.wait_ge(s("sc"), 4 * TB * b + i - 1)
        pe.wait_ge(s("q_wide"), 4 * TB * b + i + 1)
        mm(B[g % 2][:, :], a.kT[:, c], a.q_wide[:, g].rearrange("p h t -> p (h t)"), start=True, stop=True).then_inc(s("sc_ps"), 1)
        if i:
            own_keys(i - 1)
        if i == KEYS_AT:
            pe.wait_ge(s("k_tok"), b + 1)
            for n in range(TB):
                last = mm(B[2][:, n * P:], a.k_tok[:, n * P:(n + 1) * P], K("causal_then_ones")[:, 0:BL - n * P],
                          start=(n == 0), stop=(n == TB - 1), skip_group_check=True)
            last.then_inc(s("key_sums"), 1)
        if i == DEN_AT:
            pe.wait_ge(s("q_keys"), b + 1)
            pe.wait_ge(s("keys_before"), b + 2)
            mm(B[2][:, :], K("same8"), a.q_keys[:, :], start=True, stop=True).then_inc(s("den_ps"), 1)
        if i == STATES_AT:
            pe.wait_ge(s("den"), 2 * b + 1)
            for n in range(TB):
                cs = slice(n * P, (n + 1) * P)
                last = mm(B[2][:, cs], a.k_tok[:, cs], a.v_tok[:, cs], start=True, stop=True)
            last.then_inc(s("kv"), 1)
        yield
    own_keys(4 * TB - 1)
    yield
    pe.wait_ge(s("aT"), b + 1)
    for j in range(TB):
        c = slice(j * P, (j + 1) * P)
        last = mm(B[0][:, c], a.aT[:, c], W["lin_out"][:, :], start=True, stop=True)
    last.then_inc(s("y2"), 1)
    yield
    yield
    yield
    yield
    layernorm_turn(nc, pe, s, 3 * b + 2, a.xn, B[3], ident)
    yield
    pe.wait_ge(s("xnT"), 3 * b + 3)
    for j in range(TB):
        last = mm(B[2][:, j * EXP:(j + 1) * EXP], a.xnT[:, j * P:(j + 1) * P], W["gate"][:, 0:EXP], start=True, stop=True)
    last.then_inc(s("gate_ps"), 1)
    yield
    yield

    def up(i):
        e, n = UNITS[i]
        c, m = HC[n]
        def by_parts(bank, w):
            lead, rest = W[w + "_lead"][:, e, c:c + m], W[w + "_rest"][:, e, c:c + m]
            mm(bank[0:m, :], rest, a.x_lead[:, :], start=True, stop=False)
            mm(bank[0:m, :], lead, a.x_rest[:, :], start=False, stop=False)
            return mm(bank[0:m, :], lead, a.x_lead[:, :], start=False, stop=True)

        if i:
            pe.wait_ge(s("h1"), NU * b + i)
        else:
            pe.wait_ge(s("x_rest"), b + 1)
        by_parts(B[0], "w1").then_inc(s("h1_ps"), 1)
        if i:
            pe.wait_ge(s("h"), NU * b + i)
        by_parts(B[1], "w3").then_inc(s("h3_ps"), 1)

    def down(i):
        e, n = UNITS[i]
        m = HC[n][1]
        pe.wait_ge(s("h"), NU * b + i + 1)
        if n == 0:
            if e >= 2:
                pe.wait_ge(s("y3_added"), EXP * b + e - 1)
            else:
                pe.wait_ge(s("cw"), 2 * b + 2)
        for j in range(TB):
            last = mm(B[2 + e % 2][:, j * P:(j + 1) * P], a.h[0:m, i % 2, j * P:(j + 1) * P], W["w2"][0:m, e, n, :],
                      start=(n == 0 and j == 0), stop=(n == len(HC) - 1), skip_group_check=True)
        last.then_inc(s("y_part"), 1)

    for i in range(NU + 1):
        if i < NU:
            up(i)
        if i:
            down(i - 1)
        yield
    yield


def rest_act(nc, act, s, b, a, B, K, W):
    f = nc.scalar.activation

    def norm(i):
        act.wait_ge(s("ve"), i + 1)
        f(a.std[:, :], a.ve[:, :], ACT.Sqrt).then_inc(s("std"), 1)
        yield
        yield
        act.wait_ge(s("xnT_ps"), i + 1)
        f(a.xnT[:, :], B[3][:, :], ACT.Copy).then_inc(s("xnT"), 1)
        yield

    yield from norm(3 * b)
    act.wait_ge(s("shift"), 3 * (2 * b) + 3)
    f(a.ex[:, :, :], a.lg[:, :, :], ACT.Exp).then_inc(s("ex"), 1)
    yield
    yield
    act.wait_ge(s("outerT_ps"), b + 1)
    f(a.outerT[:, :], B[1][0:NL * RL + 1, :], ACT.Copy).then_inc(s("outerT"), 1)
    yield
    yield
    yield from norm(3 * b + 1)
    act.wait_ge(s("k_ps"), b + 1)
    f(a.k_tok[:, :], B[2][:, :], ACT.Copy).then_inc(s("k_tok"), 1)
    act.wait_ge(s("v_tok"), b + 1)
    for n in range(GH):
        f(a.v_wide[:, :, :, n * DL:(n + 1) * DL].rearrange("p j (g h) e -> p (j g) h e", h=GH)[:, :, n, :],
          a.v_tok[:, :].rearrange("p (g h e) -> p g h e", h=GH, e=DL)[:, :, n, :], ACT.Copy).then_inc(s("v_wide"), 1)
    yield
    for i in range(4 * TB):
        yield
    yield
    yield
    yield
    yield from norm(3 * b + 2)
    f(a.x_lead[:, :], B[3][:, :], ACT.Copy).then_inc(s("x_lead"), 1)
    act.wait_ge(s("shift"), 3 * (2 * b + 1) + 3)
    f(a.ex[:, :, 0:EXP], a.lg[:, :, 0:EXP], ACT.Exp).then_inc(s("ex"), 1)
    yield
    yield
    for i in range(NU + 1):
        if i < NU:
            m = HC[UNITS[i][1]][1]
            act.wait_ge(s("h1_ps"), NU * b + i + 1)
            if i >= 2:
                act.wait_ge(s("h"), NU * b + i - 1)
            f(a.h1[0:m, i % 2, :], B[0][0:m, :], ACT.Silu).then_inc(s("h1"), 1)
        yield
    yield


def rest_pool(nc, pool, s, b, a, K):
    pool.wait_ge(s("qT"), b + 1)
    for i in range(4 * TB):
        j, g = i // 4, i % 4
        if j:
            pool.wait_ge(s("sc_ps"), 4 * TB * b + i - 3)
        nc.gpsimd.tensor_tensor(a.q_wide[:, g], a.qT[:, j * P:(j + 1) * P].unsqueeze(1).to_broadcast([P, GH, P]),
                                K("head_of")[:, g * GH:(g + 1) * GH].unsqueeze(2).to_broadcast([P, GH, P]), ALU.mult).then_inc(s("q_wide"), 1)


def rest_dve(nc, dve, s, b, a, B, K, W, x_sb, x_in):
    v = nc.vector

    def norm(i, *added):
        layernorm_moments(nc, dve, s, i, b, x_sb, a, added)
        yield
        layernorm_apply(nc, dve, s, i, b, x_sb, a)
        yield
        yield

    def softmax(i, src, n, bias=None):
        lg = a.lg[:, :, 0:n]
        if bias is None:
            v.tensor_copy(lg, src).then_inc(s("shift"), 1)
        else:
            v.tensor_tensor(lg, src, bias.unsqueeze(1).to_broadcast([P, TB, n]), ALU.add).then_inc(s("shift"), 1)
        dve.wait_ge(s("shift"), 3 * i + 1)
        v.tensor_reduce(a.mx[:, :], lg, AX.X, ALU.max).then_inc(s("shift"), 1)
        dve.wait_ge(s("shift"), 3 * i + 2)
        v.tensor_tensor(lg, lg, a.mx[:, :].unsqueeze(2).to_broadcast([P, TB, n]), ALU.subtract).then_inc(s("shift"), 1)
        yield
        dve.wait_ge(s("ex"), i + 1)
        v.tensor_reduce(a.sm[:, :], a.ex[:, :, 0:n], AX.X, ALU.add).then_inc(s("sum"), 1)
        dve.wait_ge(s("sum"), 2 * i + 1)
        v.reciprocal(a.rs[:, :], a.sm[:, :]).then_inc(s("sum"), 1)
        dve.wait_ge(s("sum"), 2 * i + 2)

    yield from norm(3 * b, x_in, b + 2)
    small = B[0][:, 0:TB * 16].rearrange("p (j c) -> p j c", c=16)
    dve.wait_ge(s("small"), b + 1)
    v.tensor_copy(a.mid[:, :, :], small[:, :, 0:RL]).then_inc(s("mid"), 1)
    yield from softmax(2 * b, small[:, :, RL:16], NL, W["router_b"][:, :])
    v.tensor_tensor(a.gate[:, :, :], a.ex[:, :, :], a.rs[:, :].unsqueeze(2).to_broadcast([P, TB, NL]), ALU.mult).then_inc(s("gate"), 1)
    dve.wait_ge(s("gate"), b + 1)
    dve.wait_ge(s("mid"), b + 1)
    for j in range(TB):
        last = v.tensor_tensor(a.outer[:, j, 0:NL * RL].rearrange("p (e r) -> p e r", r=RL), a.gate[:, j, :].unsqueeze(2).to_broadcast([P, NL, RL]),
                               a.mid[:, j, :].unsqueeze(1).to_broadcast([P, NL, RL]), ALU.mult)
    last.then_inc(s("outer"), 1)
    yield
    yield
    dve.wait_ge(s("y1"), b + 1)
    v.tensor_tensor(columns(x_sb, b, 0), columns(x_sb, b, 0), B[2][:, :], ALU.add).then_inc(s("y1_added"), 1)
    yield
    yield from norm(3 * b + 1, s("y1_added"), b + 1)
    for n, (t, name) in ((1, (a.kT, "kT")), (0, (a.qT, "qT"))):
        dve.wait_ge(s("qk_ps"), 2 * b + 2 - n)
        v.tensor_scalar(t[:, :], B[n][:, :], W["lin_b_eps"][:, n:n + 1], 1e-6, ALU.add, ALU.max).then_inc(s(name), 1)
    tiles = lambda t: t.rearrange("p (j c) -> p j c", c=P)
    dve.wait_ge(s("v_ps"), b + 1)
    v.tensor_tensor(tiles(a.v_tok[:, :]), tiles(B[3][:, :]), W["lin_v_b"][:, :].unsqueeze(1).to_broadcast([P, TB, P]), ALU.add).then_inc(s("v_tok"), 1)
    yield

    for i in range(4 * TB):
        j, g = i // 4, i % 4
        dve.wait_ge(s("sc_ps"), 4 * TB * b + i + 1)
        if i >= 4:
            dve.wait_ge(s("own_keys"), 4 * TB * b + i - 3)
        v.tensor_tensor(a.sc[:, g], B[g % 2][:, :].rearrange("p (h t) -> p h t", t=P),
                        K("causal_then_ones")[:, 0:P].unsqueeze(1).to_broadcast([P, GH, P]), ALU.mult).then_inc(s("sc"), 1)
        if i == KEYS_AT:
            dve.wait_ge(s("key_sums"), b + 1)
            dve.wait_ge(s("keys_before"), b + 1)
            v.scalar_tensor_tensor(a.q_keys[:, :], B[2][:, :], a.keys_before[:, 0:1], a.qT[:, :], ALU.add, ALU.mult).then_inc(s("q_keys"), 1)
            dve.wait_ge(s("q_keys"), b + 1)
            v.tensor_tensor(a.keys_before[:, :], a.keys_before[:, :], B[2][:, BL - 1:BL], ALU.add).then_inc(s("keys_before"), 1)
        if i == BIAS_AT:
            dve.wait_ge(s("xn"), TB * (3 * b + 1) + TB)
            v.tensor_tensor(tiles(columns(x_sb, b, 0)), tiles(columns(x_sb, b, 0)), W["lin_out_b"][:, :].unsqueeze(1).to_broadcast([P, TB, P]),
                            ALU.add).then_inc(s("x_biased"), 1)
        if i == DEN_AT:
            dve.wait_ge(s("den_ps"), b + 1)
            v.tensor_scalar(a.den[:, :], B[2][:, :], 1e-6, None, ALU.max).then_inc(s("den"), 1)
            dve.wait_ge(s("den"), 2 * b + 1)
            v.reciprocal(a.rden[:, :], a.den[:, :]).then_inc(s("den"), 1)
        if i == STATES_AT:
            dve.wait_ge(s("kv"), b + 1)
            v.tensor_tensor(a.own[:, :, :], B[2][:, :].rearrange("p (j c) -> p j c", c=P), K("same8").unsqueeze(1).to_broadcast([P, TB, P]),
                            ALU.mult).then_inc(s("own"), 1)
            dve.wait_ge(s("own"), b + 1)
            for n in range(1, TB):
                dve.wait_ge(s("states"), TB * b + n)
                v.tensor_tensor(a.states[:, n, :], a.states[:, n - 1, :], a.own[:, n - 1, :], ALU.add).then_inc(s("states"), 1)
        yield
    dve.wait_ge(s("num"), TB * b + TB)
    dve.wait_ge(s("den"), 2 * b + 2)
    v.tensor_tensor(a.aT[:, :], B[3][:, :], a.rden[:, :], ALU.mult).then_inc(s("aT"), 1)
    dve.wait_ge(s("states"), TB * b + TB)
    v.tensor_tensor(a.states[:, 0, :], a.states[:, TB - 1, :], a.own[:, TB - 1, :], ALU.add).then_inc(s("states"), 1)
    yield
    yield
    dve.wait_ge(s("y2"), b + 1)
    dve.wait_ge(s("x_biased"), b + 1)
    v.tensor_tensor(columns(x_sb, b, 0), columns(x_sb, b, 0), B[0][:, :], ALU.add).then_inc(s("y2_added"), 1)
    yield
    yield from norm(3 * b + 2, s("y2_added"), b + 1)
    dve.wait_ge(s("xnT"), 3 * b + 3)
    dve.wait_ge(s("x_lead"), b + 1)
    v.tensor_tensor(a.x_rest[:, :], a.xnT[:, :], a.x_lead[:, :].bitcast(F32), ALU.subtract).then_inc(s("x_rest"), 1)
    dve.wait_ge(s("gate_ps"), b + 1)
    yield from softmax(2 * b + 1, B[2][:, 0:TB * EXP].rearrange("p (j e) -> p j e", e=EXP), EXP)
    v.tensor_tensor(a.p[:, :, :], a.ex[:, :, 0:EXP], a.rs[:, :].unsqueeze(2).to_broadcast([P, TB, EXP]), ALU.mult).then_inc(s("choose"), 1)
    dve.wait_ge(s("choose"), 7 * b + 1)
    for j in range(TB):
        theirs = a.p[:, j, :].unsqueeze(1).to_broadcast([P, EXP, EXP])
        mine = a.p[:, j, :].unsqueeze(2).to_broadcast([P, EXP, EXP])
        v.tensor_tensor(a.over[:, j], theirs, mine, ALU.is_gt)
        last = v.tensor_tensor(a.ties[:, j], theirs, mine, ALU.is_equal)
    last.then_inc(s("choose"), 1)
    ties = a.ties[:, :].rearrange("p j e f -> p j (e f)")
    dve.wait_ge(s("choose"), 7 * b + 2)
    v.tensor_tensor(ties, ties, K("earlier").unsqueeze(1).to_broadcast([P, TB, EXP * EXP]), ALU.mult).then_inc(s("choose"), 1)
    dve.wait_ge(s("choose"), 7 * b + 3)
    v.tensor_tensor(a.over[:, :], a.over[:, :], a.ties[:, :], ALU.add).then_inc(s("choose"), 1)
    dve.wait_ge(s("choose"), 7 * b + 4)
    v.tensor_reduce(a.rank[:, :, :], a.over[:, :, :, :], AX.X, ALU.add).then_inc(s("choose"), 1)
    dve.wait_ge(s("choose"), 7 * b + 5)
    v.scalar_tensor_tensor(a.cw[:, :, :], a.rank[:, :, :], 1.5, a.p[:, :, :], ALU.is_lt, ALU.mult).then_inc(s("cw"), 1)
    dve.wait_ge(s("cw"), 2 * b + 1)
    v.tensor_reduce(a.sm[:, :], a.cw[:, :, :], AX.X, ALU.add).then_inc(s("choose"), 1)
    dve.wait_ge(s("choose"), 7 * b + 6)
    v.reciprocal(a.rs[:, :], a.sm[:, :]).then_inc(s("choose"), 1)
    dve.wait_ge(s("choose"), 7 * b + 7)
    v.tensor_tensor(a.cw[:, :, :], a.cw[:, :, :], a.rs[:, :].unsqueeze(2).to_broadcast([P, TB, EXP]), ALU.mult).then_inc(s("cw"), 1)
    yield

    def add(e):
        dve.wait_ge(s("y_part"), NU * b + (e + 1) * len(HC))
        dve.wait_ge(s("cw"), 2 * b + 2)
        if e:
            dve.wait_ge(s("y3_added"), EXP * b + e)
        for j in range(TB):
            last = v.scalar_tensor_tensor(columns(x_sb, b, j * P, P), B[2 + e % 2][:, j * P:(j + 1) * P], a.cw[:, j, e:e + 1],
                                          columns(x_sb, b, j * P, P), ALU.mult, ALU.add)
        last.then_inc(s("y3_added"), 1)

    for i in range(NU + 1):
        if i < NU:
            e, n = UNITS[i]
            m = HC[n][1]
            dve.wait_ge(s("h1"), NU * b + i + 1)
            dve.wait_ge(s("h3_ps"), NU * b + i + 1)
            if i >= 2:
                dve.wait_ge(s("y_part"), NU * b + i - 1)
            v.tensor_tensor(a.h[0:m, i % 2, :], a.h1[0:m, i % 2, :], B[1][0:m, :], ALU.mult).then_inc(s("h"), 1)
            if n == 1 and e:
                add(e - 1)
        yield
    add(EXP - 1)
    yield


def merged(first, second, steps):
    done = 0
    for place in PLACES:
        while done < min(place, steps):
            next(first)
            done += 1
        next(second)
    while done < steps:
        next(first)
        done += 1
    assert next(first, "ended") == "ended" and next(second, "ended") == "ended"


def alone(stream, steps, prepare=None):
    for n in range(steps):
        if prepare and n == MORE_WEIGHTS_AT:
            prepare()
        next(stream)
    assert next(stream, "ended") == "ended"


def prepare_delta_act(nc, act, s, W, t):
    f = nc.scalar.activation
    f(t[:, 1, :], W["itemp"][:, :], ACT.Abs).then_inc(s("log1p"), 1)
    act.wait_ge(s("log1p"), 1)
    f(t[:, 1, :], t[:, 1, :], ACT.Exp, scale=-1.0).then_inc(s("log1p"), 1)
    act.wait_ge(s("log1p"), 2)
    f(t[:, 1, :], t[:, 1, :], ACT.Ln, bias=1.0).then_inc(s("log1p"), 1)


def prepare_delta_dve(nc, dve, s, W, t):
    v = nc.vector
    dve.wait_ge(s("log1p"), 3)
    v.tensor_scalar(t[:, 0, :], W["itemp"][:, :], 0.0, 0.5, ALU.max, ALU.add).then_inc(s("temp"), 1)
    dve.wait_ge(s("temp"), 1)
    v.tensor_tensor(t[:, 0, :], t[:, 0, :], t[:, 1, :], ALU.add).then_inc(s("temp"), 1)
    dve.wait_ge(s("temp"), 2)
    v.reciprocal(W["itemp"][:, :], t[:, 0, :]).then_inc(s("temp"), 1)
    dve.wait_ge(s("temp"), 3)
    v.tensor_tensor(W["b2"][:, :, :], W["b2"][:, :, :], W["itemp"][:, :].unsqueeze(2).to_broadcast([P, H, NBR]), ALU.mult).then_inc(s("temp"), 1)
    dve.wait_ge(s("temp"), 4)


def prepare_rest_pe(nc, pe, s, K, W, B):
    for n in range(5):
        nc.tensor.transpose(B[n // 4][:, (n % 4) * P:(n % 4 + 1) * P], W["rows"][:, n, :], K("ident")).then_inc(s("turned"), 1)
    for n in range(2):
        nc.tensor.transpose(B[1][:, (n + 1) * P:(n + 1) * P + NE], W["rows8"][:, n, :], K("ident")[0:NE, 0:NE]).then_inc(s("turned"), 1)


def prepare_rest_act(nc, act, s, W, B):
    f = nc.scalar.activation
    act.wait_ge(s("turned"), 7)
    for t, src in ((W["base"][:, :], B[0][:, 0:P]), (W["lin_qkv"][:, :, :], B[0][:, P:4 * P].rearrange("p (n o) -> p n o", o=P)),
                   (W["lin_out"][:, :], B[1][:, 0:P]), (W["mid_route"][:, RL:16], B[1][:, P:P + NE]),
                   (W["gate"][:, :], B[1][:, 2 * P:2 * P + NE])):
        f(t, src, ACT.Copy).then_inc(s("weights"), 1)


def main_phase(nc, x_sb, K, W, d, r, args, loads, out):
    with ExitStack() as ctx:
        first, more, others, late = loads
        banks = [ctx.enter_context(nc.psum_tensor(f"bank{n}", [P, BL], F32)) for n in range(8)]
        DB, RB = banks[:4], banks[4:]
        sd, sr = Signals(nc, "delta"), Signals(nc, "rest")
        y_dram = out.rearrange("a (t p) d -> p (a t) d", p=P)

        split = [(w, e) for e in range(EXP) for w in ("w1", "w3")]

        def stage(n):
            return r.sc[:, 2 * (n % 2):2 * (n % 2) + 2].rearrange("p n h t -> p (n h t)")[:, 0:HID]

        with nc.Block() as block:
            @block.gpsimd
            def _(pool):
                nc.gpsimd.memset(W["m1s"][:], 0.0).then_inc(sd("m1s_zero"), 1)
                nc.gpsimd.memset(r.outer[:], 0.0).then_inc(sr("outer_zero"), 1)
                pool.wait_ge(sr("outer_zero"), 1)
                nc.gpsimd.memset(r.outer[:, :, NL * RL:NL * RL + 1], 1.0).then_inc(sd("zeroed"), 1)
                for t in (d.pre, d.vT, d.state, r.states, r.v_wide, r.keys_before):
                    nc.gpsimd.memset(t[:], 0.0).then_inc(sd("zeroed"), 1)
                pool.wait_ge(sr("loads"), 16 * len(others))
                nc.gpsimd.tensor_scalar(W["lora_b"][0:NL * RL, :], W["lora_b"][0:NL * RL, :], 2.0, None, ALU.mult).then_inc(sr("weights"), 1)
                nc.gpsimd.tensor_scalar(W["lin_b_eps"][:, :], W["lin_b_eps"][:, :], 1e-6, None, ALU.add).then_inc(sr("weights"), 1)
                for n, (w, e) in enumerate(split):
                    lead = W[w + "_lead"][:, e, :]
                    pool.wait_ge(sr(f"staged{n % 2}"), 16 * (n // 2) + 16)
                    nc.gpsimd.tensor_copy(lead, stage(n)).then_inc(sr("w_lead"), 1)
                    pool.wait_ge(sr("w_lead"), n + 1)
                    nc.gpsimd.tensor_tensor(W[w + "_rest"][:, e, :], stage(n), lead.bitcast(F32), ALU.subtract).then_inc(sr("w_parts"), 1)
                with pool.Fori(0, NB) as b:
                    rest_pool(nc, pool, sr, b, r, K)

            @block.sync
            def _(sp):
                for group, name in ((first, sd("first_loads")), (more, sd("loads")), (others, sr("loads")), (late, sr("late_loads"))):
                    if group is more:
                        sp.wait_ge(sd("m1s_zero"), 1)
                    for dst, src in group:
                        sp.dma_start(dst, src).then_inc(name, 16)
                for n, (w, e) in enumerate(split):
                    if n >= 2:
                        sp.wait_ge(sr("w_parts"), n - 1)
                    sp.dma_start(stage(n), args[f"L1_ffn_{w}"][e]).then_inc(sr(f"staged{n % 2}"), 16)
                with sp.Fori(0, NB) as b:
                    sp.wait_ge(sr("y3_added"), EXP * b + EXP)
                    sp.dma_start(y_dram[:, bass.ds(b * TB, TB), :], columns(x_sb, b, 0).rearrange("p (t d) -> p t d", d=D)).then_inc(sr("stored"), 16)
                sp.wait_ge(sr("stored"), 16 * NB)

            @block.tensor
            def _(pe):
                pe.wait_ge(sd("zeroed"), 7)
                pe.wait_ge(sd("first_loads"), 16 * len(first))

                def delta(b):
                    return delta_pe(nc, pe, sd, b, d, DB, K, W)

                def norm(b):
                    return delta_norm_pe(nc, pe, sd, b, d, DB, K)

                def rest(b):
                    return rest_pe(nc, pe, sr, b, r, RB, K, W)

                alone(norm(0), 3)
                alone(with_next_norm(delta(0), norm(1)), DELTA_STEPS + 3, lambda: pe.wait_ge(sd("loads"), 16 * len(more)))
                pe.wait_ge(sr("loads"), 16 * len(others))
                prepare_rest_pe(nc, pe, sr, K, W, RB)
                pe.wait_ge(sr("weights"), 7)
                pe.wait_ge(sr("late_loads"), 16 * len(late))
                pe.wait_ge(sr("w_parts"), len(split))
                with pe.Fori(1, NB - 1) as b:
                    merged(with_next_norm(delta(b), norm(b + 1)), rest(b - 1), DELTA_STEPS + 3)
                merged(delta(NB - 1), rest(NB - 2), DELTA_STEPS)
                alone(rest(NB - 1), REST_STEPS)

            @block.scalar
            def _(act):
                def more_weights():
                    act.wait_ge(sd("loads"), 16 * len(more))
                    prepare_delta_act(nc, act, sd, W, d.temperature)

                act.wait_ge(sd("zeroed"), 7)
                act.wait_ge(sd("first_loads"), 16 * len(first))

                def delta(b):
                    return delta_act(nc, act, sd, b, d, DB, K, W)

                def norm(b):
                    return delta_norm_act(nc, act, sd, b, d, DB)

                def rest(b):
                    return rest_act(nc, act, sr, b, r, RB, K, W)

                alone(norm(0), 3)
                alone(with_next_norm(delta(0), norm(1)), DELTA_STEPS + 3, more_weights)
                act.wait_ge(sr("loads"), 16 * len(others))
                prepare_rest_act(nc, act, sr, W, RB)
                with act.Fori(1, NB - 1) as b:
                    merged(with_next_norm(delta(b), norm(b + 1)), rest(b - 1), DELTA_STEPS + 3)
                merged(delta(NB - 1), rest(NB - 2), DELTA_STEPS)
                alone(rest(NB - 1), REST_STEPS)

            @block.vector
            def _(dve):
                for name in ("out_added", "halo", "fu", "state"):
                    dve.sem_inc(sd(name), 1)
                for name in ("states", "keys_before"):
                    dve.sem_inc(sr(name), 1)

                def more_weights():
                    dve.wait_ge(sd("loads"), 16 * len(more))
                    prepare_delta_dve(nc, dve, sd, W, d.temperature)

                dve.wait_ge(sd("first_loads"), 16 * len(first))
                dve.wait_ge(sd("zeroed"), 7)

                def delta(b):
                    return delta_dve(nc, dve, sd, b, d, DB, K, W, x_sb)

                def norm(b):
                    return delta_norm_dve(nc, dve, sd, b, d, x_sb)

                def rest(b):
                    return rest_dve(nc, dve, sr, b, r, RB, K, W, x_sb, sd("out_added"))

                alone(norm(0), 3)
                alone(with_next_norm(delta(0), norm(1)), DELTA_STEPS + 3, more_weights)
                dve.wait_ge(sr("weights"), 7)
                dve.wait_ge(sr("w_parts"), len(split))
                with dve.Fori(1, NB - 1) as b:
                    merged(with_next_norm(delta(b), norm(b + 1)), rest(b - 1), DELTA_STEPS + 3)
                merged(delta(NB - 1), rest(NB - 2), DELTA_STEPS)
                alone(rest(NB - 1), REST_STEPS)


def build_program(nc, args, out):
    with ExitStack() as ctx:
        def sb(name, *shape, dt=F32):
            return ctx.enter_context(nc.sbuf_tensor(name, list(shape), dt))

        x_sb = sb("x_sb", P, NT * P)
        consts = sb("consts", P, CONSTS.shape[1])

        def K(name):
            a, n = CONST_AT[name]
            return consts[:, a:a + n]

        W = {"qkv": sb("w_qkv", P, 3, P), "b": sb("w_b", P, H), "taps": sb("w_taps", P, 3, KQ), "fir": sb("w_fir", P, sum(FIRS)),
             "m1x": sb("w_m1x", P, P), "m1s": sb("w_m1s", P, P), "m2": sb("w_m2", P, H * NBR), "b1": sb("w_b1", P, 1),
             "b2": sb("w_b2", P, H, NBR), "itemp": sb("w_itemp", P, H), "onorm": sb("w_onorm", P, 1),
             "o": sb("w_o", P, P),
                 "mid_route": sb("w_mid_route", P, 16), "router_b": sb("w_router_b", P, NL), "base": sb("w_base", P, P),
             "lora_b": sb("w_lora_b", NL * RL + 1, P), "lin_qkv": sb("w_lin_qkv", P, 3, P),
             "lin_v_b": sb("w_lin_v_b", P, P), "lin_b_eps": sb("w_lin_b_eps", P, 2), "lin_out": sb("w_lin_out", P, P),
             "lin_out_b": sb("w_lin_out_b", P, P), "gate": sb("w_gate", P, NE),
             "w2": sb("w_2", P, EXP, len(HC), P)}
        W.update({f"{w}_{part}": sb(f"w_{w}_{part}", P, EXP, HID, dt=F32R) for w in ("w1", "w3") for part in ("lead", "rest")})
        d, r = Arrays(nc, ctx, "delta"), Arrays(nc, ctx, "rest")
        delta_arrays(d)
        rest_arrays(r)
        W["rows"] = r.q_wide[:, 0:2].rearrange("p g h t -> p (g h) t")[:, 0:5]
        W["rows8"] = r.q_wide[0:NE, 2, 0:2]

        first, delta, rest, late = loads = [], [], [], []

        def to_all(group, dst, src):
            group.append((dst, src.rearrange("(a n) -> a n", a=1).to_broadcast([P, src.shape[0]])))

        x_in, x_tiles = args["L0_attn_hidden_states"].rearrange("a (t p) d -> p (a t) d", p=P), x_sb[:, :].rearrange("p (t d) -> p t d", d=D)
        first += [(x_tiles[:, 0:TB], x_in[:, 0:TB]), (consts[:, :], args["consts"])]
        for n, name in enumerate(("q", "k", "v")):
            first += [(W["qkv"][:, n, :], args[f"L0_attn_{name}_w"]), (W["taps"][:, n, :], args[f"L0_attn_{name}c_w"].rearrange("d a k -> d (a k)"))]
        first.append((W["b"][:, :], args["L0_attn_b_w"]))

        at = 0
        for n in FIRS:
            delta.append((W["fir"][:, at:at + n], args[f"L0_attn_fir_w{n}"].rearrange("d a k -> d (a k)")))
            at += n
        delta.append((W["m1x"][:, :], args["L0_attn_mlp_w1"][0:D, :]))
        by_kind = args["L0_attn_mlp_w1"][D:D + H * NBR * 4, :].rearrange("(r k) n -> k r n", k=4)
        for kind, row in ((0, 0), (2, 32), (1, 64), (3, 96)):
            delta.append((W["m1s"][row:row + H * NBR, :], by_kind[kind]))
        delta.append((W["m2"][:, :], args["L0_attn_mlp_w2"]))
        delta.append((W["b1"][:, :], args["L0_attn_mlp_b1"].rearrange("(n a) -> n a", a=1)))
        to_all(delta, W["b2"][:, :, :].rearrange("p h n -> p (h n)"), args["L0_attn_mlp_b2"])
        to_all(delta, W["itemp"][:, :], args["L0_attn_gate_log_temp"])
        for h in range(H):
            delta.append((W["onorm"][h * DK:(h + 1) * DK, :], args["L0_attn_onorm_w"].rearrange("(n a) -> n a", a=1)))
        delta.append((W["o"][:, :], args["L0_attn_o_w"]))
        delta.append((x_tiles[:, TB:], x_in[:, TB:]))

        rest.append((W["rows"][:, 0, :], args["L0_ffn_base_w"]))
        rest.append((W["rows"][:, 1:4, :], args["L1_attn_qkv_w"].rearrange("(n o) i -> o n i", o=P)))
        rest.append((W["rows"][:, 4, :], args["L1_attn_out_w"]))
        rest.append((W["rows8"][:, 0, :], args["L0_ffn_router_w"]))
        rest.append((W["rows8"][:, 1, :], args["L1_ffn_gate_w"]))
        rest.append((W["mid_route"][:, 0:RL], args["L0_ffn_lora_A"]))
        to_all(rest, W["router_b"][:, :], args["L0_ffn_router_b"])
        rest.append((W["lora_b"][NL * RL:, :], args["L0_ffn_base_b"].rearrange("(a n) -> a n", a=1)))
        rest.append((W["lora_b"][0:NL * RL, :], args["L0_ffn_lora_B"].rearrange("e r d -> (e r) d")))
        to_all(rest, W["lin_v_b"][:, :], args["L1_attn_qkv_b"][2 * P:3 * P])
        for n in range(2):
            rest.append((W["lin_b_eps"][:, n:n + 1], args["L1_attn_qkv_b"][n * P:(n + 1) * P].rearrange("(p a) -> p a", a=1)))
        to_all(rest, W["lin_out_b"][:, :], args["L1_attn_out_b"])

        whole = HID // P
        late += [(W["w2"][:, e, 0:whole, :], args["L1_ffn_w2"][e, 0:whole * P, :].rearrange("(c k) d -> k c d", k=P)) for e in range(EXP)]
        late += [(W["w2"][0:HID - whole * P, e, whole, :], args["L1_ffn_w2"][e, whole * P:HID, :]) for e in range(EXP)]
        main_phase(nc, x_sb, K, W, d, r, args, loads, out)


def kernel(**inputs):
    import concourse.bacc as bacc
    from concourse.bass_utils import run_bass_kernel_spmd

    nc = bacc.Bacc("TRN2", target_bir_lowering=False, num_devices=1)
    arrays, args = {}, {}
    for name, a in list(inputs.items()) + [("consts", CONSTS)]:
        a = np.ascontiguousarray(a)
        arrays[f"in_{name}_dram"] = a
        args[name] = nc.dram_tensor(f"in_{name}_dram", a.shape, mybir.dt.from_np(a.dtype), kind="ExternalInput").ap()
    out = nc.dram_tensor("out_0_dram", (1, L, D), F32, kind="ExternalOutput").ap()
    build_program(nc, args, out)
    r = run_bass_kernel_spmd(nc, [arrays], core_ids=[0])
    return r.results[0]["out_0_dram"]
```
